# Optimizing a Trainium2 kernel written in Bass

```python
import numpy as np
import jax
import jax.numpy as jnp

def _softmax(x, axis=-1):
    return jax.nn.softmax(x, axis=axis)

def _gelu(x):
    return jax.nn.gelu(x, approximate=True)

def _silu(x):
    return jax.nn.silu(x)

def _sigmoid(x):
    return jax.nn.sigmoid(x)

def _layernorm(x, axis=-1, eps=1e-05):
    m = jnp.mean(x, axis=axis, keepdims=True)
    v = jnp.var(x, axis=axis, keepdims=True)
    return (x - m) / jnp.sqrt(v + eps)

def _scatter_add(tgt, idx, src, axis=0):
    return tgt.at[idx].add(src)

def _segment_sum(src, seg, n):
    return jax.ops.segment_sum(src, seg, n)
kernel_name = 'mk_adaln_d1_jaxref_r8_e794eb'

def setup_inputs(seed: int=0):
    np.random.seed(seed)
    _w = jnp.asarray

    def _L0_attn_setup():
        import jax, jax.numpy as jnp
        import numpy as np
        B, S, D, H = (2, 256, 128, 16)
        Dh = D // H
        C = 2
        EPS = 1e-06
        LN_EPS = 1e-05

        def _rope_cache(seq_len, dh):
            half = dh // 2
            inv_freq = 1.0 / 10000.0 ** (jnp.arange(0, 2 * half, 2, dtype=jnp.float32) / dh)
            t = jnp.arange(seq_len, dtype=jnp.float32)
            freqs = t[:, None] * inv_freq[None, :]
            return (jnp.cos(freqs), jnp.sin(freqs))

        def _apply_rope(u, cos, sin):
            half = u.shape[-1] // 2
            c = cos[None, :, None, :]
            s = sin[None, :, None, :]
            u1, u2 = (u[..., :half], u[..., half:2 * half])
            return jnp.concatenate([u1 * c - u2 * s, u1 * s + u2 * c], axis=-1)

        def _deltanet_fwd(x, Wq, Wk, Wv, Wbeta, bbeta, Wo, bo, ln_gamma, ln_beta):
            Bn, Sn, Dm = x.shape
            q = (x @ Wq).reshape(Bn, Sn, H, Dh)
            k = (x @ Wk).reshape(Bn, Sn, H, Dh)
            v = (x @ Wv).reshape(Bn, Sn, H, Dh)
            cos, sin = _rope_cache(Sn, Dh)
            q = _apply_rope(q, cos, sin)
            k = _apply_rope(k, cos, sin)
            phi = lambda u: jax.nn.elu(u) + 1.0
            q_phi, k_phi = (phi(q), phi(k))
            beta = jnp.clip(jax.nn.sigmoid(x @ Wbeta + bbeta).reshape(Bn, Sn, H, C), 0.001, 0.999)

            def tm(u):
                return u.transpose(0, 2, 1, 3).reshape(Bn * H, Sn, -1).transpose(1, 0, 2)
            qs, ks_, vs, bs = (tm(q_phi), tm(k_phi), tm(v), tm(beta))
            BH = Bn * H
            M0 = jnp.zeros((BH, C, Dh, Dh), jnp.float32)
            Z0 = jnp.zeros((BH, C, Dh), jnp.float32)

            def step(carry, inp):
                M, Z = carry
                q_t, k_t, v_t, b_t = inp
                M = M * b_t[:, :, None, None] + (k_t[:, :, None] * v_t[:, None, :])[:, None]
                Z = Z * b_t[:, :, None] + k_t[:, None, :]
                num = jnp.einsum('bd,bcde->be', q_t, M)
                den = jnp.einsum('bd,bcd->b', q_t, Z) + EPS
                return ((M, Z), num / den[:, None])
            _, ys = jax.lax.scan(step, (M0, Z0), (qs, ks_, vs, bs))
            out = ys.transpose(1, 0, 2).reshape(Bn, H, Sn, Dh).transpose(0, 2, 1, 3).reshape(Bn, Sn, Dm)
            out = out @ Wo + bo
            h = x + out
            mu = jnp.mean(h, axis=-1, keepdims=True)
            var = jnp.mean((h - mu) ** 2, axis=-1, keepdims=True)
            return ln_gamma * (h - mu) / jnp.sqrt(var + LN_EPS) + ln_beta
        key = jax.random.key(seed)
        ks = jax.random.split(key, 8)
        w = 0.02
        x = jax.random.normal(ks[0], (B, S, D), jnp.float32)
        Wq = jax.random.normal(ks[1], (D, D), jnp.float32) * w
        Wk = jax.random.normal(ks[2], (D, D), jnp.float32) * w
        Wv = jax.random.normal(ks[3], (D, D), jnp.float32) * w
        Wbeta = jax.random.normal(ks[4], (D, H * C), jnp.float32) * w
        bbeta = jnp.full((H * C,), np.log(0.98 / 0.02), jnp.float32)
        Wo = jax.random.normal(ks[5], (D, D), jnp.float32) * w
        bo = jnp.zeros((D,), jnp.float32)
        ln_gamma = jnp.ones((D,), jnp.float32)
        ln_beta = jnp.zeros((D,), jnp.float32)
        return {'x': x, 'Wq': Wq, 'Wk': Wk, 'Wv': Wv, 'Wbeta': Wbeta, 'bbeta': bbeta, 'Wo': Wo, 'bo': bo, 'ln_gamma': ln_gamma, 'ln_beta': ln_beta}
    _L0_attn_in = _L0_attn_setup()

    def _L0_ffn_setup():
        import jax, jax.numpy as jnp
        import numpy as np
        NUM_EXPERTS = 8
        TOP_K = 2
        CAP_RATIO = 1.25
        INIT_STD = 0.02
        key = jax.random.key(seed)
        k1, k2, k3, k4 = jax.random.split(key, 4)
        B, T, H, F = (4, 256, 128, 512)
        x = jax.random.normal(k1, (B, T, H), jnp.float32)
        router_w = jax.random.normal(k2, (NUM_EXPERTS, H), jnp.float32) * INIT_STD
        w1 = jax.random.normal(k3, (NUM_EXPERTS, H, F), jnp.float32) * INIT_STD
        w2 = jax.random.normal(k4, (NUM_EXPERTS, F, H), jnp.float32) * INIT_STD
        return {'x': x, 'router_w': router_w, 'w1': w1, 'w2': w2}
    _L0_ffn_in = _L0_ffn_setup()
    _L0_c = _w((lambda *s: np.random.randn(*s).astype(np.float32) * 0.05)(2, 128))
    _L0_wmod = _w((lambda *s: np.random.randn(*s).astype(np.float32) * 0.05)(128, 6 * 128) * 128 ** (-0.5))
    _d = {'L0_attn_x': _L0_attn_in['x'], 'L0_attn_Wq': _L0_attn_in['Wq'], 'L0_attn_Wk': _L0_attn_in['Wk'], 'L0_attn_Wv': _L0_attn_in['Wv'], 'L0_attn_Wbeta': _L0_attn_in['Wbeta'], 'L0_attn_bbeta': _L0_attn_in['bbeta'], 'L0_attn_Wo': _L0_attn_in['Wo'], 'L0_attn_bo': _L0_attn_in['bo'], 'L0_attn_ln_gamma': _L0_attn_in['ln_gamma'], 'L0_attn_ln_beta': _L0_attn_in['ln_beta'], 'L0_ffn_router_w': _L0_ffn_in['router_w'], 'L0_ffn_w1': _L0_ffn_in['w1'], 'L0_ffn_w2': _L0_ffn_in['w2'], 'L0_c': _L0_c, 'L0_wmod': _L0_wmod}
    _x0 = _d['L0_attn_x']
    _d['L0_attn_x'] = jax.random.normal(jax.random.fold_in(jax.random.key(seed), 1), (2, 1024, 128), dtype=_x0.dtype)
    del _x0
    return _d

def reference(L0_attn_x, L0_attn_Wq, L0_attn_Wk, L0_attn_Wv, L0_attn_Wbeta, L0_attn_bbeta, L0_attn_Wo, L0_attn_bo, L0_attn_ln_gamma, L0_attn_ln_beta, L0_ffn_router_w, L0_ffn_w1, L0_ffn_w2, L0_c, L0_wmod):

    def _L0_attn_ref(x, Wq, Wk, Wv, Wbeta, bbeta, Wo, bo, ln_gamma, ln_beta):
        import jax, jax.numpy as jnp
        import numpy as np
        B, S, D, H = (2, 256, 128, 16)
        Dh = D // H
        C = 2
        EPS = 1e-06
        LN_EPS = 1e-05

        def _rope_cache(seq_len, dh):
            half = dh // 2
            inv_freq = 1.0 / 10000.0 ** (jnp.arange(0, 2 * half, 2, dtype=jnp.float32) / dh)
            t = jnp.arange(seq_len, dtype=jnp.float32)
            freqs = t[:, None] * inv_freq[None, :]
            return (jnp.cos(freqs), jnp.sin(freqs))

        def _apply_rope(u, cos, sin):
            half = u.shape[-1] // 2
            c = cos[None, :, None, :]
            s = sin[None, :, None, :]
            u1, u2 = (u[..., :half], u[..., half:2 * half])
            return jnp.concatenate([u1 * c - u2 * s, u1 * s + u2 * c], axis=-1)

        def _deltanet_fwd(x, Wq, Wk, Wv, Wbeta, bbeta, Wo, bo, ln_gamma, ln_beta):
            Bn, Sn, Dm = x.shape
            q = (x @ Wq).reshape(Bn, Sn, H, Dh)
            k = (x @ Wk).reshape(Bn, Sn, H, Dh)
            v = (x @ Wv).reshape(Bn, Sn, H, Dh)
            cos, sin = _rope_cache(Sn, Dh)
            q = _apply_rope(q, cos, sin)
            k = _apply_rope(k, cos, sin)
            phi = lambda u: jax.nn.elu(u) + 1.0
            q_phi, k_phi = (phi(q), phi(k))
            beta = jnp.clip(jax.nn.sigmoid(x @ Wbeta + bbeta).reshape(Bn, Sn, H, C), 0.001, 0.999)

            def tm(u):
                return u.transpose(0, 2, 1, 3).reshape(Bn * H, Sn, -1).transpose(1, 0, 2)
            qs, ks_, vs, bs = (tm(q_phi), tm(k_phi), tm(v), tm(beta))
            BH = Bn * H
            M0 = jnp.zeros((BH, C, Dh, Dh), jnp.float32)
            Z0 = jnp.zeros((BH, C, Dh), jnp.float32)

            def step(carry, inp):
                M, Z = carry
                q_t, k_t, v_t, b_t = inp
                M = M * b_t[:, :, None, None] + (k_t[:, :, None] * v_t[:, None, :])[:, None]
                Z = Z * b_t[:, :, None] + k_t[:, None, :]
                num = jnp.einsum('bd,bcde->be', q_t, M)
                den = jnp.einsum('bd,bcd->b', q_t, Z) + EPS
                return ((M, Z), num / den[:, None])
            _, ys = jax.lax.scan(step, (M0, Z0), (qs, ks_, vs, bs))
            out = ys.transpose(1, 0, 2).reshape(Bn, H, Sn, Dh).transpose(0, 2, 1, 3).reshape(Bn, Sn, Dm)
            out = out @ Wo + bo
            h = x + out
            mu = jnp.mean(h, axis=-1, keepdims=True)
            var = jnp.mean((h - mu) ** 2, axis=-1, keepdims=True)
            return ln_gamma * (h - mu) / jnp.sqrt(var + LN_EPS) + ln_beta
        return _deltanet_fwd(x, Wq, Wk, Wv, Wbeta, bbeta, Wo, bo, ln_gamma, ln_beta)

    def _L0_ffn_ref(x, router_w, w1, w2):
        import jax, jax.numpy as jnp
        import numpy as np
        NUM_EXPERTS = 8
        TOP_K = 2
        CAP_RATIO = 1.25
        INIT_STD = 0.02
        B, T, H = x.shape
        E, K = (NUM_EXPERTS, TOP_K)
        xf = x.reshape(-1, H)
        N = xf.shape[0]
        P = N * K
        capacity = int(CAP_RATio * N * K / E) + 1 if False else int(CAP_RATIO * N * K / E) + 1
        logits = xf @ router_w.T
        probs = jax.nn.softmax(logits, axis=-1)
        k_probs, k_idx = jax.lax.top_k(probs, K)
        k_probs = k_probs / jnp.sum(k_probs, axis=-1, keepdims=True)
        flat_e = k_idx.reshape(-1)
        onehot = jax.nn.one_hot(flat_e, E, dtype=jnp.int32)
        rank = jnp.take_along_axis(jnp.cumsum(onehot, axis=0) - 1, flat_e[:, None], axis=1)[:, 0]
        keep = rank < capacity
        slot = jnp.minimum(rank, capacity - 1)
        token_id = jnp.arange(P) // K
        dispatched = jnp.where(keep[:, None], xf[token_id], 0.0)
        buf = jnp.zeros((E, capacity, H), x.dtype).at[flat_e, slot].add(dispatched)
        h = jax.nn.silu(jnp.einsum('ech,ehf->ecf', buf, w1))
        out_buf = jnp.einsum('ecf,efh->ech', h, w2)
        pair_out = out_buf[flat_e, slot] * keep[:, None].astype(x.dtype)
        combined = jnp.sum(pair_out.reshape(N, K, H) * k_probs[..., None], axis=1)
        return combined.reshape(B, T, H) + x
    x = L0_attn_x
    mod = (_silu(L0_c) @ L0_wmod).reshape(L0_c.shape[0], 6, 1, -1)
    sa, ca, ga, sb, cb, gb = (mod[:, 0], mod[:, 1], mod[:, 2], mod[:, 3], mod[:, 4], mod[:, 5])
    ga = (2 * (ga >= 0) - 1) * jnp.maximum(jnp.abs(ga), 0.25)
    gb = (2 * (gb >= 0) - 1) * jnp.maximum(jnp.abs(gb), 0.25)
    h = _layernorm(x, axis=-1) * (1 + ca) + sa
    x = x + ga * _L0_attn_ref(h, L0_attn_Wq, L0_attn_Wk, L0_attn_Wv, L0_attn_Wbeta, L0_attn_bbeta, L0_attn_Wo, L0_attn_bo, L0_attn_ln_gamma, L0_attn_ln_beta)
    h = _layernorm(x, axis=-1) * (1 + cb) + sb
    x = x + gb * _L0_ffn_ref(h, L0_ffn_router_w, L0_ffn_w1, L0_ffn_w2)
    return x

_drawn_inputs = setup_inputs


def setup_inputs(seed=0):
    import zlib

    import numpy as np

    out = dict(_drawn_inputs(seed))
    spreads = {'L0_attn_bbeta': (3.891820192337036, 0.6),
     'L0_attn_bo': (0.0, 0.327),
     'L0_attn_ln_gamma': (1.0, 0.2),
     'L0_attn_ln_beta': (0.0, 0.304)}
    factors = {'L0_attn_Wq': 8.0,
     'L0_attn_Wk': 8.0,
     'L0_attn_Wv': 8.0,
     'L0_attn_Wbeta': 8.0,
     'L0_attn_Wo': 8.0,
     'L0_ffn_router_w': 7.093,
     'L0_ffn_w1': 6.273,
     'L0_ffn_w2': 6.251}
    for name, (base, spread) in spreads.items():
        noise = np.random.default_rng([zlib.crc32(name.encode()), seed]).standard_normal(out[name].shape)
        drawn = base * np.exp(spread * noise) if base else spread * noise
        out[name] = jnp.asarray(drawn.astype(out[name].dtype))
    for name, factor in factors.items():
        out[name] = (out[name] * factor).astype(out[name].dtype)
    return out
```

```python
import numpy as np
import concourse.bass as bass
from concourse import mybir
from contextlib import ExitStack

F32 = mybir.dt.float32
BF16 = mybir.dt.bfloat16
U32 = mybir.dt.uint32
ALU = mybir.AluOpType
ACT = mybir.ActivationFunctionType
AX = mybir.AxisListType

P = 128
B, S, DM = 2, 1024, 128
H, DH, C = 16, 8, 2
HC = H * C
ROPE_HALF = DH // 2
NE, FF = 8, 512
TOPK = 2
NTOK = B * S
PAIRS = NTOK * TOPK
CAP = int(1.25 * PAIRS / NE) + 1
LN_EPS = 1e-5
DEN_EPS = 1e-6

TG = 4
GPB = S // (TG * P)
GROUPS = B * GPB
BLK = 32
BPT = P // BLK
SUB = 8
NSUB = BLK // SUB
HG = 4
NHG = H // HG
E1 = DH + 1
HALF = H // 2
SW = HALF * E1
NB = TG * BPT
GT = TG * P

RW = DM + 2
CM = CAP - 1
CT = CM // P
ARENA = 24064
ROWS = 12 * 512
NHALF = [(0, 321), (321, 320)]
FT = FF // P

_widths = [("ident", P), ("gk", NSUB * P), ("own", P), ("cq", P), ("ck", P), ("kbias", NSUB),
           ("qmask", NSUB), ("causal", BLK), ("hmask", HG), ("smask", SW), ("tri", P), ("blk", BPT),
           ("cos", S // P * ROPE_HALF), ("sin", S // P * ROPE_HALF), ("iota", NE), ("pid", TG * TOPK)]
COL, _at = {}, 0
for _n, _w in _widths:
    COL[_n] = slice(_at, _at + _w)
    _at += _w
NCONST = _at
WALL = 3 * DM + HC
ROWV = 3 * DM + HC


def constants():
    c = np.zeros((P, NCONST), np.float32)
    p = np.arange(P)
    r, t = p[:, None], p[None, :]
    same = r // BLK == t // BLK
    c[:, COL["ident"]] = np.eye(P)
    for i in range(NSUB):
        ref = (t // BLK) * BLK + i * SUB
        plus = same & (r >= ref) & (r <= t)
        minus = same & (r < ref) & (r > t)
        c[:, COL["gk"]][:, i * P:(i + 1) * P] = plus.astype(np.float32) - minus
        c[:, COL["kbias"]][:, i] = np.where(p % BLK < (i + 1) * SUB, 0.0, -1e4)
        c[:, COL["qmask"]][:, i] = (p % BLK) // SUB == i
    c[:, COL["own"]] = (r // SUB == t // SUB) & (r <= t)
    c[:, COL["cq"]] = same & (r <= t)
    c[:, COL["ck"]] = same & (r > t)
    c[:, COL["causal"]] = (p % BLK)[:, None] <= np.arange(BLK)[None, :]
    c[:, COL["hmask"]] = (p // DH % HG)[:, None] == np.arange(HG)[None, :]
    c[:, COL["smask"]] = (p // (C * DH))[:, None] == (np.arange(SW) // E1)[None, :]
    c[:, COL["tri"]] = r < t
    c[:, COL["blk"]] = (p // BLK)[:, None] == np.arange(BPT)[None, :]
    inv = (1.0 / 10000.0 ** (np.arange(0, DH, 2, dtype=np.float32) / np.float32(DH))).astype(np.float32)
    ang = (np.arange(S, dtype=np.float32)[:, None] * inv[None, :]).astype(np.float32)
    tab = lambda f: f(ang).astype(np.float32).reshape(S // P, P, ROPE_HALF).transpose(1, 0, 2).reshape(P, -1)
    c[:, COL["cos"]] = tab(np.cos)
    c[:, COL["sin"]] = tab(np.sin)
    c[:, COL["iota"]] = np.arange(NE)[None, :]
    tok = np.arange(TG)[None, :, None] * P + p[:, None, None]
    c[:, COL["pid"]] = (TOPK * tok + np.arange(TOPK)[None, None, :]).reshape(P, -1)
    return c


class Event:

    def __init__(self, sem, per, ahead):
        self.sem, self.per, self.ahead = sem, per, per if ahead else 0

    def now(self, step, k=None):
        return step * self.per + (self.ahead + (self.per if k is None else k))

    def before(self, step, k=None):
        assert self.ahead
        return step * self.per + (self.per if k is None else k)


def program(nc, x_d, wall_d, wo_d, rows_d, rwt_d, w1_d, w2_d, ct_d, wmod_d, const_d, out_d):
    x_v = x_d.rearrange("b (g t p) c -> (b g) p t c", t=TG, p=P)
    out_v = out_d.rearrange("b (g t p) c -> (b g) p t c", t=TG, p=P)
    disp_d = nc.dram_tensor("dispatched", [ROWS, RW], F32, kind="Internal").ap()
    pair_d = nc.dram_tensor("pair_out", [PAIRS, DM], F32, kind="Internal").ap()
    pair_v = pair_d.rearrange("(g t p k) c -> g p t (k c)", t=TG, p=P, k=TOPK)

    def w1_v(e):
        return w1_d[bass.ds(e, 1), :, :].rearrange("e p f -> p (e f)")

    def w2_v(e):
        return w2_d[bass.ds(e, 1), :, :].rearrange("e (f p) h -> p (e f) h", p=P)

    ctx = ExitStack()
    with ctx:
        def sb(name, shape, dt=F32):
            return ctx.enter_context(nc.sbuf_tensor(name, shape, dt))

        def sem(name):
            return ctx.enter_context(nc.semaphore(name))

        ahead_of = {"dve": [], "act": [], "pe": [], "pool": [], "sp": []}

        def event(name, per, ahead=None):
            e = Event(sem(name), per, ahead)
            if ahead:
                ahead_of[ahead].append(e)
            return e

        const = sb("const", [P, NCONST])
        K = {n: const[:, s] for n, s in COL.items()}
        ident = K["ident"]
        tri_b = sb("tri_b", [P, P], BF16)
        ones_b = sb("ones_b", [P, P], BF16)
        ones_row = sb("ones_row", [1, P])
        vec_row = sb("vec_row", [1, ROWV])
        wall = sb("wall", [P, WALL])
        wo = sb("wo", [P, DM])
        rwt = sb("rwt", [P, NE])
        wmod = sb("wmod", [P, 6 * DM])
        cT = sb("cT", [P, B])
        c_e = sb("c_e", [P, B])
        c_s = sb("c_s", [P, B])
        c_silu = sb("c_silu", [P, B])
        c_rep = sb("c_rep", [P, B, P])
        modc = sb("modc", [P, 4, B])
        vecs = sb("vecs", [P, ROWV])
        mod_b = sb("mod_b", [P, B, 6 * DM])
        gsign = sb("gsign", [P, B, 2, DM])
        gabs = sb("gabs", [P, B, 2, DM])
        gates = sb("gates", [P, B, 2, DM])
        attn_g = sb("attn_g", [P, B, DM])
        attn_b = sb("attn_b", [P, B, DM])
        half_neg = sb("half_neg", [P, TG])
        fill = sb("fill", [P, 4, RW])
        zero = sb("zero", [P, 1024])

        arena = sb("arena", [P, ARENA])

        def carver():
            at = [0]

            def carve(*shape):
                n = int(np.prod(shape))
                v = arena[:, at[0]:at[0] + n]
                at[0] += n
                assert at[0] <= ARENA
                names = "abcd"[:len(shape)]
                return v.rearrange(f"p ({' '.join(names)}) -> p {' '.join(names)}", **dict(zip(names, shape)))

            return carve

        carve = carver()
        X = sb("X", [P, TG, DM])
        XB = sb("XB", [P, TG, DM])
        st6 = sb("st6", [P, TG, 6])
        mv = sb("mv", [P, TG, 2])
        ve = sb("ve", [P, TG])
        rstd = sb("rstd", [P, TG])
        n1 = carve(TG, DM)
        hT = sb("hT", [P, GT])
        raw = carve(TG, WALL)
        zl = sb("zl", [P, TG, HC])
        ze = sb("ze", [P, TG, HC])
        zn = sb("zn", [P, TG, HC])
        rate = sb("rate", [P, TG, HC])
        rrep = carve(TG, 2, HALF * C, DH)
        fk = sb("fk", [P, TG, HC, NSUB])
        ex = sb("ex", [P, 3 * TG * HC + TG * 2 * BPT])
        fq = sb("fq", [P, TG * HC, NSUB])
        m1 = carve(TG, 2 * H, ROPE_HALF)
        m2 = carve(TG, 2 * H, ROPE_HALF)
        m3 = carve(TG, 2 * H, ROPE_HALF)
        m4 = carve(TG, 2 * H, ROPE_HALF)
        rot = carve(TG, 2 * H, DH)
        rmin = carve(TG, 2 * H, DH)
        rexp = carve(TG, 2 * H, DH)
        phi = carve(TG, 2 * H, DH)
        qi = carve(TG, H, C, DH)
        ks = carve(TG, H, C, DH)
        v1 = sb("v1", [P, TG, H, E1])
        vx = carve(TG, BPT, H * E1)
        qx = carve(TG, BPT, HG, BLK)
        fqx = carve(TG, BPT, HG, BLK)
        kT = sb("kT", [P, GT])
        fkT = sb("fkT", [P, GT])
        qiT = sb("qiT", [P, 2, GT])
        state = carve(NB, 2, SW)
        sbd = carve(2, BPT, 2, SW)
        s_sb = sb("s_sb", [P, 2, 2, 2 * P])
        s_mk = sb("s_mk", [P, 2, 4 * HG, BLK])
        wts = sb("wts", [P, 2, 4 * HG, BLK])
        den = sb("den", [P, TG, H])
        rden = sb("rden", [P, TG, H])
        y = sb("y", [P, TG, H, DH])
        yT = sb("yT", [P, GT])
        z3 = sb("z3", [P, TG, DM])
        z3g = sb("z3g", [P, TG, DM])
        x2 = sb("x2", [P, TG, DM])
        n2 = sb("n2", [P, TG, DM])
        h2T = sb("h2T", [P, GT])
        hm = sb("hm", [P, TG, DM])
        gh = sb("gh", [P, TG, DM])
        row = sb("row", [P, TG, TOPK, RW])
        base = sb("base", [P, GROUPS, TG * DM])
        lg = sb("lg", [P, TG, NE])
        mx = sb("mx", [P, TG, NE])
        ix = sb("ix", [P, TG, NE], U32)
        ef = sb("ef", [P, TG, TOPK])
        oh = sb("oh", [P, TG, TOPK, NE])
        msk = sb("msk", [P, TG, NE], BF16)
        pre = sb("pre", [P, TG + 1, NE], BF16)
        rm = sb("rm", [P, TG, TOPK, NE])
        rk = sb("rk", [P, TG, TOPK])
        ov = sb("ov", [P, TG, TOPK])
        sl = sb("sl", [P, TG, TOPK])
        idx = sb("idx", [P, TG, TOPK], U32)
        pid = sb("pid", [P, TG, TOPK])
        dl = sb("dl", [P, TG])
        de = sb("de", [P, TG])
        dp = sb("dp", [P, TG])
        w0 = sb("w0", [P, TG])

        carve = carver()
        w1t = sb("w1t", [P, 2, FF])
        w2t = sb("w2t", [P, 2, FT, DM])
        xb = carve(2, CT, RW)
        lastx = sb("lastx", [NE, RW])
        lastT = sb("lastT", [P, NE + 1])
        lastO = sb("lastO", [P, NE])
        lastR = sb("lastR", [NE, DM])
        bT = carve(2, CAP)
        hid = carve(2, FT, CAP)
        oT = carve(2, CAP)
        meta = sb("meta", [P, 2, CT, 2])
        orow = carve(2, CT, DM)
        yb = carve(2, TG, TOPK, DM)
        ys = carve(2, TG, DM)
        yo = carve(2, TG, DM)

        ps = ctx.enter_context(nc.psum_tensor("ps", [P, 8, 512], F32))
        S_ps = ps[:, 0:4:2, 0:2 * P]
        D_ps = ps[:, 1:4:2, 0:2 * P]
        T4 = ps[:, 4, :]
        T5 = ps[:, 5, :]
        O_ps = ps[:, 6, 0:H * E1]
        U_ps = ps[:, 7, 0:BPT * SW]

        s_const, s_wall, s_vec, s_c, s_wmod = sem("const_in"), sem("wall_in"), sem("vec_in"), sem("c_in"), sem("wmod_in")
        s_small = sem("small_weights_in")
        s_ms = sem("memsets")
        s_dms = sem("vector_memsets")
        s_apart = sem("waits_taken")
        s_fillms = sem("fill_set")
        s_filled = sem("dram_filled")
        s_ce, s_cs, s_csilu, s_crep = sem("c_exp"), sem("c_sig"), sem("c_silu_done"), sem("c_rep_done")
        s_modc, s_modc_sb = sem("modc_ps"), sem("modc_done")
        s_modb, s_modb_sb = sem("modb_ps"), sem("modb_done")
        s_vecp, s_vecs = sem("vecs_ps"), sem("vecs_done")
        s_gate = sem("gates_steps")
        s_trib = sem("tri_done")
        s_state0 = sem("state_zero")

        x_in = event("x_in", 16)
        xb_done = event("x_plus_bias", 1)
        stats = event("ln_stats", 3 * TG)
        aggr = event("ln_mean_var", 3 * TG)
        veps = event("ln_var_eps", 3)
        rstd_done = event("ln_rstd", 3)
        n1_done = event("n1_done", TG)
        n1T = event("n1T_ps", 1)
        hT_done = event("hT_done", 1)
        proj = event("proj_ps", TG)
        raw_done = event("raw_done", TG)
        zadd = event("z_add", 1)
        zclamp = event("z_clamp", 1)
        zexp = event("z_exp", 1)
        zln = event("z_ln", 1)
        rate_done = event("rate_done", 1)
        rrep_done = event("rate_spread", 1)
        expo_ps = event("exponents_ps", 2)
        fk_done = event("fk_done", 1)
        ex_done = event("ex_done", 1, "act")
        fq_done = event("fq_done", 1)
        rope_a = event("rope_dve", 2)
        rope_b = event("rope_pool", 2)
        rot_done = event("rot_done", 2)
        rmin_done = event("rmin_done", 1)
        rexp_done = event("rexp_done", 1)
        phi_done = event("phi_done", 1)
        qi_done = event("qi_done", TG)
        ks_done = event("ks_done", TG)
        v1_done = event("v1_done", 1)
        vx_done = event("vx_done", BPT)
        tq = event("q_T_ps", 1)
        tfq = event("fq_T_ps", 1)
        tk = event("k_T_ps", 1)
        tfk = event("fk_T_ps", 1)
        tqi = event("qi_T_ps", 2)
        qx_done = event("qx_done", 1)
        fqx_done = event("fqx_done", 1)
        kT_done = event("kT_done", 1)
        fkT_done = event("fkT_done", 1)
        qiT_done = event("qiT_act", 1)
        qiT_done1 = event("qiT_dve", 1)
        sd_group = event("sd_head_groups", NHG * TG, "pe")
        s_copied = event("s_copied", TG, "act")
        s_masked = event("s_masked", TG, "pool")
        w_done = event("weights_done", TG, "dve")
        u_ps = event("u_ps", 2 * TG)
        st_done = event("state_done", 2 * NB, "dve")
        sbd_done = event("state_masked", TG)
        att_ps = event("attention_ps", TG, "pe")
        den_done = event("den_done", TG)
        rden_done = event("rden_done", TG)
        y_done = event("y_done", TG, "dve")
        yT_ps = event("yT_ps", 1)
        yT_done = event("yT_done", 1)
        o_ps = event("wo_ps", 1, "pe")
        z3_done = event("z3_done", TG)
        z3g_done = event("z3g_done", 1)
        x2_done = event("x2_done", 1, "dve")
        n2_done = event("n2_done", TG)
        n2T = event("n2T_ps", 1)
        h2T_done = event("h2T_done", 1)
        hm_done = event("h2_scaled", 1)
        h2_done = event("h2_rows", 1)
        row2_done = event("h2_rows_copied", 1)
        gh_done = event("gated_h2", 1)
        base_done = event("base_done", 1)
        lg_ps = event("logits_ps", 1)
        lg_done = event("logits_done", 1)
        mx_done = event("top_done", TG)
        ix_done = event("top_index", TG)
        choice_steps = event("choice_steps", 3)
        pre_done = event("prefix_done", TG + 1)
        rk_ps = event("rank_ps", 1)
        slot_steps = event("slot_steps", 6)
        idx_done = event("slot_index", 1)
        dl_done = event("logit_gap", 1)
        de_done = event("gap_exp", 1)
        wrow_done = event("row_weights", 2)
        prow_done = event("row_ids", 1)
        pid_next = event("ids_next", 1)
        scat = event("dispatched_rows", 16 * TG * TOPK)
        rows_left = event("rows_left", 1, "sp")

        w1_in = [event(f"w1_in{u}", 16) for u in range(2)]
        w2_in = [event(f"w2_in{u}", 16) for u in range(2)]
        xb_in = [event(f"xb_in{u}", 16) for u in range(2)]
        s_lastx, s_lastT, s_lastT_sb = sem("last_in"), sem("last_T"), sem("last_T_sb")
        bT_ps = [event(f"slots_T_ps{u}", 1) for u in range(2)]
        bT_done = [event(f"slots_T{u}", 3, "dve") for u in range(2)]
        meta_done = [event(f"slot_meta{u}", 1) for u in range(2)]
        up_ps = [event(f"up_ps{u}", 2 * FT, "pe") for u in range(2)]
        hid_done = [event(f"hidden{u}", 2 * FT, "act") for u in range(2)]
        dn_ps = [event(f"down_ps{u}", 2, "pe") for u in range(2)]
        oT_done = [event(f"down_T{u}", 3, "dve") for u in range(2)]
        r_ps = [event(f"rows_ps{u}", 1, "pe") for u in range(2)]
        r_done = [event(f"rows_done{u}", CT, "dve") for u in range(2)]
        osc = [event(f"rows_out{u}", 16 * CT) for u in range(2)]
        outs_left = [event(f"outs_left{u}", 1, "sp") for u in range(2)]
        s_lastO, s_lastR, s_lastS = sem("last_out_T"), sem("last_out_rows"), sem("last_rows_out")

        yb_in = [event(f"pairs_in{u}", 16) for u in range(2)]
        ys_done = [event(f"pairs_sum{u}", 1, "dve") for u in range(2)]
        yg_done = [event(f"pairs_gated{u}", 1) for u in range(2)]
        yo_done = [event(f"out_ready{u}", 1) for u in range(2)]
        out_sem = [event(f"out_written{u}", 16, "sp") for u in range(2)]

        def made(n, a):
            t, j = divmod(n - 1, BPT)
            return (2 * t + a) * BPT + j + 1

        block = ctx.enter_context(nc.Block())

        def apart(eng):
            eng.sem_inc(s_apart, 1)

        def start_ahead(eng, who):
            for e in ahead_of[who]:
                eng.sem_inc(e.sem, e.ahead)

        @block.sync
        def _(sp):
            sp.dma_start(const[:], const_d).then_inc(s_const, 16)
            sp.dma_start(vec_row[:], rows_d).then_inc(s_vec, 16)
            sp.dma_start(cT[:], ct_d).then_inc(s_c, 16)
            sp.dma_start(wall[:], wall_d).then_inc(s_wall, 16)
            sp.dma_start(wmod[:], wmod_d).then_inc(s_wmod, 16)
            sp.dma_start(wo[:], wo_d).then_inc(s_small, 16)
            sp.dma_start(rwt[:], rwt_d).then_inc(s_small, 16)
            start_ahead(sp, "sp")
            for u in range(2):
                sp.dma_start(w1t[:, u, :], w1_v(u)).then_inc(w1_in[u].sem, 16)
                sp.dma_start(w2t[:, u], w2_v(u)).then_inc(w2_in[u].sem, 16)
            sp.dma_start(X[:], x_v[0]).then_inc(x_in.sem, 16)
            with sp.Fori(0, GROUPS - 1) as g:
                sp.wait_ge(xb_done.sem, xb_done.now(g))
                sp.dma_start(X[:], x_v[bass.ds(g + 1, 1), :, :, :].rearrange("g p t c -> p (g t) c")).then_inc(x_in.sem, 16)
                sp.wait_ge(scat.sem, scat.now(g))
                sp.sem_inc(rows_left.sem, 1)
            sp.wait_ge(scat.sem, scat.now(GROUPS - 1))
            sp.dma_start(lastx[:], disp_d[0:NE * CAP, :].rearrange("(e s) c -> e s c", s=CAP)[:, CM, :]).then_inc(s_lastx, 16)

            def slots(e):
                return disp_d[bass.ds(e * CAP, CM), :].rearrange("(p a) c -> p (a c)", a=CT)

            for u in range(2):
                sp.dma_start(xb[:, u, :, :].rearrange("p a c -> p (a c)"), slots(u)).then_inc(xb_in[u].sem, 16)
            def next_slots(u, i):
                sp.wait_ge(bT_ps[u].sem, bT_ps[u].now(i))
                sp.wait_ge(meta_done[u].sem, meta_done[u].now(i))
                sp.dma_start(xb[:, u, :, :].rearrange("p a c -> p (a c)"), slots(i * 2 + (u + 2))).then_inc(xb_in[u].sem, 16)

            def outs_gone(u, i):
                sp.wait_ge(osc[u].sem, osc[u].now(i))
                sp.sem_inc(outs_left[u].sem, 1)

            with sp.Fori(0, NE // 2 - 1) as i:
                next_slots(0, i)
                sp.wait_ge(up_ps[0].sem, up_ps[0].now(i))
                sp.dma_start(w1t[:, 0, :], w1_v(i * 2 + 2)).then_inc(w1_in[0].sem, 16)
                next_slots(1, i)
                sp.wait_ge(dn_ps[0].sem, dn_ps[0].now(i))
                sp.dma_start(w2t[:, 0], w2_v(i * 2 + 2)).then_inc(w2_in[0].sem, 16)
                sp.wait_ge(up_ps[1].sem, up_ps[1].now(i))
                sp.dma_start(w1t[:, 1, :], w1_v(i * 2 + 3)).then_inc(w1_in[1].sem, 16)
                outs_gone(0, i)
                sp.wait_ge(dn_ps[1].sem, dn_ps[1].now(i))
                sp.dma_start(w2t[:, 1], w2_v(i * 2 + 3)).then_inc(w2_in[1].sem, 16)
                outs_gone(1, i)
            next_slots(0, NE // 2 - 1)
            outs_gone(0, NE // 2 - 1)
            sp.wait_ge(s_lastS, 16)
            with sp.Fori(0, B) as b:
                for u in range(2):
                    sp.wait_ge(ys_done[u].sem, ys_done[u].before(b))
                    sp.dma_start(yb[:, u].rearrange("p t k c -> p t (k c)"),
                                 pair_v[bass.ds(b * GPB + u, 1), :, :, :].rearrange("g p t c -> p (g t) c")).then_inc(yb_in[u].sem, 16)
                for u in range(2):
                    sp.wait_ge(yo_done[u].sem, yo_done[u].now(b))
                    sp.dma_start(out_v[bass.ds(b * GPB + u, 1), :, :, :].rearrange("g p t c -> p (g t) c"), yo[:, u]).then_inc(out_sem[u].sem, 16)
            for u in range(2):
                sp.wait_ge(out_sem[u].sem, out_sem[u].now(B - 1))

        @block.gpsimd
        def _(pool):
            g_ = nc.gpsimd
            g_.memset(half_neg[:], -0.5).then_inc(s_ms, 1)
            g_.memset(ones_row[:], 1.0).then_inc(s_ms, 1)
            g_.memset(ones_b[:], 1.0).then_inc(s_ms, 1)
            start_ahead(pool, "pool")
            pool.wait_ge(s_ms, 3)
            pool.wait_ge(s_modb_sb, 1)
            pool.wait_ge(s_gate, 7)
            with pool.Fori(0, B) as b:
                with pool.Fori(0, GPB) as gg:
                    g = b * GPB + gg
                    bb = bass.ds(b, 1)
                    pool.wait_ge(veps.sem, veps.now(g, 1))
                    g_.tensor_tensor(rstd[:], ve[:], half_neg[:], ALU.pow).then_inc(rstd_done.sem, 1)
                    pool.wait_ge(x_in.sem, x_in.now(g))
                    pool.wait_ge(x2_done.sem, x2_done.before(g))
                    pool.wait_ge(n1_done.sem, n1_done.now(g))
                    g_.tensor_tensor(XB[:], X[:], attn_b[:, bb, :].to_broadcast([P, TG, DM]), ALU.add).then_inc(xb_done.sem, 1)
                    pool.wait_ge(raw_done.sem, raw_done.now(g))
                    uv = raw[:, :, 0:2 * DM].rearrange("p t (h r d) -> p t h r d", r=2, d=ROPE_HALF)

                    def table(n):
                        v = K[n].rearrange("p (g t d) -> p g t d", g=GPB, t=TG)[:, bass.ds(gg, 1), :, :]
                        return v.rearrange("p g t d -> p (g t) d").unsqueeze(2).to_broadcast([P, TG, 2 * H, ROPE_HALF])

                    g_.tensor_tensor(m3[:], uv[:, :, :, 0, :], table("sin"), ALU.mult).then_inc(rope_b.sem, 1)
                    g_.tensor_tensor(m4[:], uv[:, :, :, 1, :], table("cos"), ALU.mult).then_inc(rope_b.sem, 1)
                    pool.wait_ge(ex_done.sem, ex_done.now(g))
                    g_.tensor_tensor(fq[:], ex[:, 0:TG * HC].unsqueeze(2).to_broadcast([P, TG * HC, NSUB]),
                                     K["qmask"].unsqueeze(1).to_broadcast([P, TG * HC, NSUB]), ALU.mult).then_inc(fq_done.sem, 1)
                    pool.wait_ge(phi_done.sem, phi_done.now(g))
                    for t in range(TG):
                        f = ex[:, (2 * TG + t) * HC:(2 * TG + t + 1) * HC].rearrange("p (h c) -> p h c", c=C)
                        g_.tensor_tensor(ks[:, t], phi[:, t, H:2 * H, :].unsqueeze(2).to_broadcast([P, H, C, DH]),
                                         f.unsqueeze(3).to_broadcast([P, H, C, DH]), ALU.mult).then_inc(ks_done.sem, 1)
                    for t in range(TG):
                        pool.wait_ge(s_copied.sem, s_copied.now(g, t + 1))
                        if t >= 2:
                            pool.wait_ge(w_done.sem, w_done.now(g, t - 1))
                        else:
                            pool.wait_ge(w_done.sem, w_done.before(g, TG - 1 + t))
                        g_.tensor_tensor(s_mk[:, t % 2], s_sb[:, t % 2].rearrange("p a (h t) -> p (a h) t", t=BLK),
                                         K["causal"].unsqueeze(1).to_broadcast([P, H, BLK]), ALU.mult).then_inc(s_masked.sem, 1)
                        pool.wait_ge(st_done.sem, st_done.now(g, made(BPT * t + BPT - 1, 1)))
                        if t >= 2:
                            pool.wait_ge(att_ps.sem, att_ps.now(g, t - 1))
                        else:
                            pool.wait_ge(att_ps.sem, att_ps.before(g, TG - 1 + t))
                        g_.tensor_tensor(sbd[:, t % 2].rearrange("p j a w -> p (j a) w"),
                                         state[:, BPT * t:BPT * (t + 1)].rearrange("p j a w -> p (j a) w"),
                                         K["smask"].unsqueeze(1).to_broadcast([P, BPT * 2, SW]), ALU.mult).then_inc(sbd_done.sem, 1)
                    pool.wait_ge(veps.sem, veps.now(g, 2))
                    g_.tensor_tensor(rstd[:], ve[:], half_neg[:], ALU.pow).then_inc(rstd_done.sem, 1)
                    pool.wait_ge(veps.sem, veps.now(g, 3))
                    g_.tensor_tensor(rstd[:], ve[:], half_neg[:], ALU.pow).then_inc(rstd_done.sem, 1)
                    pool.wait_ge(n2_done.sem, n2_done.now(g))
                    g_.tensor_tensor(hm[:], n2[:], mod_b[:, bb, 4 * DM:5 * DM].to_broadcast([P, TG, DM]), ALU.mult).then_inc(hm_done.sem, 1)
                    pool.wait_ge(hm_done.sem, hm_done.now(g))
                    pool.wait_ge(rows_left.sem, rows_left.before(g))
                    g_.tensor_tensor(row[:, :, 0, 0:DM], hm[:], mod_b[:, bb, 3 * DM:4 * DM].to_broadcast([P, TG, DM]), ALU.add).then_inc(h2_done.sem, 1)
                    pool.wait_ge(h2_done.sem, h2_done.now(g))
                    g_.tensor_tensor(gh[:], row[:, :, 0, 0:DM], gates[:, bb, 1, :].to_broadcast([P, TG, DM]), ALU.mult).then_inc(gh_done.sem, 1)
                    pool.wait_ge(s_filled, 16 * 16)
                    pool.wait_ge(row2_done.sem, row2_done.now(g))
                    pool.wait_ge(idx_done.sem, idx_done.now(g))
                    pool.wait_ge(wrow_done.sem, wrow_done.now(g))
                    pool.wait_ge(prow_done.sem, prow_done.now(g))
                    apart(pool)
                    for t in range(TG):
                        for k in range(TOPK):
                            pool.indirect_dma_start(disp_d, bass.IndirectOffsetOnAxis(ap=idx[:, t, k:k + 1], axis=0),
                                                    row[:, t, k, :], None, bounds_check=ROWS - 1, oob_is_err=False).then_inc(scat.sem, 16)
            with pool.Fori(0, NE // 2) as i:
                for u in range(2):
                    pool.wait_ge(r_done[u].sem, r_done[u].now(i))
                    apart(pool)
                    for a in range(CT):
                        pool.indirect_dma_start(pair_d, bass.IndirectOffsetOnAxis(ap=meta[:, u, a, 0:1].bitcast(U32), axis=0),
                                                orow[:, u, a, :], None, bounds_check=PAIRS - 1, oob_is_err=False).then_inc(osc[u].sem, 16)
            pool.wait_ge(s_lastR, 2)
            for u in range(2):
                pool.wait_ge(osc[u].sem, osc[u].now(NE // 2 - 1))
            pool.indirect_dma_start(pair_d, bass.IndirectOffsetOnAxis(ap=lastx[:, DM:DM + 1].bitcast(U32), axis=0),
                                    lastR[:], None, bounds_check=PAIRS - 1, oob_is_err=False).then_inc(s_lastS, 16)

        @block.scalar
        def _(act):
            a_ = nc.scalar
            act.preload_act_table_set("natural_log_exp_and_others")
            act.wait_ge(s_fillms, 3)
            for n in range(12):
                act.dma_start(disp_d[512 * n:512 * n + 512, :].rearrange("(p a) c -> p (a c)", a=4),
                              fill[:].rearrange("p a c -> p (a c)")).then_inc(s_filled, 16)
            for n in range(4):
                act.dma_start(pair_d[1024 * n:1024 * n + 1024, :].rearrange("(p a) c -> p (a c)", a=8), zero[:]).then_inc(s_filled, 16)
            start_ahead(act, "act")
            act.wait_ge(s_cs, 1)
            a_.activation(c_e[:], c_s[:], ACT.Exp, scale=-1.0).then_inc(s_ce, 1)
            with act.Fori(0, B) as b:
                with act.Fori(0, GPB) as gg:
                    g = b * GPB + gg
                    bb = bass.ds(b, 1)
                    act.wait_ge(n1T.sem, n1T.now(g))
                    act.wait_ge(s_modc_sb, 2)
                    act.wait_ge(o_ps.sem, o_ps.before(g))
                    a_.activation(hT[:], T4, ACT.Identity, bias=modc[:, 0, bb], scale=modc[:, 1, bb]).then_inc(hT_done.sem, 1)
                    for t in range(TG):
                        act.wait_ge(proj.sem, proj.now(g, t + 1))
                        a_.copy(raw[:, t, :], ps[:, 5 - t % 2, 0:WALL]).then_inc(raw_done.sem, 1)
                    act.wait_ge(zclamp.sem, zclamp.now(g))
                    a_.activation(ze[:], zl[:], ACT.Exp, scale=-1.0).then_inc(zexp.sem, 1)
                    act.wait_ge(zexp.sem, zexp.now(g))
                    a_.activation(zn[:], ze[:], ACT.Ln, bias=1.0).then_inc(zln.sem, 1)
                    act.wait_ge(s_dms, 1)
                    act.wait_ge(att_ps.sem, att_ps.before(g))
                    act.wait_ge(raw_done.sem, raw_done.now(g))
                    a_.copy(v1[:, :, :, 0:DH], raw[:, :, 2 * DM:3 * DM].rearrange("p t (h d) -> p t h d", d=DH)).then_inc(v1_done.sem, 1)
                    act.wait_ge(v1_done.sem, v1_done.now(g))
                    for j in range(BPT):
                        a_.mul(vx[:, :, j, :], v1[:].rearrange("p t h e -> p t (h e)"), K["blk"][:, j:j + 1]).then_inc(vx_done.sem, 1)
                    act.wait_ge(expo_ps.sem, expo_ps.now(g))
                    for i in range(NSUB):
                        f = a_.activation(fk[:].rearrange("p t h i -> p (t h) i")[:, :, i], T5[:, i * TG * HC:(i + 1) * TG * HC],
                                          ACT.Exp, bias=K["kbias"][:, i:i + 1])
                    f.then_inc(fk_done.sem, 1)
                    a_.activation(ex[:], T4[:, 0:3 * TG * HC + TG * 2 * BPT], ACT.Exp, scale=-1.0).then_inc(ex_done.sem, 1)
                    act.wait_ge(rmin_done.sem, rmin_done.now(g))
                    a_.activation(rexp[:], rmin[:], ACT.Exp).then_inc(rexp_done.sem, 1)
                    act.wait_ge(tfq.sem, tfq.now(g))
                    for j in range(HG):
                        f = a_.mul(fqx[:, :, :, j, :].rearrange("p t b s -> p (t b) s"),
                                   T5.rearrange("p (n s) -> p n s", s=BLK), K["hmask"][:, j:j + 1])
                    f.then_inc(fqx_done.sem, 1)
                    act.wait_ge(tk.sem, tk.now(g))
                    a_.copy(kT[:], T4).then_inc(kT_done.sem, 1)
                    act.wait_ge(tqi.sem, tqi.now(g, 1))
                    a_.copy(qiT[:, 0, :], T4).then_inc(qiT_done.sem, 1)
                    for t in range(TG):
                        act.wait_ge(sd_group.sem, sd_group.now(g, NHG * (t + 1)))
                        if t >= 2:
                            act.wait_ge(s_masked.sem, s_masked.now(g, t - 1))
                        else:
                            act.wait_ge(s_masked.sem, s_masked.before(g, TG - 1 + t))
                        a_.copy(s_sb[:, t % 2], S_ps).then_inc(s_copied.sem, 1)
                    act.wait_ge(yT_ps.sem, yT_ps.now(g))
                    a_.copy(yT[:], T4).then_inc(yT_done.sem, 1)
                    act.wait_ge(n2T.sem, n2T.now(g))
                    a_.activation(h2T[:], T4, ACT.Identity, bias=modc[:, 2, bb], scale=modc[:, 3, bb]).then_inc(h2T_done.sem, 1)
                    act.wait_ge(h2_done.sem, h2_done.now(g))
                    a_.copy(row[:, :, 1, 0:DM], row[:, :, 0, 0:DM]).then_inc(row2_done.sem, 1)
                    act.wait_ge(dl_done.sem, dl_done.now(g))
                    a_.activation(de[:], dl[:], ACT.Exp).then_inc(de_done.sem, 1)
            act.preload_act_table(ACT.Silu)
            with act.Fori(0, NE // 2) as i:
                for u in range(2):
                    for f in range(FT):
                        for n, (c0, cn) in enumerate(NHALF):
                            k = 2 * f + n
                            act.wait_ge(up_ps[u].sem, up_ps[u].now(i, k + 1))
                            if k == 0:
                                act.wait_ge(dn_ps[u].sem, dn_ps[u].before(i))
                            a_.activation(hid[:, u, f, c0:c0 + cn], ps[:, 2 + n, 0:cn], ACT.Silu).then_inc(hid_done[u].sem, 1)

        @block.vector
        def _(dve):
            v_ = nc.vector
            v_.memset(fill[:], 0.0).then_inc(s_fillms, 1)
            v_.memset(zero[:], 0.0).then_inc(s_fillms, 1)
            dve.wait_ge(s_fillms, 2)
            v_.memset(fill[:, :, DM:DM + 1], 1e9).then_inc(s_fillms, 1)
            v_.memset(v1[:, :, :, DH:E1], 1.0).then_inc(s_dms, 1)
            v_.memset(pre[:], 0.0).then_inc(s_dms, 1)
            start_ahead(dve, "dve")
            dve.wait_ge(s_c, 16)
            v_.tensor_scalar(c_s[:], cT[:], -80.0, None, ALU.max).then_inc(s_cs, 1)
            dve.wait_ge(s_ce, 1)
            v_.tensor_scalar(c_s[:], c_e[:], 1.0, None, ALU.add).then_inc(s_cs, 1)
            dve.wait_ge(s_cs, 2)
            v_.reciprocal(c_e[:], c_s[:]).then_inc(s_cs, 1)
            dve.wait_ge(s_cs, 3)
            v_.tensor_tensor(c_silu[:], cT[:], c_e[:], ALU.mult).then_inc(s_csilu, 1)
            dve.wait_ge(s_csilu, 1)
            v_.tensor_copy(c_rep[:], c_silu[:].unsqueeze(2).to_broadcast([P, B, P])).then_inc(s_crep, 1)
            dve.wait_ge(s_vecp, 1)
            v_.tensor_copy(vecs[:], ps[:, 1, 0:ROWV]).then_inc(s_vecs, 1)
            dve.wait_ge(s_modc, 1)
            v_.tensor_copy(modc[:], ps[:, 0, 0:4 * B].rearrange("p (j b) -> p j b", b=B)).then_inc(s_modc_sb, 1)
            dve.wait_ge(s_modc_sb, 1)
            v_.tensor_scalar(modc[:, 1:4:2, :], modc[:, 1:4:2, :], 1.0, None, ALU.add).then_inc(s_modc_sb, 1)
            dve.wait_ge(s_modb, 1)
            mb = ps[:, 2:6, :].rearrange("p (b w) n -> p b (w n)", b=B)[:, :, 0:6 * DM]
            v_.tensor_copy(mod_b[:], mb).then_inc(s_gate, 1)
            dve.wait_ge(s_gate, 1)
            gv = mod_b[:].rearrange("p b (j c) -> p b j c", c=DM)[:, :, 2:6:3, :]
            v_.tensor_scalar(gsign[:], gv, 0.0, 2.0, ALU.is_ge, ALU.mult).then_inc(s_gate, 1)
            v_.tensor_scalar(gates[:], gv, -1.0, 0.25, ALU.mult, ALU.max).then_inc(s_gate, 1)
            dve.wait_ge(s_gate, 3)
            v_.tensor_tensor(gabs[:], gates[:], gv, ALU.max).then_inc(s_gate, 1)
            dve.wait_ge(s_gate, 4)
            for n in range(2):
                v_.scalar_tensor_tensor(gates[:, :, n, :], gsign[:, :, n, :], -1.0, gabs[:, :, n, :], ALU.add, ALU.mult).then_inc(s_gate, 1)
            dve.wait_ge(s_gate, 6)
            v_.tensor_scalar(mod_b[:, :, 4 * DM:5 * DM], mod_b[:, :, 4 * DM:5 * DM], 1.0, None, ALU.add).then_inc(s_modb_sb, 1)
            dve.wait_ge(s_vecs, 1)
            v_.tensor_tensor(attn_g[:], gates[:, :, 0, :], vecs[:, DM:2 * DM].unsqueeze(1).to_broadcast([P, B, DM]), ALU.mult).then_inc(s_modb_sb, 1)
            v_.tensor_tensor(attn_b[:], gates[:, :, 0, :], vecs[:, 2 * DM:3 * DM].unsqueeze(1).to_broadcast([P, B, DM]), ALU.mult).then_inc(s_gate, 1)
            dve.wait_ge(s_const, 16)
            v_.tensor_copy(tri_b[:], K["tri"]).then_inc(s_trib, 1)
            v_.tensor_copy(pid[:], K["pid"].rearrange("p (t k) -> p t k", k=TOPK)).then_inc(s_trib, 1)
            dve.wait_ge(s_trib, 2)
            dve.wait_ge(s_modb_sb, 2)
            dve.wait_ge(s_gate, 7)
            dve.wait_ge(s_dms, 2)

            def layernorm(src, g, n):
                for t in range(TG):
                    v_.bn_stats(st6[:, t, :], src[:, t, :]).then_inc(stats.sem, 1)
                for t in range(TG):
                    dve.wait_ge(stats.sem, stats.now(g, n * TG + t + 1))
                    apart(dve)
                    v_.bn_aggr(mv[:, t, :], st6[:, t, :]).then_inc(aggr.sem, 1)
                dve.wait_ge(aggr.sem, aggr.now(g, (n + 1) * TG))
                v_.tensor_scalar(ve[:], mv[:, :, 1], LN_EPS, None, ALU.add).then_inc(veps.sem, 1)
                dve.wait_ge(rstd_done.sem, rstd_done.now(g, n + 1))

            with dve.Fori(0, B) as b:
                dve.wait_ge(st_done.sem, st_done.before(b * GPB))
                v_.memset(state[:, 0], 0.0).then_inc(s_state0, 1)
                with dve.Fori(0, GPB) as gg:
                    g = b * GPB + gg
                    bb = bass.ds(b, 1)
                    dve.wait_ge(x_in.sem, x_in.now(g))
                    layernorm(X, g, 0)
                    for t in range(TG):
                        v_.tensor_scalar(n1[:, t, :], X[:, t, :], mv[:, t, 0:1], rstd[:, t:t + 1], ALU.subtract, ALU.mult).then_inc(n1_done.sem, 1)
                    dve.wait_ge(raw_done.sem, raw_done.now(g))
                    v_.tensor_tensor(zn[:], raw[:, :, 3 * DM:WALL], vecs[:, 3 * DM:ROWV].unsqueeze(1).to_broadcast([P, TG, HC]), ALU.add).then_inc(zadd.sem, 1)
                    dve.wait_ge(zadd.sem, zadd.now(g))
                    v_.tensor_scalar(zl[:], zn[:], -30.0, None, ALU.max).then_inc(zclamp.sem, 1)
                    uv = raw[:, :, 0:2 * DM].rearrange("p t (h r d) -> p t h r d", r=2, d=ROPE_HALF)

                    def table(n):
                        v = K[n].rearrange("p (g t d) -> p g t d", g=GPB, t=TG)[:, bass.ds(gg, 1), :, :]
                        return v.rearrange("p g t d -> p (g t) d").unsqueeze(2).to_broadcast([P, TG, 2 * H, ROPE_HALF])

                    v_.tensor_tensor(m1[:], uv[:, :, :, 0, :], table("cos"), ALU.mult).then_inc(rope_a.sem, 1)
                    v_.tensor_tensor(m2[:], uv[:, :, :, 1, :], table("sin"), ALU.mult).then_inc(rope_a.sem, 1)
                    dve.wait_ge(zln.sem, zln.now(g))
                    v_.tensor_scalar(rate[:], zn[:], float(-np.log(0.999)), float(-np.log(0.001)), ALU.max, ALU.min).then_inc(rate_done.sem, 1)
                    dve.wait_ge(rate_done.sem, rate_done.now(g))
                    v_.tensor_copy(rrep[:].rearrange("p t a h d -> p (t a h) d"),
                                   rate[:].rearrange("p t h -> p (t h)").unsqueeze(2).to_broadcast([P, TG * HC, DH])).then_inc(rrep_done.sem, 1)
                    rv = rot[:].rearrange("p t h (r d) -> p t h r d", d=ROPE_HALF)
                    dve.wait_ge(rope_a.sem, rope_a.now(g))
                    v_.tensor_tensor(rv[:, :, :, 0, :], m1[:], m2[:], ALU.subtract).then_inc(rot_done.sem, 1)
                    dve.wait_ge(rope_b.sem, rope_b.now(g))
                    v_.tensor_tensor(rv[:, :, :, 1, :], m3[:], m4[:], ALU.add).then_inc(rot_done.sem, 1)
                    dve.wait_ge(rot_done.sem, rot_done.now(g))
                    v_.tensor_scalar(rmin[:], rot[:], 0.0, None, ALU.min).then_inc(rmin_done.sem, 1)
                    dve.wait_ge(rexp_done.sem, rexp_done.now(g))
                    v_.scalar_tensor_tensor(phi[:].rearrange("p t h d -> p (t h d)"), rot[:].rearrange("p t h d -> p (t h d)"), 1.0,
                                            rexp[:].rearrange("p t h d -> p (t h d)"), ALU.add, ALU.max).then_inc(phi_done.sem, 1)
                    dve.wait_ge(phi_done.sem, phi_done.now(g))
                    dve.wait_ge(ex_done.sem, ex_done.now(g))
                    for t in range(TG):
                        f = ex[:, (TG + t) * HC:(TG + t + 1) * HC].rearrange("p (h c) -> p h c", c=C)
                        v_.tensor_tensor(qi[:, t], phi[:, t, 0:H, :].unsqueeze(2).to_broadcast([P, H, C, DH]),
                                         f.unsqueeze(3).to_broadcast([P, H, C, DH]), ALU.mult).then_inc(qi_done.sem, 1)
                    dve.wait_ge(tq.sem, tq.now(g))
                    for j in range(HG):
                        f = v_.tensor_scalar(qx[:, :, :, j, :].rearrange("p t b s -> p (t b) s"),
                                             T4.rearrange("p (n s) -> p n s", s=BLK), K["hmask"][:, j:j + 1], None, ALU.mult)
                    f.then_inc(qx_done.sem, 1)
                    dve.wait_ge(tfk.sem, tfk.now(g))
                    v_.tensor_copy(fkT[:], T5).then_inc(fkT_done.sem, 1)
                    dve.wait_ge(tqi.sem, tqi.now(g))
                    v_.tensor_copy(qiT[:, 1, :], T5).then_inc(qiT_done1.sem, 1)
                    dve.wait_ge(s_state0, b + 1)

                    def states(t, a):
                        dve.wait_ge(u_ps.sem, u_ps.now(g, 2 * t + a + 1))
                        for j in range(BPT):
                            n = BPT * t + j
                            dec = 3 * TG * HC + (t * 2 + a) * BPT + j
                            if n:
                                dve.wait_ge(st_done.sem, st_done.now(g, made(n, a)))
                            else:
                                dve.wait_ge(st_done.sem, st_done.before(g))
                            if n == NB - 1 and a == 0:
                                dve.wait_ge(sbd_done.sem, sbd_done.now(g, 1))
                            v_.scalar_tensor_tensor(state[:, (n + 1) % NB, a, :], state[:, n, a, :], ex[:, dec:dec + 1],
                                                    U_ps[:, j * SW:(j + 1) * SW], ALU.mult, ALU.add).then_inc(st_done.sem, 1)

                    states(0, 0)
                    states(0, 1)
                    for t in range(TG):
                        dve.wait_ge(sd_group.sem, sd_group.now(g, NHG * (t + 1)))
                        dve.wait_ge(s_masked.sem, s_masked.now(g, t + 1))
                        if t >= 2:
                            dve.wait_ge(att_ps.sem, att_ps.now(g, t - 1))
                        else:
                            dve.wait_ge(att_ps.sem, att_ps.before(g, TG - 1 + t))
                        v_.tensor_tensor(wts[:, t % 2].rearrange("p (a h) t -> p a (h t)", a=2), s_mk[:, t % 2].rearrange("p (a h) t -> p a (h t)", a=2),
                                         D_ps, ALU.mult).then_inc(w_done.sem, 1)
                        if t + 1 < TG:
                            states(t + 1, 0)
                            states(t + 1, 1)
                        dve.wait_ge(att_ps.sem, att_ps.now(g, t + 1))
                        ov_ = O_ps.rearrange("p (h e) -> p h e", e=E1)
                        v_.tensor_scalar(den[:, t, :], ov_[:, :, DH], DEN_EPS, None, ALU.add).then_inc(den_done.sem, 1)
                        dve.wait_ge(den_done.sem, den_done.now(g, t + 1))
                        v_.reciprocal(rden[:, t, :], den[:, t, :]).then_inc(rden_done.sem, 1)
                        dve.wait_ge(rden_done.sem, rden_done.now(g, t + 1))
                        v_.tensor_tensor(y[:, t], ov_[:, :, 0:DH], rden[:, t, :].unsqueeze(2).to_broadcast([P, H, DH]), ALU.mult).then_inc(y_done.sem, 1)
                    dve.wait_ge(o_ps.sem, o_ps.now(g))
                    O3 = T5.rearrange("p (t c) -> p t c", c=DM)
                    layernorm(O3, g, 1)
                    for t in range(TG):
                        v_.tensor_scalar(z3[:, t, :], O3[:, t, :], mv[:, t, 0:1], rstd[:, t:t + 1], ALU.subtract, ALU.mult).then_inc(z3_done.sem, 1)
                    dve.wait_ge(z3_done.sem, z3_done.now(g))
                    v_.tensor_tensor(z3g[:], z3[:], attn_g[:, bb, :].to_broadcast([P, TG, DM]), ALU.mult).then_inc(z3g_done.sem, 1)
                    dve.wait_ge(z3g_done.sem, z3g_done.now(g))
                    dve.wait_ge(xb_done.sem, xb_done.now(g))
                    v_.tensor_tensor(x2[:], z3g[:], XB[:], ALU.add).then_inc(x2_done.sem, 1)
                    dve.wait_ge(x2_done.sem, x2_done.now(g))
                    layernorm(x2, g, 2)
                    for t in range(TG):
                        v_.tensor_scalar(n2[:, t, :], x2[:, t, :], mv[:, t, 0:1], rstd[:, t:t + 1], ALU.subtract, ALU.mult).then_inc(n2_done.sem, 1)
                    dve.wait_ge(lg_ps.sem, lg_ps.now(g))
                    v_.tensor_copy(lg[:], T5[:, 0:TG * NE].rearrange("p (t e) -> p t e", e=NE)).then_inc(lg_done.sem, 1)
                    dve.wait_ge(lg_done.sem, lg_done.now(g))
                    apart(dve)
                    for t in range(TG):
                        v_.max(mx[:, t, :], lg[:, t, :]).then_inc(mx_done.sem, 1)
                    for t in range(TG):
                        dve.wait_ge(mx_done.sem, mx_done.now(g, t + 1))
                        apart(dve)
                        v_.max_index(ix[:, t, :], mx[:, t, :], lg[:, t, :]).then_inc(ix_done.sem, 1)
                    v_.tensor_tensor(dl[:], mx[:, :, 1], mx[:, :, 0], ALU.subtract).then_inc(dl_done.sem, 1)
                    dve.wait_ge(ix_done.sem, ix_done.now(g))
                    v_.tensor_copy(ef[:], ix[:, :, 0:TOPK]).then_inc(choice_steps.sem, 1)
                    v_.tensor_copy(pre[:, 0, :], pre[:, TG, :]).then_inc(pre_done.sem, 1)
                    dve.wait_ge(choice_steps.sem, choice_steps.now(g, 1))
                    v_.tensor_tensor(oh[:], K["iota"].unsqueeze(1).unsqueeze(1).to_broadcast([P, TG, TOPK, NE]),
                                     ef[:].unsqueeze(3).to_broadcast([P, TG, TOPK, NE]), ALU.is_equal).then_inc(choice_steps.sem, 1)
                    dve.wait_ge(choice_steps.sem, choice_steps.now(g, 2))
                    v_.tensor_tensor(msk[:], oh[:, :, 0, :], oh[:, :, 1, :], ALU.add).then_inc(choice_steps.sem, 1)
                    dve.wait_ge(choice_steps.sem, choice_steps.now(g, 3))
                    for t in range(TG):
                        dve.wait_ge(pre_done.sem, pre_done.now(g, t + 1))
                        v_.tensor_tensor(pre[:, t + 1, :], pre[:, t, :], msk[:, t, :], ALU.add).then_inc(pre_done.sem, 1)
                    dve.wait_ge(rk_ps.sem, rk_ps.now(g))
                    rkv = T5[:, 64:64 + TG * NE].rearrange("p (t e) -> p t e", e=NE)
                    for k in range(TOPK):
                        f = v_.tensor_tensor(rm[:, :, k, :], oh[:, :, k, :], rkv, ALU.mult)
                    f.then_inc(slot_steps.sem, 1)
                    dve.wait_ge(slot_steps.sem, slot_steps.now(g, 1))
                    v_.tensor_reduce(rk[:], rm[:], AX.X, ALU.add).then_inc(slot_steps.sem, 1)
                    dve.wait_ge(slot_steps.sem, slot_steps.now(g, 2))
                    v_.tensor_scalar(ov[:], rk[:], float(CAP), 1e6, ALU.is_ge, ALU.mult).then_inc(slot_steps.sem, 1)
                    v_.scalar_tensor_tensor(sl[:], ef[:], float(CAP), rk[:], ALU.mult, ALU.add).then_inc(slot_steps.sem, 1)
                    dve.wait_ge(slot_steps.sem, slot_steps.now(g, 3))
                    dve.wait_ge(slot_steps.sem, slot_steps.now(g, 4))
                    dve.wait_ge(rows_left.sem, rows_left.before(g))
                    v_.tensor_tensor(idx[:], sl[:], ov[:], ALU.add).then_inc(idx_done.sem, 1)
                    dve.wait_ge(de_done.sem, de_done.now(g))
                    v_.tensor_scalar(dp[:], de[:], 1.0, None, ALU.add).then_inc(slot_steps.sem, 1)
                    dve.wait_ge(slot_steps.sem, slot_steps.now(g, 5))
                    v_.reciprocal(w0[:], dp[:]).then_inc(slot_steps.sem, 1)
                    dve.wait_ge(slot_steps.sem, slot_steps.now(g, 6))
                    v_.tensor_copy(row[:, :, 0, DM + 1], w0[:]).then_inc(wrow_done.sem, 1)
                    v_.tensor_tensor(row[:, :, 1, DM + 1], w0[:], de[:], ALU.mult).then_inc(wrow_done.sem, 1)
                    v_.tensor_copy(row[:, :, :, DM:DM + 1].bitcast(U32).rearrange("p t k o -> p t (k o)"), pid[:]).then_inc(prow_done.sem, 1)
                    dve.wait_ge(prow_done.sem, prow_done.now(g))
                    v_.tensor_scalar(pid[:], pid[:], float(GT * TOPK), None, ALU.add).then_inc(pid_next.sem, 1)
                    dve.wait_ge(pid_next.sem, pid_next.now(g))
                    dve.wait_ge(gh_done.sem, gh_done.now(g))
                    v_.tensor_tensor(base[:, bass.ds(g, 1), :], x2[:].rearrange("p t c -> p (t c)").unsqueeze(1),
                                     gh[:].rearrange("p t c -> p (t c)").unsqueeze(1), ALU.add).then_inc(base_done.sem, 1)

            dve.wait_ge(s_lastT, 1)
            v_.tensor_copy(lastT[:, 0:NE], T4[:, 0:NE]).then_inc(s_lastT_sb, 1)
            v_.memset(lastT[:, NE:NE + 1], 0.0).then_inc(s_lastT_sb, 1)
            dve.wait_ge(s_lastT_sb, 2)

            def slots_T(u, i, e):
                dve.wait_ge(bT_ps[u].sem, bT_ps[u].now(i))
                dve.wait_ge(up_ps[u].sem, up_ps[u].before(i))
                v_.tensor_copy(bT[:, u, 0:512], ps[:, 0, :]).then_inc(bT_done[u].sem, 1)
                v_.tensor_copy(bT[:, u, 512:CM], ps[:, 1, 0:P]).then_inc(bT_done[u].sem, 1)
                v_.tensor_copy(bT[:, u, CM:CAP], lastT[:, bass.ds(e, 1)] if not isinstance(e, int) else lastT[:, e:e + 1]).then_inc(bT_done[u].sem, 1)

                dve.wait_ge(outs_left[u].sem, outs_left[u].before(i))
                v_.tensor_copy(meta[:, u], xb[:, u, :, DM:RW]).then_inc(meta_done[u].sem, 1)

            def down_T(u, i):
                for n, (c0, cn) in enumerate(NHALF):
                    dve.wait_ge(dn_ps[u].sem, dn_ps[u].now(i, n + 1))
                    if n == 0:
                        dve.wait_ge(r_ps[u].sem, r_ps[u].before(i))
                    v_.tensor_copy(oT[:, u, c0:c0 + cn], ps[:, 4 + n, 0:cn]).then_inc(oT_done[u].sem, 1)
                dve.wait_ge(oT_done[u].sem, oT_done[u].now(i, 2))
                v_.tensor_copy(lastO[:, bass.ds(i * 2 + u, 1)], oT[:, u, CM:CAP]).then_inc(oT_done[u].sem, 1)

            def rows(u, i):
                dve.wait_ge(r_ps[u].sem, r_ps[u].now(i))
                dve.wait_ge(outs_left[u].sem, outs_left[u].before(i))
                for a in range(CT):
                    v_.tensor_scalar(orow[:, u, a, :], ps[:, 6 + a // 4, (a % 4) * P:(a % 4 + 1) * P], meta[:, u, a, 1:2], None, ALU.mult).then_inc(r_done[u].sem, 1)

            slots_T(0, 0, 0)
            with dve.Fori(0, NE // 2) as i:
                slots_T(1, i, i * 2 + 1)
                down_T(0, i)
                rows(0, i)
                slots_T(0, i + 1, i * 2 + 2)
                down_T(1, i)
                rows(1, i)
            dve.wait_ge(s_lastO, 1)
            v_.tensor_scalar(lastR[:], T4[0:NE, 0:P], lastx[:, DM + 1:RW], None, ALU.mult).then_inc(s_lastR, 2)
            with dve.Fori(0, B) as b:
                for u in range(2):
                    dve.wait_ge(yb_in[u].sem, yb_in[u].now(b))
                    v_.tensor_tensor(ys[:, u], yb[:, u, :, 0, :], yb[:, u, :, 1, :], ALU.add).then_inc(ys_done[u].sem, 1)
                    dve.wait_ge(ys_done[u].sem, ys_done[u].now(b))
                    v_.tensor_tensor(ys[:, u], ys[:, u], gates[:, bass.ds(b, 1), 1, :].to_broadcast([P, TG, DM]), ALU.mult).then_inc(yg_done[u].sem, 1)
                    dve.wait_ge(yg_done[u].sem, yg_done[u].now(b))
                    dve.wait_ge(out_sem[u].sem, out_sem[u].before(b))
                    v_.tensor_tensor(yo[:, u].rearrange("p t c -> p (t c)").unsqueeze(1), ys[:, u].rearrange("p t c -> p (t c)").unsqueeze(1),
                                     base[:, bass.ds(b * GPB + u, 1), :], ALU.add).then_inc(yo_done[u].sem, 1)

        @block.tensor
        def _(pe):
            mm = nc.tensor.matmul
            start_ahead(pe, "pe")
            pe.wait_ge(s_vec, 16)
            pe.wait_ge(s_ms, 3)
            mm(ps[:, 1, 0:ROWV], ones_row[:], vec_row[:], start=True, stop=True).then_inc(s_vecp, 1)
            pe.wait_ge(s_wmod, 16)
            pe.wait_ge(s_csilu, 1)
            for n, j in enumerate((0, 1, 3, 4)):
                f = mm(ps[:, 0, n * B:(n + 1) * B], wmod[:, j * DM:(j + 1) * DM], c_silu[:], start=True, stop=True)
            f.then_inc(s_modc, 1)
            pe.wait_ge(s_crep, 1)
            for b in range(B):
                mm(ps[:, 2 + 2 * b, :], c_rep[:, b, :], wmod[:, 0:512], start=True, stop=True)
                f = mm(ps[:, 3 + 2 * b, 0:256], c_rep[:, b, :], wmod[:, 512:768], start=True, stop=True)
            f.then_inc(s_modb, 1)
            pe.wait_ge(s_const, 16)
            pe.wait_ge(s_wall, 16)
            pe.wait_ge(s_small, 32)
            pe.wait_ge(s_trib, 2)
            pe.wait_ge(s_gate, 1)

            def tr(out, in_, **kw):
                return nc.tensor.transpose(out, in_, ident[0:in_.shape[0], 0:in_.shape[0]])

            with pe.Fori(0, GROUPS) as g:
                pe.wait_ge(n1_done.sem, n1_done.now(g))
                for t in range(TG):
                    f = tr(T4[:, t * P:(t + 1) * P], n1[:, t, :])
                f.then_inc(n1T.sem, 1)
                pe.wait_ge(hT_done.sem, hT_done.now(g))
                for t in range(TG):
                    if t >= 2:
                        pe.wait_ge(raw_done.sem, raw_done.now(g, t - 1))
                    mm(ps[:, 5 - t % 2, 0:WALL], hT[:, t * P:(t + 1) * P], wall[:], start=True, stop=True).then_inc(proj.sem, 1)
                pe.wait_ge(raw_done.sem, raw_done.now(g))
                pe.wait_ge(rate_done.sem, rate_done.now(g))
                rv = rate[:].rearrange("p t h -> p (t h)")
                for i in range(NSUB):
                    f = mm(T5[:, i * TG * HC:(i + 1) * TG * HC], K["gk"][:, i * P:(i + 1) * P], rv, start=True, stop=True)
                f.then_inc(expo_ps.sem, 1)
                for i, n in enumerate(("own", "cq", "ck")):
                    mm(T4[:, i * TG * HC:(i + 1) * TG * HC], K[n], rv, start=True, stop=True)
                pe.wait_ge(rrep_done.sem, rrep_done.now(g))
                for t in range(TG):
                    for a in range(2):
                        at = 3 * TG * HC + (2 * t + a) * BPT
                        f = mm(T4[:, at:at + BPT], rrep[:, t, a].rearrange("p h d -> p (h d)"),
                               K["blk"], start=True, stop=True)
                f.then_inc(expo_ps.sem, 1)
                pe.wait_ge(phi_done.sem, phi_done.now(g))
                pe.wait_ge(ex_done.sem, ex_done.now(g))
                for t in range(TG):
                    f = tr(T4[:, t * P:(t + 1) * P], phi[:, t, 0:H, :].rearrange("p h d -> p (h d)"))
                f.then_inc(tq.sem, 1)
                pe.wait_ge(fq_done.sem, fq_done.now(g))
                fqv = fq[:].rearrange("p (t h) i -> p t (h i)", t=TG)
                for t in range(TG):
                    f = tr(T5[:, t * P:(t + 1) * P], fqv[:, t, :])
                f.then_inc(tfq.sem, 1)
                pe.wait_ge(qx_done.sem, qx_done.now(g))
                for t in range(TG):
                    f = tr(T4[:, t * P:(t + 1) * P], phi[:, t, H:2 * H, :].rearrange("p h d -> p (h d)"))
                f.then_inc(tk.sem, 1)
                pe.wait_ge(fqx_done.sem, fqx_done.now(g))
                for t in range(TG):
                    f = tr(T5[:, t * P:(t + 1) * P], fk[:, t].rearrange("p h i -> p (h i)"))
                f.then_inc(tfk.sem, 1)
                pe.wait_ge(qi_done.sem, qi_done.now(g))
                pe.wait_ge(kT_done.sem, kT_done.now(g))
                pe.wait_ge(fkT_done.sem, fkT_done.now(g))
                for a in range(2):
                    for t in range(TG):
                        f = tr(ps[:, 4 + a, t * P:(t + 1) * P], qi[:, t, a * HALF:(a + 1) * HALF].rearrange("p h c d -> p (h c d)"))
                    f.then_inc(tqi.sem, 1)

                def attention(t):
                    pe.wait_ge(sbd_done.sem, sbd_done.now(g, t + 1))
                    pe.wait_ge(y_done.sem, y_done.now(g, t) if t else y_done.before(g))
                    for j in range(BPT):
                        for a in range(2):
                            mm(O_ps[j * BLK:(j + 1) * BLK, a * SW:(a + 1) * SW], qiT[:, a, t * P + j * BLK:t * P + (j + 1) * BLK],
                               sbd[:, t % 2, j, a, :], start=(a == 0), stop=False, skip_group_check=True, tile_position=(0, j * BLK))
                    pe.wait_ge(w_done.sem, w_done.now(g, t + 1))
                    apart(pe)
                    for n in range(H):
                        h = ((n % 8) // HG * 2 + n // 8) * HG + n % HG
                        for j in range(BPT):
                            r = slice(j * BLK, (j + 1) * BLK)
                            f = mm(O_ps[r, h * E1:(h + 1) * E1], wts[r, t % 2, n, :], v1[r, t, h, :], start=False, stop=True,
                                   skip_group_check=True, tile_position=(j * BLK, j * BLK))
                    f.then_inc(att_ps.sem, 1)

                pe.wait_ge(qiT_done.sem, qiT_done.now(g))
                pe.wait_ge(qiT_done1.sem, qiT_done1.now(g))
                pe.wait_ge(vx_done.sem, vx_done.now(g))
                pe.wait_ge(ks_done.sem, ks_done.now(g))
                def adds(t, a):
                    if t or a:
                        pe.wait_ge(st_done.sem, st_done.now(g, (2 * t + a) * BPT))
                    else:
                        pe.wait_ge(st_done.sem, st_done.before(g))
                    mm(U_ps, ks[:, t, a * HALF:(a + 1) * HALF].rearrange("p h c d -> p (h c d)"),
                       vx[:, t, :, a * SW:(a + 1) * SW], start=True, stop=True).then_inc(u_ps.sem, 1)

                def scores(t):
                    pe.wait_ge(s_copied.sem, s_copied.now(g, t) if t else s_copied.before(g))
                    pe.wait_ge(w_done.sem, w_done.now(g, t) if t else w_done.before(g))
                    apart(pe)
                    for hg in range(NHG):
                        if hg >= 2:
                            pe.wait_ge(sd_group.sem, sd_group.now(g, NHG * t + hg - 1))
                            apart(pe)
                        r = slice(hg * 32, hg * 32 + 32)
                        for w, (st, mv_) in enumerate(((kT, qx), (fkT, fqx))):
                            for j in range(BPT):
                                f = mm(ps[j * BLK:(j + 1) * BLK, 2 * (hg % 2) + w, hg // 2 * P:(hg // 2 + 1) * P],
                                       st[r, t * P + j * BLK:t * P + (j + 1) * BLK], mv_[r, t, j].rearrange("p h s -> p (h s)"),
                                       start=True, stop=True, tile_position=(hg * 32, j * BLK))
                        f.then_inc(sd_group.sem, 1)

                adds(0, 0)
                scores(0)
                adds(0, 1)
                for t in range(TG):
                    if t + 1 < TG:
                        adds(t + 1, 0)
                        scores(t + 1)
                        adds(t + 1, 1)
                    attention(t)
                pe.wait_ge(y_done.sem, y_done.now(g))
                for t in range(TG):
                    f = tr(T4[:, t * P:(t + 1) * P], y[:, t].rearrange("p h d -> p (h d)"))
                f.then_inc(yT_ps.sem, 1)
                pe.wait_ge(yT_done.sem, yT_done.now(g))
                for t in range(TG):
                    o = T5[:, t * P:(t + 1) * P]
                    mm(o, yT[:, t * P:(t + 1) * P], wo[:], start=True, stop=False)
                    mm(o, hT[:, t * P:(t + 1) * P], ident, start=False, stop=False)
                    f = mm(o, ones_row[:], vec_row[:, 0:DM], start=False, stop=True)
                f.then_inc(o_ps.sem, 1)
                pe.wait_ge(n2_done.sem, n2_done.now(g))
                for t in range(TG):
                    f = tr(T4[:, t * P:(t + 1) * P], n2[:, t, :])
                f.then_inc(n2T.sem, 1)
                pe.wait_ge(h2T_done.sem, h2T_done.now(g))
                for t in range(TG):
                    f = mm(T5[:, t * NE:(t + 1) * NE], h2T[:, t * P:(t + 1) * P], rwt[:], start=True, stop=True)
                f.then_inc(lg_ps.sem, 1)
                pe.wait_ge(lg_done.sem, lg_done.now(g))
                pe.wait_ge(pre_done.sem, pre_done.now(g))
                rk_o = T5[:, 64:64 + TG * NE]
                mm(rk_o, tri_b[:], msk[:].rearrange("p t e -> p (t e)"), start=True, stop=False)
                mm(rk_o, ones_b[:], pre[:, 0:TG, :].rearrange("p t e -> p (t e)"), start=False, stop=True).then_inc(rk_ps.sem, 1)

            pe.wait_ge(s_lastx, 16)
            tr(T4[:, 0:NE], lastx[:, 0:DM]).then_inc(s_lastT, 1)

            def slots_T(u, i):
                pe.wait_ge(xb_in[u].sem, xb_in[u].now(i))
                if u == 0:
                    pe.wait_ge(bT_done[1].sem, bT_done[1].before(i))
                else:
                    pe.wait_ge(bT_done[0].sem, bT_done[0].now(i))
                for a in range(CT):
                    f = tr(ps[:, a // 4, (a % 4) * P:(a % 4 + 1) * P], xb[:, u, a, 0:DM])
                f.then_inc(bT_ps[u].sem, 1)

            def up(u, i):
                pe.wait_ge(w1_in[u].sem, w1_in[u].now(i))
                pe.wait_ge(bT_done[u].sem, bT_done[u].now(i))
                for f in range(FT):
                    for n, (c0, cn) in enumerate(NHALF):
                        k = 2 * f + n
                        if k >= 2:
                            pe.wait_ge(hid_done[u].sem, hid_done[u].now(i, k - 1))
                        elif u:
                            pe.wait_ge(hid_done[0].sem, hid_done[0].now(i, 2 * FT - 1 + k))
                        else:
                            pe.wait_ge(hid_done[1].sem, hid_done[1].before(i, 2 * FT - 1 + k))
                        mm(ps[:, 2 + n, 0:cn], w1t[:, u, f * P:(f + 1) * P], bT[:, u, c0:c0 + cn], start=True, stop=True).then_inc(up_ps[u].sem, 1)

            def down(u, i):
                pe.wait_ge(w2_in[u].sem, w2_in[u].now(i))
                pe.wait_ge(hid_done[u].sem, hid_done[u].now(i))
                for n, (c0, cn) in enumerate(NHALF):
                    if u:
                        pe.wait_ge(oT_done[0].sem, oT_done[0].now(i, n + 1))
                    else:
                        pe.wait_ge(oT_done[1].sem, oT_done[1].before(i, n + 1))
                    for f in range(FT):
                        m = mm(ps[:, 4 + n, 0:cn], w2t[:, u, f, :], hid[:, u, f, c0:c0 + cn], start=(f == 0), stop=(f == FT - 1))
                    m.then_inc(dn_ps[u].sem, 1)

            def rows(u, i):
                pe.wait_ge(oT_done[u].sem, oT_done[u].now(i, 2))
                if u:
                    pe.wait_ge(r_done[0].sem, r_done[0].now(i))
                else:
                    pe.wait_ge(r_done[1].sem, r_done[1].before(i))
                for a in range(CT):
                    f = tr(ps[:, 6 + a // 4, (a % 4) * P:(a % 4 + 1) * P], oT[:, u, a * P:(a + 1) * P])
                f.then_inc(r_ps[u].sem, 1)

            slots_T(0, 0)
            with pe.Fori(0, NE // 2) as i:
                up(0, i)
                slots_T(1, i)
                down(0, i)
                up(1, i)
                rows(0, i)
                slots_T(0, i + 1)
                down(1, i)
                rows(1, i)
            pe.wait_ge(oT_done[1].sem, oT_done[1].now(NE // 2 - 1))
            tr(T4[0:NE, 0:P], lastO[:]).then_inc(s_lastO, 1)


_OUT = ((B, S, DM), "float32")


def kernel(**inputs):
    import concourse.bacc as _bacc
    from concourse.bass_utils import run_bass_kernel_spmd as _run

    a = {k: np.asarray(v) for k, v in inputs.items()}
    arrays = {
        "x": a["L0_attn_x"],
        "wall": np.concatenate([a["L0_attn_Wq"], a["L0_attn_Wk"], a["L0_attn_Wv"], a["L0_attn_Wbeta"]], axis=1),
        "wo": a["L0_attn_Wo"],
        "rows": np.concatenate([a["L0_attn_bo"], a["L0_attn_ln_gamma"], a["L0_attn_ln_beta"], a["L0_attn_bbeta"]])[None, :],
        "rwt": a["L0_ffn_router_w"].T,
        "w1": a["L0_ffn_w1"],
        "w2": a["L0_ffn_w2"],
        "ct": a["L0_c"].T,
        "wmod": a["L0_wmod"],
        "constants": constants(),
    }
    arrays = {f"in_{k}": np.ascontiguousarray(v) for k, v in arrays.items()}
    nc = _bacc.Bacc("TRN2", target_bir_lowering=False, num_devices=1)
    args = [nc.dram_tensor(n, v.shape, mybir.dt.from_np(v.dtype), kind="ExternalInput").ap() for n, v in arrays.items()]
    out = nc.dram_tensor("out", _OUT[0], F32, kind="ExternalOutput").ap()
    program(nc, *args, out)
    r = _run(nc, [arrays], core_ids=[0])
    return r.results[0]["out"]
```

```python
import numpy as np
import concourse.bass as bass
from concourse import mybir
from contextlib import ExitStack

F32 = mybir.dt.float32
BF16 = mybir.dt.bfloat16
U32 = mybir.dt.uint32
ALU = mybir.AluOpType
ACT = mybir.ActivationFunctionType
AX = mybir.AxisListType

P = 128
B, S, DM = 2, 1024, 128
H, DH, C = 16, 8, 2
HC = H * C
ROPE_HALF = DH // 2
NE, FF = 8, 512
TOPK = 2
NTOK = B * S
PAIRS = NTOK * TOPK
CAP = int(1.25 * PAIRS / NE) + 1
LN_EPS = 1e-5
DEN_EPS = 1e-6

TG = 4
GPB = S // (TG * P)
GROUPS = B * GPB
BLK = 32
BPT = P // BLK
SUB = 8
NSUB = BLK // SUB
HG = 4
NHG = H // HG
E1 = DH + 1
HALF = H // 2
SW = HALF * E1
NB = TG * BPT
GT = TG * P

RW = DM + 2
CM = CAP - 1
CT = CM // P
ARENA = 24064
ROWS = 12 * 512
NHALF = [(0, 321), (321, 320)]
FT = FF // P

_widths = [("ident", P), ("gk", NSUB * P), ("own", P), ("cq", P), ("ck", P), ("kbias", NSUB),
           ("qmask", NSUB), ("causal", BLK), ("hmask", HG), ("smask", SW), ("tri", P), ("spread", P), ("tile_half", TG * 2 * BPT), ("blk", BPT),
           ("cos", GROUPS * TG * ROPE_HALF), ("sin", GROUPS * TG * ROPE_HALF), ("keep", GROUPS), ("iota", NE), ("pid", TG * TOPK)]
COL, _at = {}, 0
for _n, _w in _widths:
    COL[_n] = slice(_at, _at + _w)
    _at += _w
NCONST = _at
WALL = 3 * DM + HC
ROWV = 3 * DM + HC


def constants():
    c = np.zeros((P, NCONST), np.float32)
    p = np.arange(P)
    r, t = p[:, None], p[None, :]
    same = r // BLK == t // BLK
    c[:, COL["ident"]] = np.eye(P)
    for i in range(NSUB):
        ref = (t // BLK) * BLK + i * SUB
        plus = same & (r >= ref) & (r <= t)
        minus = same & (r < ref) & (r > t)
        c[:, COL["gk"]][:, i * P:(i + 1) * P] = plus.astype(np.float32) - minus
        c[:, COL["kbias"]][:, i] = np.where(p % BLK < (i + 1) * SUB, 0.0, -1e4)
        c[:, COL["qmask"]][:, i] = (p % BLK) // SUB == i
    c[:, COL["own"]] = (r // SUB == t // SUB) & (r <= t)
    c[:, COL["cq"]] = same & (r <= t)
    c[:, COL["ck"]] = same & (r > t)
    c[:, COL["causal"]] = (p % BLK)[:, None] <= np.arange(BLK)[None, :]
    c[:, COL["hmask"]] = (p // DH % HG)[:, None] == np.arange(HG)[None, :]
    c[:, COL["smask"]] = (p // (C * DH))[:, None] == (np.arange(SW) // E1)[None, :]
    c[:, COL["tri"]] = r < t
    c[:, COL["spread"]] = r % (HALF * C) == t // DH
    col = np.arange(TG * 2 * BPT)[None, :] // BPT
    c[:, COL["tile_half"]] = (p // (HALF * C))[:, None] == col
    c[:, COL["blk"]] = (p // BLK)[:, None] == np.arange(BPT)[None, :]
    inv = (1.0 / 10000.0 ** (np.arange(0, DH, 2, dtype=np.float32) / np.float32(DH))).astype(np.float32)
    ang = (np.arange(S, dtype=np.float32)[:, None] * inv[None, :]).astype(np.float32)
    tab = lambda f: np.tile(f(ang).astype(np.float32).reshape(S // P, P, ROPE_HALF).transpose(1, 0, 2).reshape(P, -1), (1, B))
    c[:, COL["cos"]] = tab(np.cos)
    c[:, COL["sin"]] = tab(np.sin)
    c[:, COL["keep"]] = (np.arange(GROUPS) % GPB != 0)[None, :]
    c[:, COL["iota"]] = np.arange(NE)[None, :]
    tok = np.arange(TG)[None, :, None] * P + p[:, None, None]
    c[:, COL["pid"]] = (TOPK * tok + np.arange(TOPK)[None, None, :]).reshape(P, -1)
    return c


class Event:

    def __init__(self, sem, per, ahead):
        self.sem, self.per, self.ahead = sem, per, per if ahead else 0

    def now(self, step, k=None):
        return step * self.per + (self.ahead + (self.per if k is None else k))

    def before(self, step, k=None):
        assert self.ahead
        return step * self.per + (self.per if k is None else k)


def program(nc, x_d, wall_d, wo_d, rows_d, rwt_d, w1_d, w2_d, ct_d, wmod_d, const_d, bo_d, out_d):
    x_v = x_d.rearrange("b (g t p) c -> (b g) p t c", t=TG, p=P)
    out_v = out_d.rearrange("b (g t p) c -> (b g) p t c", t=TG, p=P)
    disp_d = nc.dram_tensor("dispatched", [ROWS, RW], F32, kind="Internal").ap()
    pair_d = nc.dram_tensor("pair_out", [PAIRS, DM], F32, kind="Internal").ap()
    pair_v = pair_d.rearrange("(g t p k) c -> g p t (k c)", t=TG, p=P, k=TOPK)

    def w1_v(e):
        return w1_d[bass.ds(e, 1), :, :].rearrange("e p f -> p (e f)")

    def w2_v(e):
        return w2_d[bass.ds(e, 1), :, :].rearrange("e (f p) h -> p (e f) h", p=P)

    ctx = ExitStack()
    with ctx:
        def sb(name, shape, dt=F32):
            return ctx.enter_context(nc.sbuf_tensor(name, shape, dt))

        def sem(name):
            return ctx.enter_context(nc.semaphore(name))

        ahead_of = {"dve": [], "act": [], "pe": [], "pool": [], "sp": []}

        def event(name, per, ahead=None):
            e = Event(sem(name), per, ahead)
            if ahead:
                ahead_of[ahead].append(e)
            return e

        const = sb("const", [P, NCONST])
        K = {n: const[:, s] for n, s in COL.items()}
        ident = K["ident"]
        tri_b = sb("tri_b", [P, P], BF16)
        ones_b = sb("ones_b", [P, P], BF16)
        ones_row = sb("ones_row", [1, P])
        vec_row = sb("vec_row", [1, ROWV])
        wall = sb("wall", [P, WALL])
        wo = sb("wo", [P, DM])
        rwt = sb("rwt", [P, NE])
        wmod = sb("wmod", [P, 6 * DM])
        cT = sb("cT", [P, B])
        c_e = sb("c_e", [P, B])
        c_s = sb("c_s", [P, B])
        c_silu = sb("c_silu", [P, B])
        c_rep = sb("c_rep", [P, B, P])
        modc = sb("modc", [P, 4, GROUPS])
        vecs = sb("vecs", [P, ROWV])
        gates = sb("gates", [P, B, 2, DM])
        attn_g = sb("attn_g", [P, B, GPB, DM])
        attn_b = sb("attn_b", [P, B, GPB, DM])
        gate_b = sb("gate_b", [P, B, GPB, DM])
        half_neg = sb("half_neg", [P, GROUPS + 1, TG])
        fill = sb("fill", [P, 4, RW])
        zero = sb("zero", [P, 1024])

        arena = sb("arena", [P, ARENA])

        def carver():
            at = [0]

            def carve(*shape):
                n = int(np.prod(shape))
                v = arena[:, at[0]:at[0] + n]
                at[0] += n
                assert at[0] <= ARENA
                names = "abcd"[:len(shape)]
                return v.rearrange(f"p ({' '.join(names)}) -> p {' '.join(names)}", **dict(zip(names, shape)))

            return carve

        carve = carver()
        X = sb("X", [P, GROUPS, TG * DM])
        st6 = sb("st6", [P, GROUPS + 1, TG, 6])
        mv = sb("mv", [P, GROUPS + 1, TG, 2])
        ve = sb("ve", [P, GROUPS + 1, TG])
        rstd = sb("rstd", [P, GROUPS + 1, TG])
        mod_b = carve(B, 6 * DM)
        gsign = carve(B, 2, DM)
        gabs = carve(B, 2, DM)
        n1 = carve(TG, DM)
        hT = sb("hT", [P, GT])
        h_keep = sb("h_keep", [P, GT])
        bo_col = sb("bo_col", [P, 1])
        raw = carve(TG, WALL)
        zl = sb("zl", [P, TG, HC])
        ze = sb("ze", [P, TG, HC])
        zn = sb("zn", [P, TG, HC])
        rate = sb("rate", [P, TG, HC])
        sums = sb("sums", [P, TG * 2, BPT])
        fk = sb("fk", [P, TG, HC, NSUB])
        ex = sb("ex", [P, 3 * TG * HC + TG * 2 * BPT])
        dec = sb("dec", [P, TG * 2 * BPT])
        fq = sb("fq", [P, TG * HC, NSUB])
        m1 = carve(TG, 2 * H, ROPE_HALF)
        m2 = carve(TG, 2 * H, ROPE_HALF)
        m3 = carve(TG, 2 * H, ROPE_HALF)
        m4 = carve(TG, 2 * H, ROPE_HALF)
        rot = carve(TG, 2 * H, DH)
        rmin = carve(TG, 2 * H, DH)
        rexp = carve(TG, 2 * H, DH)
        phi = carve(TG, 2 * H, DH)
        qi = carve(TG, H, C, DH)
        ks = carve(TG, H, C, DH)
        v1 = sb("v1", [P, TG, H, E1])
        vx = carve(TG, BPT, H * E1)
        qx = carve(TG, BPT, HG, BLK)
        fqx = carve(TG, BPT, HG, BLK)
        kT = sb("kT", [P, GT])
        fkT = sb("fkT", [P, GT])
        qiT = sb("qiT", [P, 2, GT])
        state = carve(NB, 2, SW)
        sbd = carve(2, BPT, 2, SW)
        s_sb = sb("s_sb", [P, 2, 2, 2 * P])
        s_mk = sb("s_mk", [P, 2, 4 * HG, BLK])
        wts = sb("wts", [P, 2, 4 * HG, BLK])
        den = sb("den", [P, TG, H])
        rden = sb("rden", [P, TG, H])
        y = sb("y", [P, TG, H, DH])
        yT = sb("yT", [P, GT])
        z3 = sb("z3", [P, TG, DM])
        z3g = sb("z3g", [P, TG, DM])
        x2 = sb("x2", [P, TG, DM])
        n2 = sb("n2", [P, TG, DM])
        h2T = sb("h2T", [P, GT])
        gh = sb("gh", [P, TG, DM])
        row = sb("row", [P, TG, TOPK, RW])
        lg = sb("lg", [P, TG, NE])
        mx = sb("mx", [P, TG, NE])
        ix = sb("ix", [P, TG, NE], U32)
        ef = sb("ef", [P, TG, TOPK])
        oh = sb("oh", [P, TG, TOPK, NE])
        msk = sb("msk", [P, TG, NE], BF16)
        pre = sb("pre", [P, TG + 1, NE], BF16)
        rm = sb("rm", [P, TG, TOPK, NE])
        rk = sb("rk", [P, TG, TOPK])
        ov = sb("ov", [P, TG, TOPK])
        sl = sb("sl", [P, TG, TOPK])
        idx = sb("idx", [P, TG, TOPK], U32)
        pid = sb("pid", [P, TG, TOPK])
        dl = sb("dl", [P, TG])
        de = sb("de", [P, TG])
        dp = sb("dp", [P, TG])
        w0 = sb("w0", [P, TG])

        carve = carver()
        w1t = sb("w1t", [P, 2, FF])
        w2t = sb("w2t", [P, 2, FT, DM])
        xb = carve(2, CT, RW)
        lastx = sb("lastx", [NE, RW])
        lastT = sb("lastT", [P, NE + 1])
        lastO = sb("lastO", [P, NE])
        lastR = sb("lastR", [NE, DM])
        bT = carve(2, CAP)
        hid = carve(2, FT, CAP)
        oT = carve(2, CAP)
        meta = sb("meta", [P, 2, CT, 2])
        orow = carve(2, CT, DM)
        yb = carve(GROUPS, TG, TOPK, DM)
        ys = carve(GROUPS, TG, DM)
        yo = carve(GROUPS, TG, DM)

        ps = ctx.enter_context(nc.psum_tensor("ps", [P, 8, 512], F32))
        S_ps = ps[:, 0:4:2, 0:2 * P]
        D_ps = ps[:, 1:4:2, 0:2 * P]
        T4 = ps[:, 4, :]
        T5 = ps[:, 5, :]
        T6 = ps[:, 6, :]
        T7 = ps[:, 7, :]
        O_ps = ps[:, 6, 0:H * E1]
        U_ps = ps[:, 7, 0:BPT * SW]

        s_const, s_wall, s_vec, s_c, s_wmod = sem("const_in"), sem("wall_in"), sem("vec_in"), sem("c_in"), sem("wmod_in")
        s_small = sem("small_weights_in")
        s_ms = sem("memsets")
        s_bo = sem("bo_in")
        s_dms = sem("vector_memsets")
        s_apart = sem("waits_taken")
        s_fillms = sem("fill_set")
        s_filled = sem("dram_filled")
        s_ce, s_cs, s_csilu, s_crep = sem("c_exp"), sem("c_sig"), sem("c_silu_done"), sem("c_rep_done")
        s_modc, s_modc_sb = sem("modc_ps"), sem("modc_done")
        s_modb, s_modb_sb = sem("modb_ps"), sem("modb_done")
        s_vecp, s_vecs = sem("vecs_ps"), sem("vecs_done")
        s_gate = sem("gates_steps")
        s_trib = sem("tri_done")
        s_state0 = sem("state_zero")
        s_tables = sem("group_tables")

        s_x0, s_x = sem("first_x_in"), sem("x_in")
        xb_done = event("x_plus_bias", 1)
        keep_done = event("h_kept", 1)
        dec_done = event("decays_kept", 1)
        carry_done = event("state_carried", 1)
        stats_a, stats_b = event("ln_a_stats", 2 * TG + 1), event("ln_b_stats", 2 * (2 * TG + 1))
        s_rstd, rstd_done = sem("ln_a_rstd"), event("ln_b_rstd", 2)
        n1_done = event("n1_done", TG)
        n1T = event("n1T_ps", 1)
        hT_done = event("hT_done", 1)
        proj = event("proj_ps", TG)
        raw_done = event("raw_done", TG)
        zadd = event("z_add", 1)
        zclamp = event("z_clamp", 1)
        zexp = event("z_exp", 1)
        zln = event("z_ln", 1)
        rate_done = event("rate_done", 1)
        sum_ps = event("block_rates_ps", 1)
        sums_done = event("block_rates", 1)
        expo_ps = event("exponents_ps", 2)
        fk_done = event("fk_done", 1)
        ex_done = event("ex_done", 1, "act")
        fq_done = event("fq_done", 1)
        rope_a = event("rope_dve", 2)
        rope_b = event("rope_pool", 2)
        rot_done = event("rot_done", 2)
        rmin_done = event("rmin_done", 1)
        rexp_done = event("rexp_done", 1)
        phi_done = event("phi_done", 1)
        qi_done = event("qi_done", TG)
        ks_done = event("ks_done", TG)
        v1_done = event("v1_done", 1)
        vx_done = event("vx_done", BPT)
        tq = event("q_T_ps", 1)
        tfq = event("fq_T_ps", 1)
        tk = event("k_T_ps", 1)
        tfk = event("fk_T_ps", 1)
        tqi = event("qi_T_ps", 2)
        qx_done = event("qx_done", 1)
        fqx_done = event("fqx_done", 1)
        kT_done = event("kT_done", 1)
        fkT_done = event("fkT_done", 1)
        qiT_done = event("qiT_act", 1)
        qiT_done1 = event("qiT_dve", 1)
        sd_group = event("sd_head_groups", NHG * TG, "pe")
        s_copied = event("s_copied", TG, "act")
        s_masked = event("s_masked", TG, "pool")
        w_done = event("weights_done", TG, "dve")
        u_ps = event("u_ps", 2 * TG)
        st_done = event("state_done", 2 * NB, "dve")
        sbd_done = event("state_masked", TG)
        att_ps = event("attention_ps", TG, "pe")
        den_done = event("den_done", TG)
        rden_done = event("rden_done", TG)
        y_done = event("y_done", TG, "dve")
        yT_ps = event("yT_ps", 1)
        yT_done = event("yT_done", 1)
        o_ps = event("wo_ps", 1, "pe")
        z3_done = event("z3_done", TG)
        z3g_done = event("z3g_done", 1)
        x2_done = event("x2_done", 1, "dve")
        n2_done = event("n2_done", TG)
        n2T = event("n2T_ps", 1)
        h2T_done = event("h2T_done", 1)
        h2_ps = event("h2_rows_ps", 1)
        row_done = event("h2_rows", 2, "act")
        gh_done = event("gated_h2", 1)
        base_done = event("base_done", 1)
        lg_ps = event("logits_ps", 1)
        lg_done = event("logits_done", 1)
        mx_done = event("top_done", TG)
        ix_done = event("top_index", TG)
        choice_steps = event("choice_steps", 3)
        pre_done = event("prefix_done", TG + 1)
        rk_ps = event("rank_ps", 1)
        slot_steps = event("slot_steps", 6, "dve")
        idx_done = event("slot_index", 1)
        dl_done = event("logit_gap", 1)
        de_done = event("gap_exp", 1)
        wrow_done = event("row_weights", 2)
        prow_done = event("row_ids", 1)
        pid_next = event("ids_next", 1)
        scat = event("dispatched_rows", 16 * TG * TOPK)
        rows_left = event("rows_left", 1, "sp")

        w1_in = [event(f"w1_in{u}", 16) for u in range(2)]
        w2_in = [event(f"w2_in{u}", 16) for u in range(2)]
        xb_in = [event(f"xb_in{u}", 16) for u in range(2)]
        s_lastx, s_lastT, s_lastT_sb = sem("last_in"), sem("last_T"), sem("last_T_sb")
        bT_ps = [event(f"slots_T_ps{u}", 1) for u in range(2)]
        bT_done = [event(f"slots_T{u}", 3, "dve") for u in range(2)]
        meta_done = [event(f"slot_meta{u}", 1) for u in range(2)]
        up_ps = [event(f"up_ps{u}", 2 * FT, "pe") for u in range(2)]
        hid_done = [event(f"hidden{u}", 2 * FT, "act") for u in range(2)]
        dn_ps = [event(f"down_ps{u}", 2, "pe") for u in range(2)]
        oT_done = [event(f"down_T{u}", 3, "dve") for u in range(2)]
        r_ps = [event(f"rows_ps{u}", 1, "pe") for u in range(2)]
        r_done = [event(f"rows_done{u}", CT, "dve") for u in range(2)]
        osc = [event(f"rows_out{u}", 16 * CT) for u in range(2)]
        outs_left = [event(f"outs_left{u}", 1, "sp") for u in range(2)]
        s_lastO, s_lastR, s_lastS = sem("last_out_T"), sem("last_out_rows"), sem("last_rows_out")

        s_yb = [sem(f"pairs_in{g}") for g in range(GROUPS)]
        s_ys, s_yg, s_yo, s_out = sem("pairs_sum"), sem("pairs_gated"), sem("out_ready"), sem("out_written")

        def made(n, a):
            t, j = divmod(n - 1, BPT)
            return (2 * t + a) * BPT + j + 1

        def rope_table(name, g):
            v = K[name].rearrange("p (g t d) -> p g t d", g=GROUPS, t=TG)[:, bass.ds(g, 1), :, :]
            return v.rearrange("p g t d -> p (g t) d").unsqueeze(2).to_broadcast([P, TG, 2 * H, ROPE_HALF])

        block = ctx.enter_context(nc.Block())

        def apart(eng):
            eng.sem_inc(s_apart, 1)

        def start_ahead(eng, who):
            for e in ahead_of[who]:
                eng.sem_inc(e.sem, e.ahead)

        @block.sync
        def _(sp):
            sp.dma_start(X[:, 0].rearrange("p (t c) -> p t c", c=DM), x_v[0]).then_inc(s_x0, 16)
            sp.dma_start(const[:], const_d).then_inc(s_const, 16)
            sp.dma_start(vec_row[:], rows_d).then_inc(s_vec, 16)
            sp.dma_start(cT[:], ct_d).then_inc(s_c, 16)
            sp.dma_start(wall[:], wall_d).then_inc(s_wall, 16)
            sp.dma_start(wmod[:], wmod_d).then_inc(s_wmod, 16)
            sp.dma_start(wo[:], wo_d).then_inc(s_small, 16)
            sp.dma_start(rwt[:], rwt_d).then_inc(s_small, 16)
            sp.dma_start(bo_col[:], bo_d).then_inc(s_bo, 16)
            sp.dma_start(X[:, 1:].rearrange("p g (t c) -> p (g t) c", c=DM),
                         x_d.rearrange("b (t p) c -> p (b t) c", p=P)[:, TG:, :]).then_inc(s_x, 16)
            start_ahead(sp, "sp")
            for u in range(2):
                sp.dma_start(w1t[:, u, :], w1_v(u)).then_inc(w1_in[u].sem, 16)
                sp.dma_start(w2t[:, u], w2_v(u)).then_inc(w2_in[u].sem, 16)
            sp.wait_ge(s_fillms, 3)
            for n in range(12):
                sp.dma_start(disp_d[512 * n:512 * n + 512, :].rearrange("(p a) c -> p (a c)", a=4),
                              fill[:].rearrange("p a c -> p (a c)")).then_inc(s_filled, 16)
            for n in range(4):
                sp.dma_start(pair_d[1024 * n:1024 * n + 1024, :].rearrange("(p a) c -> p (a c)", a=8), zero[:]).then_inc(s_filled, 16)
            with sp.Fori(0, GROUPS - 1) as g:
                sp.wait_ge(scat.sem, scat.now(g))
                sp.sem_inc(rows_left.sem, 1)
            sp.wait_ge(scat.sem, scat.now(GROUPS - 1))
            sp.dma_start(lastx[:], disp_d[0:NE * CAP, :].rearrange("(e s) c -> e s c", s=CAP)[:, CM, :]).then_inc(s_lastx, 16)

            def slots(e):
                return disp_d[bass.ds(e * CAP, CM), :].rearrange("(p a) c -> p (a c)", a=CT)

            for u in range(2):
                sp.dma_start(xb[:, u, :, :].rearrange("p a c -> p (a c)"), slots(u)).then_inc(xb_in[u].sem, 16)
            def next_slots(u, i):
                sp.wait_ge(bT_ps[u].sem, bT_ps[u].now(i))
                sp.wait_ge(meta_done[u].sem, meta_done[u].now(i))
                sp.dma_start(xb[:, u, :, :].rearrange("p a c -> p (a c)"), slots(i * 2 + (u + 2))).then_inc(xb_in[u].sem, 16)

            def outs_gone(u, i):
                sp.wait_ge(osc[u].sem, osc[u].now(i))
                sp.sem_inc(outs_left[u].sem, 1)

            with sp.Fori(0, NE // 2 - 1) as i:
                next_slots(0, i)
                sp.wait_ge(up_ps[0].sem, up_ps[0].now(i))
                sp.dma_start(w1t[:, 0, :], w1_v(i * 2 + 2)).then_inc(w1_in[0].sem, 16)
                next_slots(1, i)
                sp.wait_ge(dn_ps[0].sem, dn_ps[0].now(i))
                sp.dma_start(w2t[:, 0], w2_v(i * 2 + 2)).then_inc(w2_in[0].sem, 16)
                sp.wait_ge(up_ps[1].sem, up_ps[1].now(i))
                sp.dma_start(w1t[:, 1, :], w1_v(i * 2 + 3)).then_inc(w1_in[1].sem, 16)
                outs_gone(0, i)
                sp.wait_ge(dn_ps[1].sem, dn_ps[1].now(i))
                sp.dma_start(w2t[:, 1], w2_v(i * 2 + 3)).then_inc(w2_in[1].sem, 16)
                outs_gone(1, i)
            next_slots(0, NE // 2 - 1)
            outs_gone(0, NE // 2 - 1)
            for u in range(2):
                sp.wait_ge(osc[u].sem, osc[u].now(NE // 2 - 1))
            sp.wait_ge(s_lastS, 16)
            for g in range(GROUPS):
                sp.dma_start(yb[:, g].rearrange("p t k c -> p t (k c)"), pair_v[g]).then_inc(s_yb[g], 16)
            for g in range(GROUPS):
                sp.wait_ge(s_yo, g + 1)
                sp.dma_start(out_v[g], yo[:, g]).then_inc(s_out, 16)
            sp.wait_ge(s_out, 16 * GROUPS)

        @block.gpsimd
        def _(pool):
            g_ = nc.gpsimd
            g_.memset(half_neg[:], -0.5).then_inc(s_ms, 1)
            g_.memset(ones_row[:], 1.0).then_inc(s_ms, 1)
            g_.memset(ones_b[:], 1.0).then_inc(s_ms, 1)
            start_ahead(pool, "pool")
            pool.wait_ge(s_ms, 3)

            def inv_std(g, n):
                pool.wait_ge(stats_b.sem, stats_b.now(g, (n + 1) * (2 * TG + 1)))
                g_.tensor_tensor(rstd[:, 0], ve[:, 0], half_neg[:, 0], ALU.pow).then_inc(rstd_done.sem, 1)

            def group_table(v, g):
                return v[:].rearrange("p b g c -> p (b g) c")[:, bass.ds(g, 1), :].to_broadcast([P, TG, DM])

            def rows_of(v, g):
                return v[:, bass.ds(g, 1), :].rearrange("p g (t c) -> p (g t) c", c=DM)

            def rope_products(g):
                pool.wait_ge(raw_done.sem, raw_done.now(g))
                uv = raw[:, :, 0:2 * DM].rearrange("p t (h r d) -> p t h r d", r=2, d=ROPE_HALF)
                g_.tensor_tensor(m3[:], uv[:, :, :, 0, :], rope_table("sin", g), ALU.mult).then_inc(rope_b.sem, 1)
                g_.tensor_tensor(m4[:], uv[:, :, :, 1, :], rope_table("cos", g), ALU.mult).then_inc(rope_b.sem, 1)

            def residual_bias(g):
                pool.wait_ge(n1_done.sem, n1_done.now(g))
                pool.wait_ge(s_tables, 3)
                x_ = rows_of(X, g)
                g_.tensor_tensor(x_, x_, group_table(attn_b, g), ALU.add).then_inc(xb_done.sem, 1)

            def query_factors(g):
                pool.wait_ge(ex_done.sem, ex_done.now(g))
                g_.tensor_tensor(fq[:], ex[:, 0:TG * HC].unsqueeze(2).to_broadcast([P, TG * HC, NSUB]),
                                 K["qmask"].unsqueeze(1).to_broadcast([P, TG * HC, NSUB]), ALU.mult).then_inc(fq_done.sem, 1)

            def keys_decayed(g):
                pool.wait_ge(phi_done.sem, phi_done.now(g))
                for t in range(TG):
                    f = ex[:, (2 * TG + t) * HC:(2 * TG + t + 1) * HC].rearrange("p (h c) -> p h c", c=C)
                    g_.tensor_tensor(ks[:, t], phi[:, t, H:2 * H, :].unsqueeze(2).to_broadcast([P, H, C, DH]),
                                     f.unsqueeze(3).to_broadcast([P, H, C, DH]), ALU.mult).then_inc(ks_done.sem, 1)

            def mask_scores(g, t):
                pool.wait_ge(s_copied.sem, s_copied.now(g, t + 1))
                if t >= 2:
                    pool.wait_ge(w_done.sem, w_done.now(g, t - 1))
                else:
                    pool.wait_ge(w_done.sem, w_done.before(g, TG - 1 + t))
                g_.tensor_tensor(s_mk[:, t % 2], s_sb[:, t % 2].rearrange("p a (h t) -> p (a h) t", t=BLK),
                                 K["causal"].unsqueeze(1).to_broadcast([P, H, BLK]), ALU.mult).then_inc(s_masked.sem, 1)

            def mask_states(g, t):
                pool.wait_ge(st_done.sem, st_done.now(g, made(BPT * t + BPT - 1, 1)))
                if t >= 2:
                    pool.wait_ge(att_ps.sem, att_ps.now(g, t - 1))
                else:
                    pool.wait_ge(att_ps.sem, att_ps.before(g, TG - 1 + t))
                g_.tensor_tensor(sbd[:, t % 2].rearrange("p j a w -> p (j a) w"),
                                 state[:, BPT * t:BPT * (t + 1)].rearrange("p j a w -> p (j a) w"),
                                 K["smask"].unsqueeze(1).to_broadcast([P, BPT * 2, SW]), ALU.mult).then_inc(sbd_done.sem, 1)

            def pool_body(g, more):
                n = g + 1
                mask_states(g, 1)
                mask_scores(g, 2)
                mask_states(g, 2)
                if more:
                    rope_products(n)
                mask_scores(g, 3)
                mask_states(g, 3)
                if more:
                    query_factors(n)
                    residual_bias(n)
                    pool.wait_ge(u_ps.sem, u_ps.now(g))
                    keys_decayed(n)
                inv_std(g, 0)
                inv_std(g, 1)
                if more:
                    mask_scores(n, 0)
                    mask_states(n, 0)
                pool.wait_ge(row_done.sem, row_done.now(g, 1))
                g_.tensor_tensor(gh[:], row[:, :, 0, 0:DM], group_table(gate_b, g), ALU.mult).then_inc(gh_done.sem, 1)
                if more:
                    mask_scores(n, 1)
                pool.wait_ge(s_filled, 16 * 16)
                pool.wait_ge(row_done.sem, row_done.now(g))
                pool.wait_ge(idx_done.sem, idx_done.now(g))
                pool.wait_ge(wrow_done.sem, wrow_done.now(g))
                pool.wait_ge(prow_done.sem, prow_done.now(g))
                apart(pool)
                for t in range(TG):
                    for k in range(TOPK):
                        pool.indirect_dma_start(disp_d, bass.IndirectOffsetOnAxis(ap=idx[:, t, k:k + 1], axis=0),
                                                row[:, t, k, :], None, bounds_check=ROWS - 1, oob_is_err=False).then_inc(scat.sem, 16)

            for n, at in enumerate((slice(1, 2), slice(2, GROUPS + 1))):
                pool.wait_ge(stats_a.sem, stats_a.now(0 if n == 0 else GROUPS - 1))
                g_.tensor_tensor(rstd[:, at], ve[:, at], half_neg[:, at], ALU.pow).then_inc(s_rstd, 1)
            pool.wait_ge(s_const, 16)
            rope_products(0)
            query_factors(0)
            keys_decayed(0)
            mask_scores(0, 0)
            mask_states(0, 0)
            mask_scores(0, 1)
            residual_bias(0)
            with pool.Fori(0, GROUPS - 1) as g:
                pool_body(g, True)
            pool_body(GROUPS - 1, False)
            with pool.Fori(0, NE // 2) as i:
                for u in range(2):
                    pool.wait_ge(r_done[u].sem, r_done[u].now(i))
                    apart(pool)
                    for a in range(CT):
                        pool.indirect_dma_start(pair_d, bass.IndirectOffsetOnAxis(ap=meta[:, u, a, 0:1].bitcast(U32), axis=0),
                                                orow[:, u, a, :], None, bounds_check=PAIRS - 1, oob_is_err=False).then_inc(osc[u].sem, 16)
            pool.wait_ge(s_lastR, 2)
            pool.indirect_dma_start(pair_d, bass.IndirectOffsetOnAxis(ap=lastx[:, DM:DM + 1].bitcast(U32), axis=0),
                                    lastR[:], None, bounds_check=PAIRS - 1, oob_is_err=False).then_inc(s_lastS, 16)

        @block.scalar
        def _(act):
            a_ = nc.scalar
            act.preload_act_table_set("natural_log_exp_and_others")
            start_ahead(act, "act")
            act.wait_ge(s_cs, 1)
            a_.activation(c_e[:], c_s[:], ACT.Exp, scale=-1.0).then_inc(s_ce, 1)

            def layer_input(g):
                act.wait_ge(n1T.sem, n1T.now(g))
                act.wait_ge(s_modc_sb, 3)
                a_.activation(hT[:], T4, ACT.Identity, bias=modc[:, 0, bass.ds(g, 1)], scale=modc[:, 1, bass.ds(g, 1)]).then_inc(hT_done.sem, 1)

            def projections(g):
                for t in range(TG):
                    act.wait_ge(proj.sem, proj.now(g, t + 1))
                    a_.copy(raw[:, t, :], ps[:, 5 - t % 2, 0:WALL]).then_inc(raw_done.sem, 1)

            def softplus(g):
                act.wait_ge(zclamp.sem, zclamp.now(g))
                a_.activation(ze[:], zl[:], ACT.Exp, scale=-1.0).then_inc(zexp.sem, 1)
                act.wait_ge(zexp.sem, zexp.now(g))
                a_.activation(zn[:], ze[:], ACT.Ln, bias=1.0).then_inc(zln.sem, 1)

            def factors(g):
                act.wait_ge(expo_ps.sem, expo_ps.now(g))
                for i in range(NSUB):
                    f = a_.activation(fk[:].rearrange("p t h i -> p (t h) i")[:, :, i], T5[:, i * TG * HC:(i + 1) * TG * HC],
                                      ACT.Exp, bias=K["kbias"][:, i:i + 1])
                f.then_inc(fk_done.sem, 1)
                a_.activation(ex[:], T4[:, 0:3 * TG * HC + TG * 2 * BPT], ACT.Exp, scale=-1.0).then_inc(ex_done.sem, 1)

            def feature_exp(g):
                act.wait_ge(rmin_done.sem, rmin_done.now(g))
                a_.activation(rexp[:], rmin[:], ACT.Exp).then_inc(rexp_done.sem, 1)

            def query_factors_T(g):
                act.wait_ge(tfq.sem, tfq.now(g))
                for j in range(HG):
                    f = a_.mul(fqx[:, :, :, j, :].rearrange("p t b s -> p (t b) s"),
                               T5.rearrange("p (n s) -> p n s", s=BLK), K["hmask"][:, j:j + 1])
                f.then_inc(fqx_done.sem, 1)

            def keys_T(g):
                act.wait_ge(tk.sem, tk.now(g))
                a_.copy(kT[:], T4).then_inc(kT_done.sem, 1)

            def values(g):
                act.wait_ge(s_dms, 1)
                act.wait_ge(raw_done.sem, raw_done.now(g))
                a_.copy(v1[:, :, :, 0:DH], raw[:, :, 2 * DM:3 * DM].rearrange("p t (h d) -> p t h d", d=DH)).then_inc(v1_done.sem, 1)
                act.wait_ge(v1_done.sem, v1_done.now(g))
                for j in range(BPT):
                    a_.mul(vx[:, :, j, :], v1[:].rearrange("p t h e -> p t (h e)"), K["blk"][:, j:j + 1]).then_inc(vx_done.sem, 1)

            def queries_T(g):
                act.wait_ge(tqi.sem, tqi.now(g, 1))
                a_.copy(qiT[:, 0, :], T4).then_inc(qiT_done.sem, 1)

            def copy_scores(g, t):
                act.wait_ge(sd_group.sem, sd_group.now(g, NHG * (t + 1)))
                if t >= 2:
                    act.wait_ge(s_masked.sem, s_masked.now(g, t - 1))
                else:
                    act.wait_ge(s_masked.sem, s_masked.before(g, TG - 1 + t))
                a_.copy(s_sb[:, t % 2], S_ps).then_inc(s_copied.sem, 1)

            def act_body(g, more):
                n = g + 1
                act.wait_ge(o_ps.sem, o_ps.before(g))
                act.wait_ge(hT_done.sem, hT_done.now(g))
                a_.activation(h_keep[:], hT[:], ACT.Identity, bias=bo_col[:], scale=1.0).then_inc(keep_done.sem, 1)
                if more:
                    act.wait_ge(keep_done.sem, keep_done.now(g))
                    layer_input(n)
                copy_scores(g, 2)
                if more:
                    projections(n)
                    softplus(n)
                copy_scores(g, 3)
                if more:
                    factors(n)
                    feature_exp(n)
                    query_factors_T(n)
                    keys_T(n)
                    act.wait_ge(att_ps.sem, att_ps.now(g))
                    values(n)
                act.wait_ge(yT_ps.sem, yT_ps.now(g))
                a_.copy(yT[:], T6).then_inc(yT_done.sem, 1)
                if more:
                    queries_T(n)
                    copy_scores(n, 0)
                act.wait_ge(n2T.sem, n2T.now(g))
                a_.activation(h2T[:], T4, ACT.Identity, bias=modc[:, 2, bass.ds(g, 1)], scale=modc[:, 3, bass.ds(g, 1)]).then_inc(h2T_done.sem, 1)
                act.wait_ge(h2_ps.sem, h2_ps.now(g))
                act.wait_ge(rows_left.sem, rows_left.before(g))
                for k in range(TOPK):
                    a_.copy(row[:, :, k, 0:DM], T5.rearrange("p (t c) -> p t c", c=DM)).then_inc(row_done.sem, 1)
                act.wait_ge(dl_done.sem, dl_done.now(g))
                a_.activation(de[:], dl[:], ACT.Exp).then_inc(de_done.sem, 1)
                if more:
                    copy_scores(n, 1)
            act.wait_ge(s_bo, 16)
            layer_input(0)
            projections(0)
            softplus(0)
            act.wait_ge(s_const, 16)
            factors(0)
            feature_exp(0)
            query_factors_T(0)
            keys_T(0)
            values(0)
            queries_T(0)
            copy_scores(0, 0)
            copy_scores(0, 1)
            with act.Fori(0, GROUPS - 1) as g:
                act_body(g, True)
            act_body(GROUPS - 1, False)
            act.preload_act_table(ACT.Silu)
            with act.Fori(0, NE // 2) as i:
                for u in range(2):
                    for f in range(FT):
                        for n, (c0, cn) in enumerate(NHALF):
                            k = 2 * f + n
                            act.wait_ge(up_ps[u].sem, up_ps[u].now(i, k + 1))
                            if k == 0:
                                act.wait_ge(dn_ps[u].sem, dn_ps[u].before(i))
                            a_.activation(hid[:, u, f, c0:c0 + cn], ps[:, k % 4, 0:cn], ACT.Silu).then_inc(hid_done[u].sem, 1)

        @block.vector
        def _(dve):
            v_ = nc.vector
            v_.memset(fill[:], 0.0).then_inc(s_fillms, 1)
            v_.memset(zero[:], 0.0).then_inc(s_fillms, 1)
            dve.wait_ge(s_fillms, 2)
            v_.memset(fill[:, :, DM:DM + 1], 1e9).then_inc(s_fillms, 1)
            v_.memset(v1[:, :, :, DH:E1], 1.0).then_inc(s_dms, 1)
            v_.memset(pre[:], 0.0).then_inc(s_dms, 1)
            start_ahead(dve, "dve")
            dve.wait_ge(s_dms, 2)
            v_.memset(state[:, 0], 0.0).then_inc(s_state0, 1)

            def layernorm(src, at, done, first):
                for t in range(TG):
                    v_.bn_stats(st6[:, at, t, :], src[:, t, :]).then_inc(done, 1)
                for t in range(TG):
                    dve.wait_ge(done, first + (t + 1))
                    apart(dve)
                    v_.bn_aggr(mv[:, at, t, :], st6[:, at, t, :]).then_inc(done, 1)
                dve.wait_ge(done, first + 2 * TG)
                v_.tensor_scalar(ve[:, at], mv[:, at, :, 1], LN_EPS, None, ALU.add).then_inc(done, 1)

            def rows_of(v, g):
                return v[:, bass.ds(g, 1), :].rearrange("p g (t c) -> p (g t) c", c=DM)

            def statistics(g):
                dve.wait_ge(s_x if g else s_x0, 16)
                layernorm(rows_of(X, g), g + 1, stats_a.sem, g * (2 * TG + 1))

            def normalised(g):
                dve.wait_ge(s_rstd, 1 if isinstance(g, int) else 2)
                at = bass.ds(g + 1, 1)
                for t in range(TG):
                    v_.tensor_scalar(n1[:, t, :], rows_of(X, g)[:, t, :], mv[:, at, t, 0:1].rearrange("p a o -> p (a o)"),
                                     rstd[:, at, t], ALU.subtract, ALU.mult).then_inc(n1_done.sem, 1)

            def decay_logits(g):
                dve.wait_ge(raw_done.sem, raw_done.now(g))
                v_.tensor_tensor(zn[:], raw[:, :, 3 * DM:WALL], vecs[:, 3 * DM:ROWV].unsqueeze(1).to_broadcast([P, TG, HC]), ALU.add).then_inc(zadd.sem, 1)
                dve.wait_ge(zadd.sem, zadd.now(g))
                v_.tensor_scalar(zl[:], zn[:], -30.0, None, ALU.max).then_inc(zclamp.sem, 1)

            def rope_products(g):
                uv = raw[:, :, 0:2 * DM].rearrange("p t (h r d) -> p t h r d", r=2, d=ROPE_HALF)
                v_.tensor_tensor(m1[:], uv[:, :, :, 0, :], rope_table("cos", g), ALU.mult).then_inc(rope_a.sem, 1)
                v_.tensor_tensor(m2[:], uv[:, :, :, 1, :], rope_table("sin", g), ALU.mult).then_inc(rope_a.sem, 1)

            def rates(g):
                dve.wait_ge(zln.sem, zln.now(g))
                v_.tensor_scalar(rate[:], zn[:], float(-np.log(0.999)), float(-np.log(0.001)), ALU.max, ALU.min).then_inc(rate_done.sem, 1)
                dve.wait_ge(rate_done.sem, rate_done.now(g))

            def block_rates(g):
                dve.wait_ge(sum_ps.sem, sum_ps.now(g))
                v_.tensor_tensor(sums[:], T4[:, 448:448 + BPT].unsqueeze(1).to_broadcast([P, TG * 2, BPT]),
                                 K["tile_half"].rearrange("p (a b) -> p a b", b=BPT), ALU.mult).then_inc(sums_done.sem, 1)

            def rotated(g):
                rv = rot[:].rearrange("p t h (r d) -> p t h r d", d=ROPE_HALF)
                dve.wait_ge(rope_a.sem, rope_a.now(g))
                v_.tensor_tensor(rv[:, :, :, 0, :], m1[:], m2[:], ALU.subtract).then_inc(rot_done.sem, 1)
                dve.wait_ge(rope_b.sem, rope_b.now(g))
                v_.tensor_tensor(rv[:, :, :, 1, :], m3[:], m4[:], ALU.add).then_inc(rot_done.sem, 1)
                dve.wait_ge(rot_done.sem, rot_done.now(g))
                v_.tensor_scalar(rmin[:], rot[:], 0.0, None, ALU.min).then_inc(rmin_done.sem, 1)

            def features(g):
                dve.wait_ge(rexp_done.sem, rexp_done.now(g))
                v_.scalar_tensor_tensor(phi[:].rearrange("p t h d -> p (t h d)"), rot[:].rearrange("p t h d -> p (t h d)"), 1.0,
                                        rexp[:].rearrange("p t h d -> p (t h d)"), ALU.add, ALU.max).then_inc(phi_done.sem, 1)
                dve.wait_ge(phi_done.sem, phi_done.now(g))
                dve.wait_ge(ex_done.sem, ex_done.now(g))
                for t in range(TG):
                    f = ex[:, (TG + t) * HC:(TG + t + 1) * HC].rearrange("p (h c) -> p h c", c=C)
                    v_.tensor_tensor(qi[:, t], phi[:, t, 0:H, :].unsqueeze(2).to_broadcast([P, H, C, DH]),
                                     f.unsqueeze(3).to_broadcast([P, H, C, DH]), ALU.mult).then_inc(qi_done.sem, 1)

            def queries_T(g):
                dve.wait_ge(tq.sem, tq.now(g))
                for j in range(HG):
                    f = v_.tensor_scalar(qx[:, :, :, j, :].rearrange("p t b s -> p (t b) s"),
                                         T4.rearrange("p (n s) -> p n s", s=BLK), K["hmask"][:, j:j + 1], None, ALU.mult)
                f.then_inc(qx_done.sem, 1)

            def factors_T(g):
                dve.wait_ge(tfk.sem, tfk.now(g))
                v_.tensor_copy(fkT[:], T5).then_inc(fkT_done.sem, 1)

            def kept_decays(g):
                dve.wait_ge(ex_done.sem, ex_done.now(g))
                v_.tensor_copy(dec[:], ex[:, 3 * TG * HC:3 * TG * HC + TG * 2 * BPT]).then_inc(dec_done.sem, 1)

            def decayed_queries_T(g):
                dve.wait_ge(tqi.sem, tqi.now(g))
                v_.tensor_copy(qiT[:, 1, :], T5).then_inc(qiT_done1.sem, 1)

            def states(g, t, halves=(0, 1), first=False):
                for a in halves:
                    dve.wait_ge(u_ps.sem, u_ps.now(g, 2 * t + a + 1))
                    for j in range(BPT):
                        n = BPT * t + j
                        if n:
                            dve.wait_ge(st_done.sem, st_done.now(g, made(n, a)))
                        elif first:
                            dve.wait_ge(s_state0, 1)
                            dve.wait_ge(dec_done.sem, dec_done.now(g))
                        else:
                            dve.wait_ge(carry_done.sem, carry_done.now(g - 1))
                            dve.wait_ge(dec_done.sem, dec_done.now(g))
                        if n == NB - 1 and a == 0:
                            dve.wait_ge(sbd_done.sem, sbd_done.now(g, 1))
                        at = (2 * t + a) * BPT + j
                        v_.scalar_tensor_tensor(state[:, (n + 1) % NB, a, :], state[:, n, a, :], dec[:, at:at + 1],
                                                U_ps[:, j * SW:(j + 1) * SW], ALU.mult, ALU.add).then_inc(st_done.sem, 1)

            def gated(g, t):
                dve.wait_ge(sd_group.sem, sd_group.now(g, NHG * (t + 1)))
                dve.wait_ge(s_masked.sem, s_masked.now(g, t + 1))
                if t >= 2:
                    dve.wait_ge(att_ps.sem, att_ps.now(g, t - 1))
                else:
                    dve.wait_ge(att_ps.sem, att_ps.before(g, TG - 1 + t))
                v_.tensor_tensor(wts[:, t % 2].rearrange("p (a h) t -> p a (h t)", a=2), s_mk[:, t % 2].rearrange("p (a h) t -> p a (h t)", a=2),
                                 D_ps, ALU.mult).then_inc(w_done.sem, 1)

            def normed(g, t):
                dve.wait_ge(att_ps.sem, att_ps.now(g, t + 1))
                ov_ = O_ps.rearrange("p (h e) -> p h e", e=E1)
                v_.tensor_scalar(den[:, t, :], ov_[:, :, DH], DEN_EPS, None, ALU.add).then_inc(den_done.sem, 1)
                dve.wait_ge(den_done.sem, den_done.now(g, t + 1))
                v_.reciprocal(rden[:, t, :], den[:, t, :]).then_inc(rden_done.sem, 1)
                dve.wait_ge(rden_done.sem, rden_done.now(g, t + 1))
                v_.tensor_tensor(y[:, t], ov_[:, :, 0:DH], rden[:, t, :].unsqueeze(2).to_broadcast([P, H, DH]), ALU.mult).then_inc(y_done.sem, 1)

            def residual(g):
                for t in range(TG):
                    v_.tensor_scalar(z3[:, t, :], T7[:, t * P:(t + 1) * P], mv[:, 0, t, 0:1], rstd[:, 0, t:t + 1], ALU.subtract, ALU.mult).then_inc(z3_done.sem, 1)
                dve.wait_ge(z3_done.sem, z3_done.now(g))
                ag = attn_g[:].rearrange("p b g c -> p (b g) c")[:, bass.ds(g, 1), :].to_broadcast([P, TG, DM])
                v_.tensor_tensor(z3g[:], z3[:], ag, ALU.mult).then_inc(z3g_done.sem, 1)
                dve.wait_ge(z3g_done.sem, z3g_done.now(g))
                dve.wait_ge(xb_done.sem, xb_done.now(g))
                v_.tensor_tensor(x2[:], z3g[:], rows_of(X, g), ALU.add).then_inc(x2_done.sem, 1)

            def choice(g):
                dve.wait_ge(lg_ps.sem, lg_ps.now(g))
                v_.tensor_copy(lg[:], T4[:, 0:TG * NE].rearrange("p (t e) -> p t e", e=NE)).then_inc(lg_done.sem, 1)
                dve.wait_ge(lg_done.sem, lg_done.now(g))
                apart(dve)
                for t in range(TG):
                    v_.max(mx[:, t, :], lg[:, t, :]).then_inc(mx_done.sem, 1)
                for t in range(TG):
                    dve.wait_ge(mx_done.sem, mx_done.now(g, t + 1))
                    apart(dve)
                    v_.max_index(ix[:, t, :], mx[:, t, :], lg[:, t, :]).then_inc(ix_done.sem, 1)
                v_.tensor_tensor(dl[:], mx[:, :, 1], mx[:, :, 0], ALU.subtract).then_inc(dl_done.sem, 1)
                dve.wait_ge(ix_done.sem, ix_done.now(g))
                v_.tensor_copy(ef[:], ix[:, :, 0:TOPK]).then_inc(choice_steps.sem, 1)
                v_.tensor_copy(pre[:, 0, :], pre[:, TG, :]).then_inc(pre_done.sem, 1)
                dve.wait_ge(choice_steps.sem, choice_steps.now(g, 1))
                v_.tensor_tensor(oh[:], K["iota"].unsqueeze(1).unsqueeze(1).to_broadcast([P, TG, TOPK, NE]),
                                 ef[:].unsqueeze(3).to_broadcast([P, TG, TOPK, NE]), ALU.is_equal).then_inc(choice_steps.sem, 1)
                dve.wait_ge(choice_steps.sem, choice_steps.now(g, 2))
                v_.tensor_tensor(msk[:], oh[:, :, 0, :], oh[:, :, 1, :], ALU.add).then_inc(choice_steps.sem, 1)
                dve.wait_ge(choice_steps.sem, choice_steps.now(g, 3))
                for t in range(TG):
                    dve.wait_ge(pre_done.sem, pre_done.now(g, t + 1))
                    v_.tensor_tensor(pre[:, t + 1, :], pre[:, t, :], msk[:, t, :], ALU.add).then_inc(pre_done.sem, 1)

            def slot(g):
                dve.wait_ge(rk_ps.sem, rk_ps.now(g))
                rkv = T4[:, 64:64 + TG * NE].rearrange("p (t e) -> p t e", e=NE)
                for k in range(TOPK):
                    f = v_.tensor_tensor(rm[:, :, k, :], oh[:, :, k, :], rkv, ALU.mult)
                f.then_inc(slot_steps.sem, 1)
                dve.wait_ge(slot_steps.sem, slot_steps.now(g, 1))
                v_.tensor_reduce(rk[:], rm[:], AX.X, ALU.add).then_inc(slot_steps.sem, 1)
                dve.wait_ge(slot_steps.sem, slot_steps.now(g, 2))
                v_.tensor_scalar(ov[:], rk[:], float(CAP), 1e6, ALU.is_ge, ALU.mult).then_inc(slot_steps.sem, 1)
                v_.scalar_tensor_tensor(sl[:], ef[:], float(CAP), rk[:], ALU.mult, ALU.add).then_inc(slot_steps.sem, 1)
                dve.wait_ge(slot_steps.sem, slot_steps.now(g, 4))
                dve.wait_ge(rows_left.sem, rows_left.before(g))
                v_.tensor_tensor(idx[:], sl[:], ov[:], ALU.add).then_inc(idx_done.sem, 1)

            def weights(g):
                dve.wait_ge(de_done.sem, de_done.now(g))
                v_.tensor_scalar(dp[:], de[:], 1.0, None, ALU.add).then_inc(slot_steps.sem, 1)
                dve.wait_ge(slot_steps.sem, slot_steps.now(g, 5))
                v_.reciprocal(w0[:], dp[:]).then_inc(slot_steps.sem, 1)
                dve.wait_ge(slot_steps.sem, slot_steps.now(g, 6))
                v_.tensor_copy(row[:, :, 0, DM + 1], w0[:]).then_inc(wrow_done.sem, 1)
                v_.tensor_tensor(row[:, :, 1, DM + 1], w0[:], de[:], ALU.mult).then_inc(wrow_done.sem, 1)
                v_.tensor_copy(row[:, :, :, DM:DM + 1].bitcast(U32).rearrange("p t k o -> p t (k o)"), pid[:]).then_inc(prow_done.sem, 1)
                dve.wait_ge(prow_done.sem, prow_done.now(g))
                v_.tensor_scalar(pid[:], pid[:], float(GT * TOPK), None, ALU.add).then_inc(pid_next.sem, 1)
                dve.wait_ge(pid_next.sem, pid_next.now(g))

            def dve_body(g, more):
                n = g + 1
                if more:
                    normalised(n)
                gated(g, 1)
                normed(g, 0)
                states(g, 2)
                gated(g, 2)
                if more:
                    decay_logits(n)
                    rope_products(n)
                normed(g, 1)
                states(g, 3)
                if more:
                    rates(n)
                    block_rates(n)
                    rotated(n)
                gated(g, 3)
                if more:
                    dve.wait_ge(st_done.sem, st_done.now(g))
                    v_.tensor_scalar(state[:, 0], state[:, 0], K["keep"][:, bass.ds(n, 1)], None, ALU.mult).then_inc(carry_done.sem, 1)
                    features(n)
                    kept_decays(n)
                normed(g, 2)
                if more:
                    queries_T(n)
                    factors_T(n)
                normed(g, 3)
                if more:
                    decayed_queries_T(n)
                dve.wait_ge(o_ps.sem, o_ps.now(g))
                layernorm(T7.rearrange("p (t c) -> p t c", c=DM), 0, stats_b.sem, stats_b.now(g, 0))
                dve.wait_ge(rstd_done.sem, rstd_done.now(g, 1))
                residual(g)
                dve.wait_ge(x2_done.sem, x2_done.now(g))
                layernorm(x2, 0, stats_b.sem, stats_b.now(g, 2 * TG + 1))
                dve.wait_ge(rstd_done.sem, rstd_done.now(g, 2))
                for t in range(TG):
                    v_.tensor_scalar(n2[:, t, :], x2[:, t, :], mv[:, 0, t, 0:1], rstd[:, 0, t:t + 1], ALU.subtract, ALU.mult).then_inc(n2_done.sem, 1)
                if more:
                    states(n, 0, (0,))
                    gated(n, 0)
                    states(n, 0, (1,))
                choice(g)
                if more:
                    states(n, 1)
                slot(g)
                weights(g)
                dve.wait_ge(gh_done.sem, gh_done.now(g))
                v_.tensor_tensor(X[:, bass.ds(g, 1), :], x2[:].rearrange("p t c -> p (t c)").unsqueeze(1),
                                 gh[:].rearrange("p t c -> p (t c)").unsqueeze(1), ALU.add).then_inc(base_done.sem, 1)

            statistics(0)
            normalised(0)
            dve.wait_ge(s_c, 16)
            v_.tensor_scalar(c_s[:], cT[:], -80.0, None, ALU.max).then_inc(s_cs, 1)
            dve.wait_ge(s_ce, 1)
            v_.tensor_scalar(c_s[:], c_e[:], 1.0, None, ALU.add).then_inc(s_cs, 1)
            dve.wait_ge(s_cs, 2)
            v_.reciprocal(c_e[:], c_s[:]).then_inc(s_cs, 1)
            dve.wait_ge(s_cs, 3)
            v_.tensor_tensor(c_silu[:], cT[:], c_e[:], ALU.mult).then_inc(s_csilu, 1)
            dve.wait_ge(s_csilu, 1)
            v_.tensor_copy(c_rep[:], c_silu[:].unsqueeze(2).to_broadcast([P, B, P])).then_inc(s_crep, 1)
            dve.wait_ge(s_vecp, 1)
            v_.tensor_copy(vecs[:], ps[:, 1, 0:ROWV]).then_inc(s_vecs, 1)
            dve.wait_ge(s_modc, 1)
            mc = ps[:, 0, 0:4 * B].rearrange("p (j b) -> p j b", b=B)
            for b in range(B):
                v_.tensor_copy(modc[:, :, b * GPB:(b + 1) * GPB], mc[:, :, b:b + 1].to_broadcast([P, 4, GPB])).then_inc(s_modc_sb, 1)
            dve.wait_ge(s_modc_sb, 2)
            v_.tensor_scalar(modc[:, 1:4:2, :], modc[:, 1:4:2, :], 1.0, None, ALU.add).then_inc(s_modc_sb, 1)
            for g in range(1, GROUPS):
                statistics(g)
            decay_logits(0)
            dve.wait_ge(s_const, 16)
            v_.tensor_copy(tri_b[:], K["tri"]).then_inc(s_trib, 1)
            v_.tensor_copy(pid[:], K["pid"].rearrange("p (t k) -> p t k", k=TOPK)).then_inc(s_trib, 1)
            dve.wait_ge(s_trib, 2)
            rope_products(0)
            rates(0)
            block_rates(0)
            rotated(0)
            dve.wait_ge(s_modb, 1)
            for b in range(B):
                v_.tensor_copy(mod_b[:, b], ps[:, 2 + 4 * b:4 + 4 * b, :].rearrange("p w n -> p (w n)")[:, 0:6 * DM]).then_inc(s_gate, 1)
            features(0)
            kept_decays(0)
            queries_T(0)
            factors_T(0)
            decayed_queries_T(0)
            states(0, 0, first=True)
            gated(0, 0)
            states(0, 1)
            dve.wait_ge(s_gate, 2)
            gv = mod_b[:].rearrange("p b (j c) -> p b j c", c=DM)[:, :, 2:6:3, :]
            v_.tensor_scalar(gsign[:], gv, 0.0, 2.0, ALU.is_ge, ALU.mult).then_inc(s_gate, 1)
            v_.tensor_scalar(gates[:], gv, -1.0, 0.25, ALU.mult, ALU.max).then_inc(s_gate, 1)
            dve.wait_ge(s_gate, 4)
            v_.tensor_tensor(gabs[:], gates[:], gv, ALU.max).then_inc(s_gate, 1)
            dve.wait_ge(s_gate, 5)
            for n in range(2):
                v_.scalar_tensor_tensor(gates[:, :, n, :], gsign[:, :, n, :], -1.0, gabs[:, :, n, :], ALU.add, ALU.mult).then_inc(s_gate, 1)
            dve.wait_ge(s_gate, 7)
            dve.wait_ge(s_vecs, 1)

            def per_group(v):
                return v.unsqueeze(2).to_broadcast([P, B, GPB, DM])

            for out_, j in ((attn_g, 1), (attn_b, 2)):
                v_.tensor_tensor(out_[:], per_group(gates[:, :, 0, :]),
                                 vecs[:, j * DM:(j + 1) * DM].unsqueeze(1).unsqueeze(1).to_broadcast([P, B, GPB, DM]), ALU.mult).then_inc(s_tables, 1)
            v_.tensor_copy(gate_b[:], per_group(gates[:, :, 1, :])).then_inc(s_tables, 1)
            with dve.Fori(0, GROUPS - 1) as g:
                dve_body(g, True)
            dve_body(GROUPS - 1, False)

            dve.wait_ge(s_lastT, 1)
            v_.tensor_copy(lastT[:, 0:NE], T4[:, 0:NE]).then_inc(s_lastT_sb, 1)
            v_.memset(lastT[:, NE:NE + 1], 0.0).then_inc(s_lastT_sb, 1)
            dve.wait_ge(s_lastT_sb, 2)

            def slots_T(u, i, e):
                dve.wait_ge(bT_ps[u].sem, bT_ps[u].now(i))
                dve.wait_ge(up_ps[u].sem, up_ps[u].before(i))
                v_.tensor_copy(bT[:, u, 0:512], ps[:, 0, :]).then_inc(bT_done[u].sem, 1)
                v_.tensor_copy(bT[:, u, 512:CM], ps[:, 1, 0:P]).then_inc(bT_done[u].sem, 1)
                v_.tensor_copy(bT[:, u, CM:CAP], lastT[:, bass.ds(e, 1)] if not isinstance(e, int) else lastT[:, e:e + 1]).then_inc(bT_done[u].sem, 1)

            def slot_meta(u, i):
                dve.wait_ge(xb_in[u].sem, xb_in[u].now(i))
                dve.wait_ge(outs_left[u].sem, outs_left[u].before(i))
                v_.tensor_copy(meta[:, u], xb[:, u, :, DM:RW]).then_inc(meta_done[u].sem, 1)

            def down_T(u, i, only=None):
                for n, (c0, cn) in enumerate(NHALF):
                    if only in (None, n):
                        dve.wait_ge(dn_ps[u].sem, dn_ps[u].now(i, n + 1))
                        if n == 0:
                            dve.wait_ge(r_ps[u].sem, r_ps[u].before(i))
                        v_.tensor_copy(oT[:, u, c0:c0 + cn], ps[:, 4 + n, 0:cn]).then_inc(oT_done[u].sem, 1)
                if only != 0:
                    dve.wait_ge(oT_done[u].sem, oT_done[u].now(i, 2))
                    v_.tensor_copy(lastO[:, bass.ds(i * 2 + u, 1)], oT[:, u, CM:CAP]).then_inc(oT_done[u].sem, 1)

            def rows(u, i):
                dve.wait_ge(r_ps[u].sem, r_ps[u].now(i))
                dve.wait_ge(outs_left[u].sem, outs_left[u].before(i))
                for a in range(CT):
                    v_.tensor_scalar(orow[:, u, a, :], ps[:, 6 + a // 4, (a % 4) * P:(a % 4 + 1) * P], meta[:, u, a, 1:2], None, ALU.mult).then_inc(r_done[u].sem, 1)

            slots_T(0, 0, 0)
            slot_meta(0, 0)
            with dve.Fori(0, NE // 2) as i:
                slots_T(1, i, i * 2 + 1)
                down_T(0, i)
                slot_meta(1, i)
                rows(0, i)
                down_T(1, i, 0)
                slots_T(0, i + 1, i * 2 + 2)
                down_T(1, i, 1)
                rows(1, i)
                slot_meta(0, i + 1)
            dve.wait_ge(s_lastO, 1)
            v_.tensor_scalar(lastR[:], T4[0:NE, 0:P], lastx[:, DM + 1:RW], None, ALU.mult).then_inc(s_lastR, 2)
            for g in range(GROUPS):
                dve.wait_ge(s_yb[g], 16)
                v_.tensor_tensor(ys[:, g], yb[:, g, :, 0, :], yb[:, g, :, 1, :], ALU.add).then_inc(s_ys, 1)
                dve.wait_ge(s_ys, g + 1)
                gb = gate_b[:].rearrange("p b g c -> p (b g) c")[:, g:g + 1, :].to_broadcast([P, TG, DM])
                v_.tensor_tensor(ys[:, g], ys[:, g], gb, ALU.mult).then_inc(s_yg, 1)
                dve.wait_ge(s_yg, g + 1)
                v_.tensor_tensor(yo[:, g].rearrange("p t c -> p (t c)"), ys[:, g].rearrange("p t c -> p (t c)"), X[:, g], ALU.add).then_inc(s_yo, 1)

        @block.tensor
        def _(pe):
            mm = nc.tensor.matmul
            start_ahead(pe, "pe")
            pe.wait_ge(s_vec, 16)
            pe.wait_ge(s_ms, 3)
            mm(ps[:, 1, 0:ROWV], ones_row[:], vec_row[:], start=True, stop=True).then_inc(s_vecp, 1)
            pe.wait_ge(s_wmod, 16)
            pe.wait_ge(s_csilu, 1)
            for n, j in enumerate((0, 1, 3, 4)):
                f = mm(ps[:, 0, n * B:(n + 1) * B], wmod[:, j * DM:(j + 1) * DM], c_silu[:], start=True, stop=True)
            f.then_inc(s_modc, 1)
            pe.wait_ge(s_const, 16)
            pe.wait_ge(s_wall, 16)

            def tr(out, in_, **kw):
                return nc.tensor.transpose(out, in_, ident[0:in_.shape[0], 0:in_.shape[0]])

            def norm_T(g):
                pe.wait_ge(n1_done.sem, n1_done.now(g))
                for t in range(TG):
                    f = tr(T4[:, t * P:(t + 1) * P], n1[:, t, :])
                f.then_inc(n1T.sem, 1)

            def project(g):
                pe.wait_ge(hT_done.sem, hT_done.now(g))
                for t in range(TG):
                    if t >= 2:
                        pe.wait_ge(raw_done.sem, raw_done.now(g, t - 1))
                    mm(ps[:, 5 - t % 2, 0:WALL], hT[:, t * P:(t + 1) * P], wall[:], start=True, stop=True).then_inc(proj.sem, 1)

            def exponents(g):
                pe.wait_ge(raw_done.sem, raw_done.now(g))
                pe.wait_ge(rate_done.sem, rate_done.now(g))
                rv = rate[:].rearrange("p t h -> p (t h)")
                mm(T4[:, 448:448 + BPT], rv, K["blk"], start=True, stop=True).then_inc(sum_ps.sem, 1)
                for i in range(NSUB):
                    f = mm(T5[:, i * TG * HC:(i + 1) * TG * HC], K["gk"][:, i * P:(i + 1) * P], rv, start=True, stop=True)
                f.then_inc(expo_ps.sem, 1)
                pe.wait_ge(sums_done.sem, sums_done.now(g))
                for i, n in enumerate(("own", "cq", "ck")):
                    mm(T4[:, i * TG * HC:(i + 1) * TG * HC], K[n], rv, start=True, stop=True)
                mm(T4[:, 3 * TG * HC:3 * TG * HC + TG * 2 * BPT], K["spread"], sums[:].rearrange("p a b -> p (a b)"),
                   start=True, stop=True).then_inc(expo_ps.sem, 1)

            def query_T(g):
                pe.wait_ge(phi_done.sem, phi_done.now(g))
                pe.wait_ge(ex_done.sem, ex_done.now(g))
                for t in range(TG):
                    f = tr(T4[:, t * P:(t + 1) * P], phi[:, t, 0:H, :].rearrange("p h d -> p (h d)"))
                f.then_inc(tq.sem, 1)
                pe.wait_ge(fq_done.sem, fq_done.now(g))
                fqv = fq[:].rearrange("p (t h) i -> p t (h i)", t=TG)
                for t in range(TG):
                    f = tr(T5[:, t * P:(t + 1) * P], fqv[:, t, :])
                f.then_inc(tfq.sem, 1)

            def key_T(g):
                pe.wait_ge(qx_done.sem, qx_done.now(g))
                for t in range(TG):
                    f = tr(T4[:, t * P:(t + 1) * P], phi[:, t, H:2 * H, :].rearrange("p h d -> p (h d)"))
                f.then_inc(tk.sem, 1)
                pe.wait_ge(fqx_done.sem, fqx_done.now(g))
                for t in range(TG):
                    f = tr(T5[:, t * P:(t + 1) * P], fk[:, t].rearrange("p h i -> p (h i)"))
                f.then_inc(tfk.sem, 1)

            def decayed_query_T(g):
                pe.wait_ge(qi_done.sem, qi_done.now(g))
                pe.wait_ge(kT_done.sem, kT_done.now(g))
                pe.wait_ge(fkT_done.sem, fkT_done.now(g))
                for a in range(2):
                    for t in range(TG):
                        f = tr(ps[:, 4 + a, t * P:(t + 1) * P], qi[:, t, a * HALF:(a + 1) * HALF].rearrange("p h c d -> p (h c d)"))
                    f.then_inc(tqi.sem, 1)

            def attention(g, t):
                if t == 0:
                    pe.wait_ge(qiT_done.sem, qiT_done.now(g))
                    pe.wait_ge(qiT_done1.sem, qiT_done1.now(g))
                pe.wait_ge(sbd_done.sem, sbd_done.now(g, t + 1))
                pe.wait_ge(y_done.sem, y_done.now(g, t) if t else y_done.before(g))
                for j in range(BPT):
                    for a in range(2):
                        mm(O_ps[j * BLK:(j + 1) * BLK, a * SW:(a + 1) * SW], qiT[:, a, t * P + j * BLK:t * P + (j + 1) * BLK],
                           sbd[:, t % 2, j, a, :], start=(a == 0), stop=False, skip_group_check=True, tile_position=(0, j * BLK))
                pe.wait_ge(w_done.sem, w_done.now(g, t + 1))
                apart(pe)
                for n in range(H):
                    h = ((n % 8) // HG * 2 + n // 8) * HG + n % HG
                    for j in range(BPT):
                        r = slice(j * BLK, (j + 1) * BLK)
                        f = mm(O_ps[r, h * E1:(h + 1) * E1], wts[r, t % 2, n, :], v1[r, t, h, :], start=False, stop=True,
                               skip_group_check=True, tile_position=(j * BLK, j * BLK))
                f.then_inc(att_ps.sem, 1)

            def adds(g, t, a, first=False):
                if t or a:
                    pe.wait_ge(st_done.sem, st_done.now(g, (2 * t + a) * BPT))
                else:
                    if not first:
                        pe.wait_ge(z3_done.sem, z3_done.now(g - 1))
                    pe.wait_ge(vx_done.sem, vx_done.now(g))
                    pe.wait_ge(ks_done.sem, ks_done.now(g))
                mm(U_ps, ks[:, t, a * HALF:(a + 1) * HALF].rearrange("p h c d -> p (h c d)"),
                   vx[:, t, :, a * SW:(a + 1) * SW], start=True, stop=True).then_inc(u_ps.sem, 1)

            def scores(g, t):
                pe.wait_ge(s_copied.sem, s_copied.now(g, t) if t else s_copied.before(g))
                pe.wait_ge(w_done.sem, w_done.now(g, t) if t else w_done.before(g))
                apart(pe)
                for hg in range(NHG):
                    if hg >= 2:
                        pe.wait_ge(sd_group.sem, sd_group.now(g, NHG * t + hg - 1))
                        apart(pe)
                    r = slice(hg * 32, hg * 32 + 32)
                    for w, (st, mv_) in enumerate(((kT, qx), (fkT, fqx))):
                        for j in range(BPT):
                            f = mm(ps[j * BLK:(j + 1) * BLK, 2 * (hg % 2) + w, hg // 2 * P:(hg // 2 + 1) * P],
                                   st[r, t * P + j * BLK:t * P + (j + 1) * BLK], mv_[r, t, j].rearrange("p h s -> p (h s)"),
                                   start=True, stop=True, tile_position=(hg * 32, j * BLK))
                    f.then_inc(sd_group.sem, 1)

            def tile_ahead(g, t):
                adds(g, t, 0)
                scores(g, t)
                adds(g, t, 1)

            def pe_body(g, more):
                n = g + 1
                attention(g, 0)
                if more:
                    pe.wait_ge(slot_steps.sem, slot_steps.before(g))
                    pe.wait_ge(row_done.sem, row_done.before(g))
                    norm_T(n)
                tile_ahead(g, 2)
                if more:
                    project(n)
                attention(g, 1)
                tile_ahead(g, 3)
                if more:
                    exponents(n)
                attention(g, 2)
                if more:
                    query_T(n)
                attention(g, 3)
                if more:
                    key_T(n)
                pe.wait_ge(y_done.sem, y_done.now(g))
                for t in range(TG):
                    f = tr(T6[:, t * P:(t + 1) * P], y[:, t].rearrange("p h d -> p (h d)"))
                f.then_inc(yT_ps.sem, 1)
                if more:
                    decayed_query_T(n)
                pe.wait_ge(yT_done.sem, yT_done.now(g))
                pe.wait_ge(st_done.sem, st_done.now(g))
                pe.wait_ge(keep_done.sem, keep_done.now(g))
                for t in range(TG):
                    o = T7[:, t * P:(t + 1) * P]
                    mm(o, yT[:, t * P:(t + 1) * P], wo[:], start=True, stop=False)
                    f = mm(o, h_keep[:, t * P:(t + 1) * P], ident, start=False, stop=True)
                f.then_inc(o_ps.sem, 1)
                if more:
                    scores(n, 0)
                    adds(n, 0, 0)
                if more:
                    pe.wait_ge(qiT_done.sem, qiT_done.now(n))
                    pe.wait_ge(qiT_done1.sem, qiT_done1.now(n))
                pe.wait_ge(n2_done.sem, n2_done.now(g))
                for t in range(TG):
                    f = tr(T4[:, t * P:(t + 1) * P], n2[:, t, :])
                f.then_inc(n2T.sem, 1)
                if more:
                    adds(n, 0, 1)
                pe.wait_ge(h2T_done.sem, h2T_done.now(g))
                for t in range(TG):
                    f = mm(T4[:, t * NE:(t + 1) * NE], h2T[:, t * P:(t + 1) * P], rwt[:], start=True, stop=True)
                f.then_inc(lg_ps.sem, 1)
                for t in range(TG):
                    f = tr(T5[:, t * P:(t + 1) * P], h2T[:, t * P:(t + 1) * P])
                f.then_inc(h2_ps.sem, 1)
                if more:
                    tile_ahead(n, 1)
                pe.wait_ge(lg_done.sem, lg_done.now(g))
                pe.wait_ge(pre_done.sem, pre_done.now(g))
                rk_o = T4[:, 64:64 + TG * NE]
                mm(rk_o, tri_b[:], msk[:].rearrange("p t e -> p (t e)"), start=True, stop=False)
                mm(rk_o, ones_b[:], pre[:, 0:TG, :].rearrange("p t e -> p (t e)"), start=False, stop=True).then_inc(rk_ps.sem, 1)

            norm_T(0)
            project(0)
            pe.wait_ge(s_crep, 1)
            for b in range(B):
                mm(ps[:, 2 + 4 * b, :], c_rep[:, b, :], wmod[:, 0:512], start=True, stop=True)
                f = mm(ps[:, 3 + 4 * b, 0:256], c_rep[:, b, :], wmod[:, 512:768], start=True, stop=True)
            f.then_inc(s_modb, 1)
            pe.wait_ge(s_small, 32)
            pe.wait_ge(s_trib, 2)
            exponents(0)
            query_T(0)
            key_T(0)
            decayed_query_T(0)
            pe.wait_ge(s_gate, 2)
            adds(0, 0, 0, first=True)
            scores(0, 0)
            adds(0, 0, 1)
            tile_ahead(0, 1)
            with pe.Fori(0, GROUPS - 1) as g:
                pe_body(g, True)
            pe_body(GROUPS - 1, False)

            pe.wait_ge(s_lastx, 16)
            tr(T4[:, 0:NE], lastx[:, 0:DM]).then_inc(s_lastT, 1)

            def slots_T(u, i):
                pe.wait_ge(xb_in[u].sem, xb_in[u].now(i))
                if u == 0:
                    pe.wait_ge(bT_done[1].sem, bT_done[1].before(i))
                    pe.wait_ge(hid_done[1].sem, hid_done[1].before(i, 2 * FT - 2))
                else:
                    pe.wait_ge(bT_done[0].sem, bT_done[0].now(i))
                    pe.wait_ge(hid_done[0].sem, hid_done[0].now(i, 2 * FT - 2))
                for a in range(CT):
                    f = tr(ps[:, a // 4, (a % 4) * P:(a % 4 + 1) * P], xb[:, u, a, 0:DM])
                f.then_inc(bT_ps[u].sem, 1)

            def up(u, i):
                pe.wait_ge(w1_in[u].sem, w1_in[u].now(i))
                pe.wait_ge(bT_done[u].sem, bT_done[u].now(i))
                for f in range(FT):
                    for n, (c0, cn) in enumerate(NHALF):
                        k = 2 * f + n
                        if k >= 4:
                            pe.wait_ge(hid_done[u].sem, hid_done[u].now(i, k - 3))
                        elif k >= 2 and u:
                            pe.wait_ge(hid_done[0].sem, hid_done[0].now(i, 2 * FT - 3 + k))
                        elif k >= 2:
                            pe.wait_ge(hid_done[1].sem, hid_done[1].before(i, 2 * FT - 3 + k))
                        mm(ps[:, k % 4, 0:cn], w1t[:, u, f * P:(f + 1) * P], bT[:, u, c0:c0 + cn], start=True, stop=True).then_inc(up_ps[u].sem, 1)

            def down(u, i, n):
                c0, cn = NHALF[n]
                if n == 0:
                    pe.wait_ge(w2_in[u].sem, w2_in[u].now(i))
                pe.wait_ge(hid_done[u].sem, hid_done[u].now(i))
                if u:
                    pe.wait_ge(oT_done[0].sem, oT_done[0].now(i, n + 1))
                else:
                    pe.wait_ge(oT_done[1].sem, oT_done[1].before(i, n + 1))
                for f in range(FT):
                    m = mm(ps[:, 4 + n, 0:cn], w2t[:, u, f, :], hid[:, u, f, c0:c0 + cn], start=(f == 0), stop=(f == FT - 1))
                m.then_inc(dn_ps[u].sem, 1)

            def rows(u, i):
                pe.wait_ge(oT_done[u].sem, oT_done[u].now(i, 1))
                if u:
                    pe.wait_ge(r_done[0].sem, r_done[0].now(i))
                else:
                    pe.wait_ge(r_done[1].sem, r_done[1].before(i))
                for a in range(CT):
                    if a == NHALF[1][0] // P:
                        pe.wait_ge(oT_done[u].sem, oT_done[u].now(i, 2))
                    f = tr(ps[:, 6 + a // 4, (a % 4) * P:(a % 4 + 1) * P], oT[:, u, a * P:(a + 1) * P])
                f.then_inc(r_ps[u].sem, 1)

            slots_T(0, 0)
            with pe.Fori(0, NE // 2) as i:
                up(0, i)
                slots_T(1, i)
                down(0, i, 0)
                down(0, i, 1)
                up(1, i)
                rows(0, i)
                down(1, i, 0)
                slots_T(0, i + 1)
                down(1, i, 1)
                rows(1, i)
            pe.wait_ge(oT_done[1].sem, oT_done[1].now(NE // 2 - 1))
            tr(T4[0:NE, 0:P], lastO[:]).then_inc(s_lastO, 1)


_OUT = ((B, S, DM), "float32")


def kernel(**inputs):
    import concourse.bacc as _bacc
    from concourse.bass_utils import run_bass_kernel_spmd as _run

    a = {k: np.asarray(v) for k, v in inputs.items()}
    arrays = {
        "x": a["L0_attn_x"],
        "wall": np.concatenate([a["L0_attn_Wq"], a["L0_attn_Wk"], a["L0_attn_Wv"], a["L0_attn_Wbeta"]], axis=1),
        "wo": a["L0_attn_Wo"],
        "rows": np.concatenate([a["L0_attn_bo"], a["L0_attn_ln_gamma"], a["L0_attn_ln_beta"], a["L0_attn_bbeta"]])[None, :],
        "rwt": a["L0_ffn_router_w"].T,
        "w1": a["L0_ffn_w1"],
        "w2": a["L0_ffn_w2"],
        "ct": a["L0_c"].T,
        "wmod": a["L0_wmod"],
        "constants": constants(),
        "bo": a["L0_attn_bo"][:, None],
    }
    arrays = {f"in_{k}": np.ascontiguousarray(v) for k, v in arrays.items()}
    nc = _bacc.Bacc("TRN2", target_bir_lowering=False, num_devices=1)
    args = [nc.dram_tensor(n, v.shape, mybir.dt.from_np(v.dtype), kind="ExternalInput").ap() for n, v in arrays.items()]
    out = nc.dram_tensor("out", _OUT[0], F32, kind="ExternalOutput").ap()
    program(nc, *args, out)
    r = _run(nc, [arrays], core_ids=[0])
    return r.results[0]["out"]
```

```python
import numpy as np
import concourse.bass as bass
from concourse import mybir
from contextlib import ExitStack

F32 = mybir.dt.float32
BF16 = mybir.dt.bfloat16
U32 = mybir.dt.uint32
ALU = mybir.AluOpType
ACT = mybir.ActivationFunctionType
AX = mybir.AxisListType

P = 128
B, S, DM = 2, 1024, 128
H, DH, C = 16, 8, 2
HC = H * C
ROPE_HALF = DH // 2
NE, FF = 8, 512
TOPK = 2
NTOK = B * S
PAIRS = NTOK * TOPK
CAP = int(1.25 * PAIRS / NE) + 1
LN_EPS = 1e-5
DEN_EPS = 1e-6

TG = 4
GPB = S // (TG * P)
GROUPS = B * GPB
BLK = 32
BPT = P // BLK
SUB = 8
NSUB = BLK // SUB
HG = 4
NHG = H // HG
E1 = DH + 1
HALF = H // 2
SW = HALF * E1
HP = BLK // (C * DH)
PW = HP * E1
NB = TG * BPT
GT = TG * P

RW = DM + 2
CM = CAP - 1
CT = CM // P
ARENA = 24064
ROWS = 12 * 512
CH = (CT + 1) // 2 * P
NHALF = [(0, CH), (CH, CAP - CH)]
FT = FF // P

_widths = [("ident", P), ("gk", NSUB * P), ("own", P), ("cq", P), ("ck", P), ("kbias", NSUB),
           ("qmask", NSUB), ("causal", BLK), ("hmask", HG), ("smask", SW), ("tri", P), ("spread", P), ("tile_half", TG * 2 * BPT), ("blk", BPT),
           ("cos", GROUPS * TG * ROPE_HALF), ("sin", GROUPS * TG * ROPE_HALF), ("keep", GROUPS), ("iota", NE), ("pid", TG * TOPK)]
COL, _at = {}, 0
for _n, _w in _widths:
    COL[_n] = slice(_at, _at + _w)
    _at += _w
NCONST = _at
WALL = 3 * DM + HC
ROWV = 3 * DM + HC


def constants():
    c = np.zeros((P, NCONST), np.float32)
    p = np.arange(P)
    r, t = p[:, None], p[None, :]
    same = r // BLK == t // BLK
    c[:, COL["ident"]] = np.eye(P)
    for i in range(NSUB):
        ref = (t // BLK) * BLK + i * SUB
        plus = same & (r >= ref) & (r <= t)
        minus = same & (r < ref) & (r > t)
        c[:, COL["gk"]][:, i * P:(i + 1) * P] = plus.astype(np.float32) - minus
        c[:, COL["kbias"]][:, i] = np.where(p % BLK < (i + 1) * SUB, 0.0, -1e4)
        c[:, COL["qmask"]][:, i] = (p % BLK) // SUB == i
    c[:, COL["own"]] = (r // SUB == t // SUB) & (r <= t)
    c[:, COL["cq"]] = same & (r <= t)
    c[:, COL["ck"]] = same & (r > t)
    c[:, COL["causal"]] = (p % BLK)[:, None] <= np.arange(BLK)[None, :]
    c[:, COL["hmask"]] = (p // DH % HG)[:, None] == np.arange(HG)[None, :]
    c[:, COL["smask"]] = (p // (C * DH))[:, None] == (np.arange(SW) // E1)[None, :]
    c[:, COL["tri"]] = r < t
    c[:, COL["spread"]] = r % (HALF * C) == t // DH
    col = np.arange(TG * 2 * BPT)[None, :] // BPT
    c[:, COL["tile_half"]] = (p // (HALF * C))[:, None] == col
    c[:, COL["blk"]] = (p // BLK)[:, None] == np.arange(BPT)[None, :]
    inv = (1.0 / 10000.0 ** (np.arange(0, DH, 2, dtype=np.float32) / np.float32(DH))).astype(np.float32)
    ang = (np.arange(S, dtype=np.float32)[:, None] * inv[None, :]).astype(np.float32)
    tab = lambda f: np.tile(f(ang).astype(np.float32).reshape(S // P, P, ROPE_HALF).transpose(1, 0, 2).reshape(P, -1), (1, B))
    c[:, COL["cos"]] = tab(np.cos)
    c[:, COL["sin"]] = tab(np.sin)
    c[:, COL["keep"]] = (np.arange(GROUPS) % GPB != 0)[None, :]
    c[:, COL["iota"]] = np.arange(NE)[None, :]
    tok = np.arange(TG)[None, :, None] * P + p[:, None, None]
    c[:, COL["pid"]] = (TOPK * tok + np.arange(TOPK)[None, None, :]).reshape(P, -1)
    return c


OUT_ORDER = list(range(GROUPS))
POOL_OUT = OUT_ORDER[1::4]
VECTOR_OUT = [g for g in OUT_ORDER if g not in POOL_OUT]


class Event:

    def __init__(self, sem, per, ahead):
        self.sem, self.per, self.ahead = sem, per, per if ahead else 0

    def now(self, step, k=None):
        return step * self.per + (self.ahead + (self.per if k is None else k))

    def before(self, step, k=None):
        assert self.ahead
        return step * self.per + (self.per if k is None else k)


class Part:

    def __init__(self, g, step, lo, hi, banks):
        self.g, self.step, self.lo, self.hi = g, step, lo, hi
        self.n = hi - lo
        self.tiles = range(lo, hi)
        self.T_y, self.T_o, self.T_n, self.T_l, self.T_h = banks
        self.stats = 2 * (2 * lo + 1) if lo else 0


def program(nc, x_d, wall_d, wo_d, rows_d, rwt_d, w1_d, w2_d, ct_d, wmod_d, const_d, bo_d, out_d):
    x_v = x_d.rearrange("b (g t p) c -> (b g) p t c", t=TG, p=P)
    out_v = out_d.rearrange("b (g t p) c -> (b g) p t c", t=TG, p=P)
    disp_d = nc.dram_tensor("dispatched", [ROWS, RW], F32, kind="Internal").ap()
    pair_d = nc.dram_tensor("pair_out", [PAIRS, DM], F32, kind="Internal").ap()
    pair_v = pair_d.rearrange("(g t p k) c -> g p t (k c)", t=TG, p=P, k=TOPK)

    def w1_v(e):
        return w1_d[bass.ds(e, 1), :, :].rearrange("e p f -> p (e f)")

    def w2_v(e):
        return w2_d[bass.ds(e, 1), :, :].rearrange("e (f p) h -> p (e f) h", p=P)

    ctx = ExitStack()
    with ctx:
        def sb(name, shape, dt=F32):
            return ctx.enter_context(nc.sbuf_tensor(name, shape, dt))

        def sem(name):
            return ctx.enter_context(nc.semaphore(name))

        ahead_of = {"dve": [], "act": [], "pe": [], "pool": [], "sp": []}

        def event(name, per, ahead=None):
            e = Event(sem(name), per, ahead)
            if ahead:
                ahead_of[ahead].append(e)
            return e

        const = sb("const", [P, NCONST])
        K = {n: const[:, s] for n, s in COL.items()}
        ident = K["ident"]
        tri_b = sb("tri_b", [P, P], BF16)
        ones_b = sb("ones_b", [P, P], BF16)
        ones_row = sb("ones_row", [1, P])
        vec_row = sb("vec_row", [1, ROWV])
        wall = sb("wall", [P, WALL])
        wo = sb("wo", [P, DM])
        rwt = sb("rwt", [P, NE])
        wmod = sb("wmod", [P, 6 * DM])
        cT = sb("cT", [P, B])
        c_e = sb("c_e", [P, B])
        c_s = sb("c_s", [P, B])
        c_silu = sb("c_silu", [P, B])
        c_rep = sb("c_rep", [P, B, P])
        modc = sb("modc", [P, 4, GROUPS])
        vecs = sb("vecs", [P, ROWV])
        gates = sb("gates", [P, B, 2, DM])
        attn_g = sb("attn_g", [P, B, GPB, DM])
        attn_b = sb("attn_b", [P, B, GPB, DM])
        gate_b = sb("gate_b", [P, B, GPB, DM])
        half_neg = sb("half_neg", [P, GROUPS + 1, TG])
        fill = sb("fill", [P, 4, RW])
        zero = sb("zero", [P, 1024])

        arena = sb("arena", [P, ARENA])

        def carver():
            at = [0]

            def carve(*shape):
                n = int(np.prod(shape))
                v = arena[:, at[0]:at[0] + n]
                at[0] += n
                assert at[0] <= ARENA
                names = "abcd"[:len(shape)]
                return v.rearrange(f"p ({' '.join(names)}) -> p {' '.join(names)}", **dict(zip(names, shape)))

            return carve

        carve = carver()
        X = sb("X", [P, GROUPS, TG * DM])
        st6 = sb("st6", [P, GROUPS + 1, TG, 6])
        mv = sb("mv", [P, GROUPS + 1, TG, 2])
        ve = sb("ve", [P, GROUPS + 1, TG])
        rstd = sb("rstd", [P, GROUPS + 1, TG])
        mod_b = carve(B, 6 * DM)
        gsign = carve(B, 2, DM)
        gabs = carve(B, 2, DM)
        n1 = carve(TG, DM)
        hT = sb("hT", [P, GT])
        h_keep = sb("h_keep", [P, GT])
        bo_col = sb("bo_col", [P, 1])
        raw = carve(TG, WALL)
        zl = sb("zl", [P, TG, HC])
        ze = sb("ze", [P, TG, HC])
        zn = sb("zn", [P, TG, HC])
        rate = sb("rate", [P, TG, HC])
        sums = sb("sums", [P, TG * 2, BPT])
        fk = sb("fk", [P, TG, HC, NSUB])
        ex = sb("ex", [P, 3 * TG * HC + TG * 2 * BPT])
        dec = sb("dec", [P, TG * 2 * BPT])
        fq = sb("fq", [P, TG * HC, NSUB])
        m1 = carve(TG, 2 * H, ROPE_HALF)
        m2 = carve(TG, 2 * H, ROPE_HALF)
        m3 = carve(TG, 2 * H, ROPE_HALF)
        m4 = carve(TG, 2 * H, ROPE_HALF)
        rot = carve(TG, 2 * H, DH)
        rmin = carve(TG, 2 * H, DH)
        rexp = carve(TG, 2 * H, DH)
        phi = carve(TG, 2 * H, DH)
        qi = carve(TG, H, C, DH)
        ks = carve(TG, H, C, DH)
        v1 = sb("v1", [P, TG, H, E1])
        vx = carve(TG, BPT, H * E1)
        qx = carve(TG, BPT, HG, BLK)
        fqx = carve(TG, BPT, HG, BLK)
        kT = sb("kT", [P, GT])
        fkT = sb("fkT", [P, GT])
        qiT = sb("qiT", [P, 2, GT])
        state = carve(NB, 2, PW)
        sbd = carve(2, BPT, 2, SW)
        s_sb = sb("s_sb", [P, 2, 2, 2 * P])
        s_mk = sb("s_mk", [P, 2, 4 * HG, BLK])
        wts = sb("wts", [P, 2, 4 * HG, BLK])
        den = sb("den", [P, TG, H])
        rden = sb("rden", [P, TG, H])
        y = sb("y", [P, TG, H, DH])
        yT = sb("yT", [P, GT])
        z3 = sb("z3", [P, TG, DM])
        x2 = sb("x2", [P, TG, DM])
        n2 = sb("n2", [P, TG, DM])
        h2T = sb("h2T", [P, GT])
        gh = sb("gh", [P, TG, DM])
        row = sb("row", [P, TG, TOPK, RW])
        lg = sb("lg", [P, TG, NE])
        mx = sb("mx", [P, TG, NE])
        ix = sb("ix", [P, TG, NE], U32)
        ef = sb("ef", [P, TG, TOPK])
        oh = sb("oh", [P, TG, TOPK, NE])
        msk = sb("msk", [P, TG, NE], BF16)
        pre = sb("pre", [P, TG + 1, NE], BF16)
        rm = sb("rm", [P, TG, TOPK, NE])
        rk = sb("rk", [P, TG, TOPK])
        ov = sb("ov", [P, TG, TOPK])
        sl = sb("sl", [P, TG, TOPK])
        idx = sb("idx", [P, TG, TOPK], U32)
        pid = sb("pid", [P, TG, TOPK])
        dl = sb("dl", [P, TG])
        de = sb("de", [P, TG])
        dp = sb("dp", [P, TG])
        w0 = sb("w0", [P, TG])

        carve = carver()
        w1t = sb("w1t", [P, 2, FF])
        w2t = sb("w2t", [P, 2, FT, DM])
        xb = carve(2, CT, RW)
        lastx = sb("lastx", [NE, RW])
        last_p = sb("last_p", [P, 2, DM])
        ones_col = sb("ones_col", [P, 1])
        lastT = sb("lastT", [P, NE + 1])
        lastO = sb("lastO", [P, NE])
        lastR = sb("lastR", [NE, DM])
        bT = carve(2, CAP)
        hid = carve(2, FT, CAP)
        meta = sb("meta", [P, 2, CT, 2])
        orow = carve(2, CT, DM)
        yb = carve(GROUPS, TG, TOPK, DM)
        ys = carve(GROUPS, TG, DM)
        yo = carve(GROUPS, TG, DM)

        ps = ctx.enter_context(nc.psum_tensor("ps", [P, 8, 512], F32))
        S_ps = ps[:, 0:4:2, 0:2 * P]
        D_ps = ps[:, 1:4:2, 0:2 * P]
        T4 = ps[:, 4, :]
        T5 = ps[:, 5, :]
        T6 = ps[:, 6, :]
        T7 = ps[:, 7, :]
        O_ps = ps[:, 6, 0:H * E1]
        U_ps = ps[:, 7, 0:2 * BPT * PW].rearrange("p (a j w) -> p a j w", a=2, w=PW)

        s_const, s_wall, s_vec, s_c, s_wmod = sem("const_in"), sem("wall_in"), sem("vec_in"), sem("c_in"), sem("wmod_in")
        s_small = sem("small_weights_in")
        s_ms = sem("memsets")
        s_bo = sem("bo_in")
        s_dms = sem("vector_memsets")
        s_apart = sem("waits_taken")
        s_fillms = sem("fill_set")
        s_filled = sem("dram_filled")
        s_ce, s_cs, s_csilu, s_crep = sem("c_exp"), sem("c_sig"), sem("c_silu_done"), sem("c_rep_done")
        s_modc, s_modc_sb = sem("modc_ps"), sem("modc_done")
        s_modb = sem("modb_ps")
        s_vecp, s_vecs = sem("vecs_ps"), sem("vecs_done")
        s_gate = sem("gates_steps")
        s_trib = sem("tri_done")
        s_state0 = sem("state_zero")
        s_tables = sem("group_tables")

        s_x0, s_x = sem("first_x_in"), sem("x_in")
        xb_done = event("x_plus_bias", 1)
        keep_done = event("h_kept", 1)
        dec_done = event("decays_kept", 1)
        carry_done = event("state_carried", 1)
        stats_a, stats_b = event("ln_a_stats", 2 * TG + 1), event("ln_b_stats", 2 * (2 * TG + 1))
        s_rstd, rstd_done = sem("ln_a_rstd"), event("ln_b_rstd", 2)
        n1_done = event("n1_done", TG)
        n1T = event("n1T_ps", 1)
        hT_done = event("hT_done", 1)
        proj = event("proj_ps", TG)
        raw_done = event("raw_done", TG)
        zadd = event("z_add", 1)
        zclamp = event("z_clamp", 1)
        zexp = event("z_exp", 1)
        zln = event("z_ln", 1)
        rate_done = event("rate_done", 1)
        sum_ps = event("block_rates_ps", 1)
        sums_done = event("block_rates", 1)
        expo_ps = event("exponents_ps", 2)
        fk_done = event("fk_done", 1)
        ex_done = event("ex_done", 1, "act")
        fq_done = event("fq_done", 1)
        rope_a = event("rope_dve", 2)
        rope_b = event("rope_pool", 2)
        rot_done = event("rot_done", 2)
        rmin_done = event("rmin_done", 1)
        rexp_done = event("rexp_done", 1)
        phi_done = event("phi_done", 1)
        qi_done = event("qi_done", TG)
        ks_done = event("ks_done", TG)
        v1_done = event("v1_done", 1)
        vx_done = event("vx_done", BPT)
        tq = event("q_T_ps", 1)
        tfq = event("fq_T_ps", 1)
        tk = event("k_T_ps", 1)
        tfk = event("fk_T_ps", 1)
        tqi = event("qi_T_ps", 2)
        qx_done = event("qx_done", 1)
        fqx_done = event("fqx_done", 1)
        kT_done = event("kT_done", 1)
        fkT_done = event("fkT_done", 1)
        qiT_done = event("qiT_done", 2)
        sd_group = event("sd_head_groups", NHG * TG, "pe")
        s_copied = event("s_copied", TG, "act")
        s_masked = event("s_masked", TG, "pool")
        w_done = event("weights_done", TG, "dve")
        u_ps = event("u_ps", TG)
        st_done = event("state_done", 2 * NB, "dve")
        sbd_done = event("state_masked", TG)
        att_ps = event("attention_ps", TG, "pe")
        den_done = event("den_done", TG)
        rden_done = event("rden_done", TG)
        y_done = event("y_done", TG, "dve")
        yT_ps = event("yT_ps", 1)
        yT_done = event("yT_done", 1)
        o_ps = event("wo_ps", 1, "pe")
        z3_done = event("z3_done", TG)
        x2_done = event("x2_done", TG)
        n2_done = event("n2_done", TG)
        n2T = event("n2T_ps", 1)
        h2T_done = event("h2T_done", 1)
        h2_ps = event("h2_rows_ps", 1)
        row_done = event("h2_rows", 2, "act")
        gh_done = event("gated_h2", 1)
        base_done = event("base_done", 1)
        lg_ps = event("logits_ps", 1)
        lg_done = event("logits_done", 1)
        mx_done = event("top_done", TG)
        ix_done = event("top_index", TG)
        choice_steps = event("choice_steps", 3)
        pre_done = event("prefix_done", TG + 1)
        rk_ps = event("rank_ps", 1)
        slot_steps = event("slot_steps", 6, "dve")
        idx_done = event("slot_index", 1)
        dl_done = event("logit_gap", 1)
        de_done = event("gap_exp", 1)
        wrow_done = event("row_weights", 2)
        prow_done = event("row_ids", 1)
        pid_next = event("ids_next", 1)
        scat = event("dispatched_rows", 16 * TG * TOPK)
        rows_left = event("rows_left", 1, "sp")

        w1_in = [event(f"w1_in{u}", 16) for u in range(2)]
        w2_in = [event(f"w2_in{u}", 16) for u in range(2)]
        xb_in = [event(f"xb_in{u}", 16) for u in range(2)]
        s_lastx, s_lastT, s_lastT_sb = sem("last_in"), sem("last_T"), sem("last_T_sb")
        bT_ps = [event(f"slots_T_ps{u}", 1) for u in range(2)]
        bT_done = [event(f"slots_T{u}", 3, "dve") for u in range(2)]
        meta_done = [event(f"slot_meta{u}", 1) for u in range(2)]
        up_ps = [event(f"up_ps{u}", 2 * FT, "pe") for u in range(2)]
        hid_done = [event(f"hidden{u}", 2 * FT, "act") for u in range(2)]
        r_ps = [event(f"rows_ps{u}", CT, "pe") for u in range(2)]
        last_done = [event(f"last_products{u}", FT) for u in range(2)]
        r_done = [event(f"rows_done{u}", CT + 1, "dve") for u in range(2)]
        osc = [event(f"rows_out{u}", 16 * CT) for u in range(2)]
        outs_left = [event(f"outs_left{u}", 1, "sp") for u in range(2)]
        s_lastO, s_lastR, s_lastS = sem("last_out_T"), sem("last_out_rows"), sem("last_rows_out")

        s_yb = [sem(f"pairs_in{g}") for g in range(GROUPS)]
        s_ys, s_yg, s_yo = sem("pairs_sum"), sem("pairs_gated"), sem("out_ready")
        s_pys, s_pyg, s_pyo = sem("pool_pairs_sum"), sem("pool_pairs_gated"), sem("pool_out_ready")
        s_out = sem("out_written")

        def made(n, a):
            return 2 * (n - 1) + a + 1

        def whole(g):
            return Part(g, g, 0, TG, (T6, T7, T4, T4, T5))

        half_a = Part(GROUPS - 1, GROUPS - 1, 0, TG // 2, (T4, T5, T4, T4, T5))
        half_b = Part(GROUPS - 1, GROUPS, TG // 2, TG, (T6, T7, T6, T6, T7))

        def rope_table(name, g):
            v = K[name].rearrange("p (g t d) -> p g t d", g=GROUPS, t=TG)[:, bass.ds(g, 1), :, :]
            return v.rearrange("p g t d -> p (g t) d").unsqueeze(2).to_broadcast([P, TG, 2 * H, ROPE_HALF])

        def row_bank(u, a):
            return ps[:, 4 + (u * CT + a) % 4, :]

        def output_gate(g):
            return gate_b[:].rearrange("p b g c -> p (b g) c")[:, g:g + 1, :].to_broadcast([P, TG, DM])

        block = ctx.enter_context(nc.Block())

        def apart(eng):
            eng.sem_inc(s_apart, 1)

        def start_ahead(eng, who):
            for e in ahead_of[who]:
                eng.sem_inc(e.sem, e.ahead)

        @block.sync
        def _(sp):
            sp.dma_start(X[:, 0].rearrange("p (t c) -> p t c", c=DM), x_v[0]).then_inc(s_x0, 16)
            sp.dma_start(const[:], const_d).then_inc(s_const, 16)
            sp.dma_start(vec_row[:], rows_d).then_inc(s_vec, 16)
            sp.dma_start(cT[:], ct_d).then_inc(s_c, 16)
            sp.dma_start(wall[:], wall_d).then_inc(s_wall, 16)
            sp.dma_start(wmod[:], wmod_d).then_inc(s_wmod, 16)
            sp.dma_start(wo[:], wo_d).then_inc(s_small, 16)
            sp.dma_start(rwt[:], rwt_d).then_inc(s_small, 16)
            sp.dma_start(bo_col[:], bo_d).then_inc(s_bo, 16)
            sp.dma_start(X[:, 1:].rearrange("p g (t c) -> p (g t) c", c=DM),
                         x_d.rearrange("b (t p) c -> p (b t) c", p=P)[:, TG:, :]).then_inc(s_x, 16)
            start_ahead(sp, "sp")
            for u in range(2):
                sp.dma_start(w1t[:, u, :], w1_v(u)).then_inc(w1_in[u].sem, 16)
                sp.dma_start(w2t[:, u], w2_v(u)).then_inc(w2_in[u].sem, 16)
            sp.wait_ge(s_fillms, 3)
            for n in range(12):
                sp.dma_start(disp_d[512 * n:512 * n + 512, :].rearrange("(p a) c -> p (a c)", a=4),
                              fill[:].rearrange("p a c -> p (a c)")).then_inc(s_filled, 16)
            for n in range(4):
                sp.dma_start(pair_d[1024 * n:1024 * n + 1024, :].rearrange("(p a) c -> p (a c)", a=8), zero[:]).then_inc(s_filled, 16)
            with sp.Fori(0, GROUPS - 1) as g:
                sp.wait_ge(scat.sem, scat.now(g))
                sp.sem_inc(rows_left.sem, 1)
            sp.wait_ge(scat.sem, scat.now(GROUPS - 1))
            def slots(e):
                return disp_d[bass.ds(e * CAP, CM), :].rearrange("(p a) c -> p (a c)", a=CT)

            sp.dma_start(xb[:, 0, :, :].rearrange("p a c -> p (a c)"), slots(0)).then_inc(xb_in[0].sem, 16)
            sp.dma_start(lastx[:], disp_d[0:NE * CAP, :].rearrange("(e s) c -> e s c", s=CAP)[:, CM, :]).then_inc(s_lastx, 16)
            sp.dma_start(xb[:, 1, :, :].rearrange("p a c -> p (a c)"), slots(1)).then_inc(xb_in[1].sem, 16)

            def next_slots(u, i):
                sp.wait_ge(bT_ps[u].sem, bT_ps[u].now(i))
                sp.wait_ge(meta_done[u].sem, meta_done[u].now(i))
                sp.dma_start(xb[:, u, :, :].rearrange("p a c -> p (a c)"), slots(i * 2 + (u + 2))).then_inc(xb_in[u].sem, 16)

            def outs_gone(u, i):
                sp.wait_ge(osc[u].sem, osc[u].now(i))
                sp.sem_inc(outs_left[u].sem, 1)

            with sp.Fori(0, NE // 2 - 1) as i:
                next_slots(0, i)
                sp.wait_ge(up_ps[0].sem, up_ps[0].now(i))
                sp.dma_start(w1t[:, 0, :], w1_v(i * 2 + 2)).then_inc(w1_in[0].sem, 16)
                next_slots(1, i)
                sp.wait_ge(r_ps[0].sem, r_ps[0].now(i))
                sp.dma_start(w2t[:, 0], w2_v(i * 2 + 2)).then_inc(w2_in[0].sem, 16)
                sp.wait_ge(up_ps[1].sem, up_ps[1].now(i))
                sp.dma_start(w1t[:, 1, :], w1_v(i * 2 + 3)).then_inc(w1_in[1].sem, 16)
                outs_gone(0, i)
                sp.wait_ge(r_ps[1].sem, r_ps[1].now(i))
                sp.dma_start(w2t[:, 1], w2_v(i * 2 + 3)).then_inc(w2_in[1].sem, 16)
                outs_gone(1, i)
            next_slots(0, NE // 2 - 1)
            outs_gone(0, NE // 2 - 1)
            for u in range(2):
                sp.wait_ge(osc[u].sem, osc[u].now(NE // 2 - 1))
            sp.wait_ge(s_lastS, 16)
            for g in range(GROUPS):
                sp.dma_start(yb[:, g].rearrange("p t k c -> p t (k c)"), pair_v[g]).then_inc(s_yb[g], 16)
            for g in OUT_ORDER:
                if g in POOL_OUT:
                    sp.wait_ge(s_pyo, POOL_OUT.index(g) + 1)
                else:
                    sp.wait_ge(s_yo, VECTOR_OUT.index(g) + 1)
                sp.dma_start(out_v[g], yo[:, g]).then_inc(s_out, 16)
            sp.wait_ge(s_out, 16 * GROUPS)

        @block.gpsimd
        def _(pool):
            g_ = nc.gpsimd
            g_.memset(half_neg[:], -0.5).then_inc(s_ms, 1)
            g_.memset(ones_row[:], 1.0).then_inc(s_ms, 1)
            g_.memset(ones_col[:], 1.0).then_inc(s_ms, 1)
            g_.memset(ones_b[:], 1.0).then_inc(s_ms, 1)
            start_ahead(pool, "pool")
            pool.wait_ge(s_ms, 4)

            def inv_std(p, n):
                pool.wait_ge(stats_b.sem, stats_b.now(p.g, p.stats + (n + 1) * (2 * p.n + 1)))
                g_.tensor_tensor(rstd[:, 0, p.lo:p.hi], ve[:, 0, p.lo:p.hi], half_neg[:, 0, p.lo:p.hi], ALU.pow).then_inc(rstd_done.sem, 1)

            def gated_rows(p):
                pool.wait_ge(row_done.sem, row_done.now(p.step, 1))
                g_.tensor_tensor(gh[:, p.lo:p.hi], row[:, p.lo:p.hi, 0, 0:DM], group_table(gate_b, p.g, p.n), ALU.mult).then_inc(gh_done.sem, 1)

            def dispatch(p):
                pool.wait_ge(s_filled, 16 * 16)
                pool.wait_ge(row_done.sem, row_done.now(p.step))
                pool.wait_ge(idx_done.sem, idx_done.now(p.step))
                pool.wait_ge(wrow_done.sem, wrow_done.now(p.step))
                pool.wait_ge(prow_done.sem, prow_done.now(p.step))
                apart(pool)
                for t in p.tiles:
                    for k in range(TOPK):
                        pool.indirect_dma_start(disp_d, bass.IndirectOffsetOnAxis(ap=idx[:, t, k:k + 1], axis=0),
                                                row[:, t, k, :], None, bounds_check=ROWS - 1, oob_is_err=False).then_inc(scat.sem, 16)

            def group_table(v, g, tiles=TG):
                return v[:].rearrange("p b g c -> p (b g) c")[:, bass.ds(g, 1), :].to_broadcast([P, tiles, DM])

            def rows_of(v, g):
                return v[:, bass.ds(g, 1), :].rearrange("p g (t c) -> p (g t) c", c=DM)

            def rope_products(g):
                pool.wait_ge(raw_done.sem, raw_done.now(g))
                uv = raw[:, :, 0:2 * DM].rearrange("p t (h r d) -> p t h r d", r=2, d=ROPE_HALF)
                g_.tensor_tensor(m3[:], uv[:, :, :, 0, :], rope_table("sin", g), ALU.mult).then_inc(rope_b.sem, 1)
                g_.tensor_tensor(m4[:], uv[:, :, :, 1, :], rope_table("cos", g), ALU.mult).then_inc(rope_b.sem, 1)

            def residual_bias(g):
                pool.wait_ge(n1_done.sem, n1_done.now(g))
                pool.wait_ge(s_tables, 3)
                x_ = rows_of(X, g)
                g_.tensor_tensor(x_, x_, group_table(attn_b, g), ALU.add).then_inc(xb_done.sem, 1)

            def query_factors(g):
                pool.wait_ge(ex_done.sem, ex_done.now(g))
                g_.tensor_tensor(fq[:], ex[:, 0:TG * HC].unsqueeze(2).to_broadcast([P, TG * HC, NSUB]),
                                 K["qmask"].unsqueeze(1).to_broadcast([P, TG * HC, NSUB]), ALU.mult).then_inc(fq_done.sem, 1)

            def keys_decayed(g):
                pool.wait_ge(phi_done.sem, phi_done.now(g))
                for t in range(TG):
                    f = ex[:, (2 * TG + t) * HC:(2 * TG + t + 1) * HC].rearrange("p (h c) -> p h c", c=C)
                    g_.tensor_tensor(ks[:, t], phi[:, t, H:2 * H, :].unsqueeze(2).to_broadcast([P, H, C, DH]),
                                     f.unsqueeze(3).to_broadcast([P, H, C, DH]), ALU.mult).then_inc(ks_done.sem, 1)

            def mask_scores(g, t):
                pool.wait_ge(s_copied.sem, s_copied.now(g, t + 1))
                if t >= 2:
                    pool.wait_ge(w_done.sem, w_done.now(g, t - 1))
                else:
                    pool.wait_ge(w_done.sem, w_done.before(g, TG - 1 + t))
                g_.tensor_tensor(s_mk[:, t % 2], s_sb[:, t % 2].rearrange("p a (h t) -> p (a h) t", t=BLK),
                                 K["causal"].unsqueeze(1).to_broadcast([P, H, BLK]), ALU.mult).then_inc(s_masked.sem, 1)

            def mask_states(g, t):
                pool.wait_ge(st_done.sem, st_done.now(g, made(BPT * t + BPT - 1, 1)))
                if t >= 2:
                    pool.wait_ge(att_ps.sem, att_ps.now(g, t - 1))
                else:
                    pool.wait_ge(att_ps.sem, att_ps.before(g, TG - 1 + t))
                pairs = [P, BPT * 2, SW // PW, PW]
                g_.tensor_tensor(sbd[:, t % 2].rearrange("p j a (h w) -> p (j a) h w", w=PW),
                                 state[:, BPT * t:BPT * (t + 1)].rearrange("p j a w -> p (j a) w").unsqueeze(2).to_broadcast(pairs),
                                 K["smask"].rearrange("p (h w) -> p h w", w=PW).unsqueeze(1).to_broadcast(pairs), ALU.mult).then_inc(sbd_done.sem, 1)

            def pool_body(g, more):
                n = g + 1
                mask_scores(g, 2)
                mask_states(g, 2)
                if more:
                    rope_products(n)
                mask_scores(g, 3)
                mask_states(g, 3)
                if more:
                    query_factors(n)
                    residual_bias(n)
                    pool.wait_ge(u_ps.sem, u_ps.now(g))
                    keys_decayed(n)
                if more:
                    inv_std(whole(g), 0)
                    mask_scores(n, 0)
                    inv_std(whole(g), 1)
                    mask_states(n, 0)
                    mask_scores(n, 1)
                    gated_rows(whole(g))
                    mask_states(n, 1)
                    dispatch(whole(g))
                else:
                    inv_std(half_a, 0)
                    inv_std(half_a, 1)
                    inv_std(half_b, 0)
                    inv_std(half_b, 1)
                    dispatch(half_a)
                    dispatch(half_b)
                    gated_rows(half_a)
                    gated_rows(half_b)

            for n, at in enumerate((slice(1, 2), slice(2, GROUPS + 1))):
                pool.wait_ge(stats_a.sem, stats_a.now(0 if n == 0 else GROUPS - 1))
                g_.tensor_tensor(rstd[:, at], ve[:, at], half_neg[:, at], ALU.pow).then_inc(s_rstd, 1)
            pool.wait_ge(s_const, 16)
            rope_products(0)
            query_factors(0)
            keys_decayed(0)
            mask_scores(0, 0)
            mask_states(0, 0)
            mask_scores(0, 1)
            mask_states(0, 1)
            residual_bias(0)
            with pool.Fori(0, GROUPS - 1) as g:
                pool_body(g, True)
            pool_body(GROUPS - 1, False)
            with pool.Fori(0, NE // 2) as i:
                for u in range(2):
                    for a in range(CT):
                        pool.wait_ge(r_done[u].sem, r_done[u].now(i, a + 1))
                        apart(pool)
                        pool.indirect_dma_start(pair_d, bass.IndirectOffsetOnAxis(ap=meta[:, u, a, 0:1].bitcast(U32), axis=0),
                                                orow[:, u, a, :], None, bounds_check=PAIRS - 1, oob_is_err=False).then_inc(osc[u].sem, 16)
            pool.wait_ge(s_lastR, 2)
            pool.indirect_dma_start(pair_d, bass.IndirectOffsetOnAxis(ap=lastx[:, DM:DM + 1].bitcast(U32), axis=0),
                                    lastR[:], None, bounds_check=PAIRS - 1, oob_is_err=False).then_inc(s_lastS, 16)
            for n, g in enumerate(POOL_OUT):
                pool.wait_ge(s_yb[g], 16)
                g_.tensor_tensor(ys[:, g], yb[:, g, :, 0, :], yb[:, g, :, 1, :], ALU.add).then_inc(s_pys, 1)
                pool.wait_ge(s_pys, n + 1)
                g_.tensor_tensor(ys[:, g], ys[:, g], output_gate(g), ALU.mult).then_inc(s_pyg, 1)
                pool.wait_ge(s_pyg, n + 1)
                g_.tensor_tensor(yo[:, g].rearrange("p t c -> p (t c)"), ys[:, g].rearrange("p t c -> p (t c)"), X[:, g], ALU.add).then_inc(s_pyo, 1)

        @block.scalar
        def _(act):
            a_ = nc.scalar
            act.preload_act_table_set("natural_log_exp_and_others")
            start_ahead(act, "act")
            act.wait_ge(s_cs, 1)
            a_.activation(c_e[:], c_s[:], ACT.Exp, scale=-1.0).then_inc(s_ce, 1)

            def layer_input(g):
                act.wait_ge(n1T.sem, n1T.now(g))
                act.wait_ge(s_modc_sb, 3)
                a_.activation(hT[:], T4, ACT.Identity, bias=modc[:, 0, bass.ds(g, 1)], scale=modc[:, 1, bass.ds(g, 1)]).then_inc(hT_done.sem, 1)

            def projections(g):
                for t in range(TG):
                    act.wait_ge(proj.sem, proj.now(g, t + 1))
                    a_.copy(raw[:, t, :], ps[:, 5 - t % 2, 0:WALL]).then_inc(raw_done.sem, 1)

            def softplus(g):
                act.wait_ge(zclamp.sem, zclamp.now(g))
                a_.activation(ze[:], zl[:], ACT.Exp, scale=-1.0).then_inc(zexp.sem, 1)
                act.wait_ge(zexp.sem, zexp.now(g))
                a_.activation(zn[:], ze[:], ACT.Ln, bias=1.0).then_inc(zln.sem, 1)

            def factors(g):
                act.wait_ge(expo_ps.sem, expo_ps.now(g))
                for i in range(NSUB):
                    f = a_.activation(fk[:].rearrange("p t h i -> p (t h) i")[:, :, i], T5[:, i * TG * HC:(i + 1) * TG * HC],
                                      ACT.Exp, bias=K["kbias"][:, i:i + 1])
                f.then_inc(fk_done.sem, 1)
                a_.activation(ex[:], T4[:, 0:3 * TG * HC + TG * 2 * BPT], ACT.Exp, scale=-1.0).then_inc(ex_done.sem, 1)

            def feature_exp(g):
                act.wait_ge(rmin_done.sem, rmin_done.now(g))
                a_.activation(rexp[:], rmin[:], ACT.Exp).then_inc(rexp_done.sem, 1)

            def query_factors_T(g):
                act.wait_ge(tfq.sem, tfq.now(g))
                for j in range(HG):
                    f = a_.mul(fqx[:, :, :, j, :].rearrange("p t b s -> p (t b) s"),
                               T5.rearrange("p (n s) -> p n s", s=BLK), K["hmask"][:, j:j + 1])
                f.then_inc(fqx_done.sem, 1)

            def keys_T(g):
                act.wait_ge(tk.sem, tk.now(g))
                a_.copy(kT[:], T4).then_inc(kT_done.sem, 1)

            def values(g):
                act.wait_ge(s_dms, 1)
                act.wait_ge(raw_done.sem, raw_done.now(g))
                a_.copy(v1[:, :, :, 0:DH], raw[:, :, 2 * DM:3 * DM].rearrange("p t (h d) -> p t h d", d=DH)).then_inc(v1_done.sem, 1)
                act.wait_ge(v1_done.sem, v1_done.now(g))
                for j in range(BPT):
                    a_.mul(vx[:, :, j, :], v1[:].rearrange("p t h e -> p t (h e)"), K["blk"][:, j:j + 1]).then_inc(vx_done.sem, 1)

            def queries_T(g):
                for a, bank in enumerate((T4, T5)):
                    act.wait_ge(tqi.sem, tqi.now(g, a + 1))
                    a_.copy(qiT[:, a, :], bank).then_inc(qiT_done.sem, 1)

            def copy_scores(g, t):
                act.wait_ge(sd_group.sem, sd_group.now(g, NHG * (t + 1)))
                if t >= 2:
                    act.wait_ge(s_masked.sem, s_masked.now(g, t - 1))
                else:
                    act.wait_ge(s_masked.sem, s_masked.before(g, TG - 1 + t))
                a_.copy(s_sb[:, t % 2], S_ps).then_inc(s_copied.sem, 1)

            def output_T(p):
                act.wait_ge(yT_ps.sem, yT_ps.now(p.step))
                a_.copy(yT[:, p.lo * P:p.hi * P], p.T_y[:, p.lo * P:p.hi * P]).then_inc(yT_done.sem, 1)

            def second_input(p):
                act.wait_ge(n2T.sem, n2T.now(p.step))
                at = bass.ds(p.g, 1)
                a_.activation(h2T[:, p.lo * P:p.hi * P], p.T_n[:, p.lo * P:p.hi * P], ACT.Identity, bias=modc[:, 2, at], scale=modc[:, 3, at]).then_inc(h2T_done.sem, 1)

            def pair_rows(p):
                act.wait_ge(h2_ps.sem, h2_ps.now(p.step))
                act.wait_ge(rows_left.sem, rows_left.before(p.g))
                for k in range(TOPK):
                    a_.copy(row[:, p.lo:p.hi, k, 0:DM], p.T_h.rearrange("p (t c) -> p t c", c=DM)[:, p.lo:p.hi]).then_inc(row_done.sem, 1)

            def gap(p):
                act.wait_ge(dl_done.sem, dl_done.now(p.step))
                a_.activation(de[:, p.lo:p.hi], dl[:, p.lo:p.hi], ACT.Exp).then_inc(de_done.sem, 1)

            def act_body(g, more):
                n = g + 1
                act.wait_ge(o_ps.sem, o_ps.before(g))
                act.wait_ge(hT_done.sem, hT_done.now(g))
                a_.activation(h_keep[:], hT[:], ACT.Identity, bias=bo_col[:], scale=1.0).then_inc(keep_done.sem, 1)
                if more:
                    act.wait_ge(keep_done.sem, keep_done.now(g))
                    layer_input(n)
                copy_scores(g, 2)
                if more:
                    projections(n)
                    softplus(n)
                copy_scores(g, 3)
                if more:
                    factors(n)
                    feature_exp(n)
                    query_factors_T(n)
                    keys_T(n)
                    act.wait_ge(att_ps.sem, att_ps.now(g))
                    values(n)
                if more:
                    output_T(whole(g))
                    queries_T(n)
                    copy_scores(n, 0)
                    second_input(whole(g))
                    copy_scores(n, 1)
                    pair_rows(whole(g))
                    gap(whole(g))
                else:
                    output_T(half_a)
                    second_input(half_a)
                    output_T(half_b)
                    pair_rows(half_a)
                    gap(half_a)
                    second_input(half_b)
                    pair_rows(half_b)
                    gap(half_b)

            act.wait_ge(s_bo, 16)
            layer_input(0)
            projections(0)
            softplus(0)
            act.wait_ge(s_const, 16)
            factors(0)
            feature_exp(0)
            query_factors_T(0)
            keys_T(0)
            values(0)
            queries_T(0)
            copy_scores(0, 0)
            copy_scores(0, 1)
            with act.Fori(0, GROUPS - 1) as g:
                act_body(g, True)
            act_body(GROUPS - 1, False)
            act.preload_act_table(ACT.Silu)
            with act.Fori(0, NE // 2) as i:
                for u in range(2):
                    for f in range(FT):
                        for n, (c0, cn) in enumerate(NHALF):
                            k = 2 * f + n
                            act.wait_ge(up_ps[u].sem, up_ps[u].now(i, k + 1))
                            if k == 0:
                                act.wait_ge(r_ps[u].sem, r_ps[u].before(i))
                            a_.activation(hid[:, u, f, c0:c0 + cn], ps[:, k % 4, 0:cn], ACT.Silu).then_inc(hid_done[u].sem, 1)

        @block.vector
        def _(dve):
            v_ = nc.vector
            v_.memset(fill[:], 0.0).then_inc(s_fillms, 1)
            v_.memset(zero[:], 0.0).then_inc(s_fillms, 1)
            dve.wait_ge(s_fillms, 2)
            v_.memset(fill[:, :, DM:DM + 1], 1e9).then_inc(s_fillms, 1)
            v_.memset(v1[:, :, :, DH:E1], 1.0).then_inc(s_dms, 1)
            v_.memset(pre[:], 0.0).then_inc(s_dms, 1)
            start_ahead(dve, "dve")
            dve.wait_ge(s_dms, 2)
            v_.memset(state[:, 0], 0.0).then_inc(s_state0, 1)

            def layernorm(src, at, done, first, lo=0, hi=TG, ready=None):
                for t in range(lo, hi):
                    if ready:
                        dve.wait_ge(*ready(t))
                    v_.bn_stats(st6[:, at, t, :], src[:, t, :]).then_inc(done, 1)
                for t in range(lo, hi):
                    dve.wait_ge(done, first + (t - lo + 1))
                    apart(dve)
                    v_.bn_aggr(mv[:, at, t, :], st6[:, at, t, :]).then_inc(done, 1)
                dve.wait_ge(done, first + 2 * (hi - lo))
                v_.tensor_scalar(ve[:, at, lo:hi], mv[:, at, lo:hi, 1], LN_EPS, None, ALU.add).then_inc(done, 1)

            def rows_of(v, g):
                return v[:, bass.ds(g, 1), :].rearrange("p g (t c) -> p (g t) c", c=DM)

            def statistics(g):
                dve.wait_ge(s_x if g else s_x0, 16)
                layernorm(rows_of(X, g), g + 1, stats_a.sem, g * (2 * TG + 1))

            def normalised(g):
                dve.wait_ge(s_rstd, 1 if isinstance(g, int) else 2)
                at = bass.ds(g + 1, 1)
                for t in range(TG):
                    v_.tensor_scalar(n1[:, t, :], rows_of(X, g)[:, t, :], mv[:, at, t, 0:1].rearrange("p a o -> p (a o)"),
                                     rstd[:, at, t], ALU.subtract, ALU.mult).then_inc(n1_done.sem, 1)

            def decay_logits(g):
                dve.wait_ge(raw_done.sem, raw_done.now(g))
                v_.tensor_tensor(zn[:], raw[:, :, 3 * DM:WALL], vecs[:, 3 * DM:ROWV].unsqueeze(1).to_broadcast([P, TG, HC]), ALU.add).then_inc(zadd.sem, 1)
                dve.wait_ge(zadd.sem, zadd.now(g))
                v_.tensor_scalar(zl[:], zn[:], -30.0, None, ALU.max).then_inc(zclamp.sem, 1)

            def rope_products(g):
                uv = raw[:, :, 0:2 * DM].rearrange("p t (h r d) -> p t h r d", r=2, d=ROPE_HALF)
                v_.tensor_tensor(m1[:], uv[:, :, :, 0, :], rope_table("cos", g), ALU.mult).then_inc(rope_a.sem, 1)
                v_.tensor_tensor(m2[:], uv[:, :, :, 1, :], rope_table("sin", g), ALU.mult).then_inc(rope_a.sem, 1)

            def rates(g):
                dve.wait_ge(zln.sem, zln.now(g))
                v_.tensor_scalar(rate[:], zn[:], float(-np.log(0.999)), float(-np.log(0.001)), ALU.max, ALU.min).then_inc(rate_done.sem, 1)
                dve.wait_ge(rate_done.sem, rate_done.now(g))

            def block_rates(g):
                dve.wait_ge(sum_ps.sem, sum_ps.now(g))
                v_.tensor_tensor(sums[:], T4[:, 448:448 + BPT].unsqueeze(1).to_broadcast([P, TG * 2, BPT]),
                                 K["tile_half"].rearrange("p (a b) -> p a b", b=BPT), ALU.mult).then_inc(sums_done.sem, 1)

            def rotated(g):
                rv = rot[:].rearrange("p t h (r d) -> p t h r d", d=ROPE_HALF)
                dve.wait_ge(rope_a.sem, rope_a.now(g))
                v_.tensor_tensor(rv[:, :, :, 0, :], m1[:], m2[:], ALU.subtract).then_inc(rot_done.sem, 1)
                dve.wait_ge(rope_b.sem, rope_b.now(g))
                v_.tensor_tensor(rv[:, :, :, 1, :], m3[:], m4[:], ALU.add).then_inc(rot_done.sem, 1)
                dve.wait_ge(rot_done.sem, rot_done.now(g))
                v_.tensor_scalar(rmin[:], rot[:], 0.0, None, ALU.min).then_inc(rmin_done.sem, 1)

            def features(g):
                dve.wait_ge(rexp_done.sem, rexp_done.now(g))
                v_.scalar_tensor_tensor(phi[:].rearrange("p t h d -> p (t h d)"), rot[:].rearrange("p t h d -> p (t h d)"), 1.0,
                                        rexp[:].rearrange("p t h d -> p (t h d)"), ALU.add, ALU.max).then_inc(phi_done.sem, 1)
                dve.wait_ge(phi_done.sem, phi_done.now(g))
                dve.wait_ge(ex_done.sem, ex_done.now(g))
                for t in range(TG):
                    f = ex[:, (TG + t) * HC:(TG + t + 1) * HC].rearrange("p (h c) -> p h c", c=C)
                    v_.tensor_tensor(qi[:, t], phi[:, t, 0:H, :].unsqueeze(2).to_broadcast([P, H, C, DH]),
                                     f.unsqueeze(3).to_broadcast([P, H, C, DH]), ALU.mult).then_inc(qi_done.sem, 1)

            def queries_T(g):
                dve.wait_ge(tq.sem, tq.now(g))
                for j in range(HG):
                    f = v_.tensor_scalar(qx[:, :, :, j, :].rearrange("p t b s -> p (t b) s"),
                                         T4.rearrange("p (n s) -> p n s", s=BLK), K["hmask"][:, j:j + 1], None, ALU.mult)
                f.then_inc(qx_done.sem, 1)

            def factors_T(g):
                dve.wait_ge(tfk.sem, tfk.now(g))
                v_.tensor_copy(fkT[:], T5).then_inc(fkT_done.sem, 1)

            def kept_decays(g):
                dve.wait_ge(ex_done.sem, ex_done.now(g))
                v_.tensor_copy(dec[:], ex[:, 3 * TG * HC:3 * TG * HC + TG * 2 * BPT]).then_inc(dec_done.sem, 1)

            def states(g, t, first=False):
                dve.wait_ge(u_ps.sem, u_ps.now(g, t + 1))
                for j in range(BPT):
                    n = BPT * t + j
                    for a in range(2):
                        if n:
                            dve.wait_ge(st_done.sem, st_done.now(g, made(n, a)))
                        elif first:
                            dve.wait_ge(s_state0, 1)
                            dve.wait_ge(dec_done.sem, dec_done.now(g))
                        else:
                            dve.wait_ge(carry_done.sem, carry_done.now(g - 1))
                            dve.wait_ge(dec_done.sem, dec_done.now(g))
                        if n == NB - 1 and a == 0:
                            dve.wait_ge(sbd_done.sem, sbd_done.now(g, 1))
                        at = (2 * t + a) * BPT + j
                        v_.scalar_tensor_tensor(state[:, (n + 1) % NB, a, :], state[:, n, a, :], dec[:, at:at + 1],
                                                U_ps[:, a, j, :], ALU.mult, ALU.add).then_inc(st_done.sem, 1)

            def gated(g, t):
                dve.wait_ge(sd_group.sem, sd_group.now(g, NHG * (t + 1)))
                dve.wait_ge(s_masked.sem, s_masked.now(g, t + 1))
                if t >= 2:
                    dve.wait_ge(att_ps.sem, att_ps.now(g, t - 1))
                else:
                    dve.wait_ge(att_ps.sem, att_ps.before(g, TG - 1 + t))
                v_.tensor_tensor(wts[:, t % 2].rearrange("p (a h) t -> p a (h t)", a=2), s_mk[:, t % 2].rearrange("p (a h) t -> p a (h t)", a=2),
                                 D_ps, ALU.mult).then_inc(w_done.sem, 1)

            def normed(g, t):
                dve.wait_ge(att_ps.sem, att_ps.now(g, t + 1))
                ov_ = O_ps.rearrange("p (h e) -> p h e", e=E1)
                v_.tensor_scalar(den[:, t, :], ov_[:, :, DH], DEN_EPS, None, ALU.add).then_inc(den_done.sem, 1)
                dve.wait_ge(den_done.sem, den_done.now(g, t + 1))
                v_.reciprocal(rden[:, t, :], den[:, t, :]).then_inc(rden_done.sem, 1)
                dve.wait_ge(rden_done.sem, rden_done.now(g, t + 1))
                v_.tensor_tensor(y[:, t], ov_[:, :, 0:DH], rden[:, t, :].unsqueeze(2).to_broadcast([P, H, DH]), ALU.mult).then_inc(y_done.sem, 1)

            def own_norm(p):
                dve.wait_ge(o_ps.sem, o_ps.now(p.step))
                layernorm(p.T_o.rearrange("p (t c) -> p t c", c=DM), 0, stats_b.sem, stats_b.now(p.g, p.stats), p.lo, p.hi)
                ag = attn_g[:].rearrange("p b g c -> p (b g) c")[:, bass.ds(p.g, 1), :].rearrange("p a c -> p (a c)")
                for t in p.tiles:
                    v_.scalar_tensor_tensor(z3[:, t, :], p.T_o[:, t * P:(t + 1) * P], mv[:, 0, t, 0:1], ag, ALU.subtract, ALU.mult).then_inc(z3_done.sem, 1)
                dve.wait_ge(rstd_done.sem, rstd_done.now(p.step, 1))
                dve.wait_ge(xb_done.sem, xb_done.now(p.g))
                for t in p.tiles:
                    dve.wait_ge(z3_done.sem, z3_done.now(p.g, t + 1))
                    v_.scalar_tensor_tensor(x2[:, t, :], z3[:, t, :], rstd[:, 0, t:t + 1], rows_of(X, p.g)[:, t, :], ALU.mult, ALU.add).then_inc(x2_done.sem, 1)

            def second_statistics(p):
                layernorm(x2, 0, stats_b.sem, stats_b.now(p.g, p.stats + 2 * p.n + 1), p.lo, p.hi,
                          ready=lambda t: (x2_done.sem, x2_done.now(p.g, t + 1)))

            def second_norm(p):
                dve.wait_ge(rstd_done.sem, rstd_done.now(p.step, 2))
                for t in p.tiles:
                    v_.tensor_scalar(n2[:, t, :], x2[:, t, :], mv[:, 0, t, 0:1], rstd[:, 0, t:t + 1], ALU.subtract, ALU.mult).then_inc(n2_done.sem, 1)

            def choice(p):
                at = slice(p.lo, p.hi)
                dve.wait_ge(lg_ps.sem, lg_ps.now(p.step))
                v_.tensor_copy(lg[:, at], p.T_l[:, 0:TG * NE].rearrange("p (t e) -> p t e", e=NE)[:, at]).then_inc(lg_done.sem, 1)
                dve.wait_ge(lg_done.sem, lg_done.now(p.step))
                apart(dve)
                for t in p.tiles:
                    v_.max(mx[:, t, :], lg[:, t, :]).then_inc(mx_done.sem, 1)
                for t in p.tiles:
                    dve.wait_ge(mx_done.sem, mx_done.now(p.g, t + 1))
                    apart(dve)
                    v_.max_index(ix[:, t, :], mx[:, t, :], lg[:, t, :]).then_inc(ix_done.sem, 1)
                v_.tensor_tensor(dl[:, at], mx[:, at, 1], mx[:, at, 0], ALU.subtract).then_inc(dl_done.sem, 1)
                dve.wait_ge(ix_done.sem, ix_done.now(p.g, p.hi))
                v_.tensor_copy(ef[:, at], ix[:, at, 0:TOPK]).then_inc(choice_steps.sem, 1)
                if p.lo == 0:
                    v_.tensor_copy(pre[:, 0, :], pre[:, TG, :]).then_inc(pre_done.sem, 1)
                dve.wait_ge(choice_steps.sem, choice_steps.now(p.step, 1))
                v_.tensor_tensor(oh[:, at], K["iota"].unsqueeze(1).unsqueeze(1).to_broadcast([P, p.n, TOPK, NE]),
                                 ef[:, at].unsqueeze(3).to_broadcast([P, p.n, TOPK, NE]), ALU.is_equal).then_inc(choice_steps.sem, 1)
                dve.wait_ge(choice_steps.sem, choice_steps.now(p.step, 2))
                v_.tensor_tensor(msk[:, at], oh[:, at, 0, :], oh[:, at, 1, :], ALU.add).then_inc(choice_steps.sem, 1)
                dve.wait_ge(choice_steps.sem, choice_steps.now(p.step, 3))
                for t in p.tiles:
                    dve.wait_ge(pre_done.sem, pre_done.now(p.g, t + 1))
                    v_.tensor_tensor(pre[:, t + 1, :], pre[:, t, :], msk[:, t, :], ALU.add).then_inc(pre_done.sem, 1)

            def slot(p):
                at = slice(p.lo, p.hi)
                dve.wait_ge(rk_ps.sem, rk_ps.now(p.step))
                rkv = p.T_l[:, 64:64 + TG * NE].rearrange("p (t e) -> p t e", e=NE)
                for k in range(TOPK):
                    f = v_.tensor_tensor(rm[:, at, k, :], oh[:, at, k, :], rkv[:, at], ALU.mult)
                f.then_inc(slot_steps.sem, 1)
                dve.wait_ge(slot_steps.sem, slot_steps.now(p.step, 1))
                v_.tensor_reduce(rk[:, at], rm[:, at], AX.X, ALU.add).then_inc(slot_steps.sem, 1)
                dve.wait_ge(slot_steps.sem, slot_steps.now(p.step, 2))
                v_.tensor_scalar(ov[:, at], rk[:, at], float(CAP), 1e6, ALU.is_ge, ALU.mult).then_inc(slot_steps.sem, 1)
                v_.scalar_tensor_tensor(sl[:, at], ef[:, at], float(CAP), rk[:, at], ALU.mult, ALU.add).then_inc(slot_steps.sem, 1)
                dve.wait_ge(slot_steps.sem, slot_steps.now(p.step, 4))
                dve.wait_ge(rows_left.sem, rows_left.before(p.g))
                v_.tensor_tensor(idx[:, at], sl[:, at], ov[:, at], ALU.add).then_inc(idx_done.sem, 1)

            def weights(p):
                at = slice(p.lo, p.hi)
                dve.wait_ge(de_done.sem, de_done.now(p.step))
                v_.tensor_scalar(dp[:, at], de[:, at], 1.0, None, ALU.add).then_inc(slot_steps.sem, 1)
                dve.wait_ge(slot_steps.sem, slot_steps.now(p.step, 5))
                v_.reciprocal(w0[:, at], dp[:, at]).then_inc(slot_steps.sem, 1)
                dve.wait_ge(slot_steps.sem, slot_steps.now(p.step, 6))
                v_.tensor_copy(row[:, at, 0, DM + 1], w0[:, at]).then_inc(wrow_done.sem, 1)
                v_.tensor_tensor(row[:, at, 1, DM + 1], w0[:, at], de[:, at], ALU.mult).then_inc(wrow_done.sem, 1)
                v_.tensor_copy(row[:, at, :, DM:DM + 1].bitcast(U32).rearrange("p t k o -> p t (k o)"), pid[:, at]).then_inc(prow_done.sem, 1)

            def residual(p):
                dve.wait_ge(gh_done.sem, gh_done.now(p.step))
                x_ = rows_of(X, p.g)[:, p.lo:p.hi, :]
                v_.tensor_tensor(x_, x2[:, p.lo:p.hi, :], gh[:, p.lo:p.hi, :], ALU.add).then_inc(base_done.sem, 1)

            def dve_body(g, more):
                n = g + 1
                if more:
                    normalised(n)
                normed(g, 0)
                states(g, 2)
                gated(g, 2)
                if more:
                    decay_logits(n)
                    rope_products(n)
                normed(g, 1)
                states(g, 3)
                if more:
                    rates(n)
                    block_rates(n)
                    rotated(n)
                gated(g, 3)
                if more:
                    dve.wait_ge(st_done.sem, st_done.now(g))
                    v_.tensor_scalar(state[:, 0], state[:, 0], K["keep"][:, bass.ds(n, 1)], None, ALU.mult).then_inc(carry_done.sem, 1)
                    features(n)
                    kept_decays(n)
                    normed(g, 2)
                    queries_T(n)
                    factors_T(n)
                    normed(g, 3)
                    own_norm(whole(g))
                    second_statistics(whole(g))
                    gated(n, 0)
                    second_norm(whole(g))
                    states(n, 0)
                    choice(whole(g))
                    states(n, 1)
                    gated(n, 1)
                    slot(whole(g))
                    weights(whole(g))
                    dve.wait_ge(prow_done.sem, prow_done.now(g))
                    v_.tensor_scalar(pid[:], pid[:], float(GT * TOPK), None, ALU.add).then_inc(pid_next.sem, 1)
                    dve.wait_ge(pid_next.sem, pid_next.now(g))
                    residual(whole(g))
                else:
                    own_norm(half_a)
                    normed(g, 2)
                    second_statistics(half_a)
                    second_norm(half_a)
                    normed(g, 3)
                    choice(half_a)
                    own_norm(half_b)
                    slot(half_a)
                    second_statistics(half_b)
                    second_norm(half_b)
                    weights(half_a)
                    choice(half_b)
                    slot(half_b)
                    weights(half_b)
                    residual(half_a)
                    residual(half_b)

            statistics(0)
            normalised(0)
            dve.wait_ge(s_c, 16)
            v_.tensor_scalar(c_s[:], cT[:], -80.0, None, ALU.max).then_inc(s_cs, 1)
            dve.wait_ge(s_ce, 1)
            v_.tensor_scalar(c_s[:], c_e[:], 1.0, None, ALU.add).then_inc(s_cs, 1)
            dve.wait_ge(s_cs, 2)
            v_.reciprocal(c_e[:], c_s[:]).then_inc(s_cs, 1)
            dve.wait_ge(s_cs, 3)
            v_.tensor_tensor(c_silu[:], cT[:], c_e[:], ALU.mult).then_inc(s_csilu, 1)
            dve.wait_ge(s_csilu, 1)
            v_.tensor_copy(c_rep[:], c_silu[:].unsqueeze(2).to_broadcast([P, B, P])).then_inc(s_crep, 1)
            dve.wait_ge(s_vecp, 1)
            v_.tensor_copy(vecs[:], ps[:, 1, 0:ROWV]).then_inc(s_vecs, 1)
            dve.wait_ge(s_modc, 1)
            mc = ps[:, 0, 0:4 * B].rearrange("p (j b) -> p j b", b=B)
            for b in range(B):
                v_.tensor_copy(modc[:, :, b * GPB:(b + 1) * GPB], mc[:, :, b:b + 1].to_broadcast([P, 4, GPB])).then_inc(s_modc_sb, 1)
            dve.wait_ge(s_modc_sb, 2)
            v_.tensor_scalar(modc[:, 1:4:2, :], modc[:, 1:4:2, :], 1.0, None, ALU.add).then_inc(s_modc_sb, 1)
            for g in range(1, GROUPS):
                statistics(g)
            decay_logits(0)
            dve.wait_ge(s_const, 16)
            v_.tensor_copy(tri_b[:], K["tri"]).then_inc(s_trib, 1)
            v_.tensor_copy(pid[:], K["pid"].rearrange("p (t k) -> p t k", k=TOPK)).then_inc(s_trib, 1)
            dve.wait_ge(s_trib, 2)
            rope_products(0)
            rates(0)
            block_rates(0)
            rotated(0)
            dve.wait_ge(s_modb, 1)
            for b in range(B):
                v_.tensor_copy(mod_b[:, b], ps[:, 2 + 4 * b:4 + 4 * b, :].rearrange("p w n -> p (w n)")[:, 0:6 * DM]).then_inc(s_gate, 1)
            features(0)
            kept_decays(0)
            queries_T(0)
            factors_T(0)
            states(0, 0, first=True)
            gated(0, 0)
            states(0, 1)
            gated(0, 1)
            dve.wait_ge(s_gate, 2)
            gv = mod_b[:].rearrange("p b (j c) -> p b j c", c=DM)[:, :, 2:6:3, :]
            v_.tensor_scalar(gsign[:], gv, 0.0, 2.0, ALU.is_ge, ALU.mult).then_inc(s_gate, 1)
            v_.tensor_scalar(gates[:], gv, -1.0, 0.25, ALU.mult, ALU.max).then_inc(s_gate, 1)
            dve.wait_ge(s_gate, 4)
            v_.tensor_tensor(gabs[:], gates[:], gv, ALU.max).then_inc(s_gate, 1)
            dve.wait_ge(s_gate, 5)
            for n in range(2):
                v_.scalar_tensor_tensor(gates[:, :, n, :], gsign[:, :, n, :], -1.0, gabs[:, :, n, :], ALU.add, ALU.mult).then_inc(s_gate, 1)
            dve.wait_ge(s_gate, 7)
            dve.wait_ge(s_vecs, 1)

            def per_group(v):
                return v.unsqueeze(2).to_broadcast([P, B, GPB, DM])

            for out_, j in ((attn_g, 1), (attn_b, 2)):
                v_.tensor_tensor(out_[:], per_group(gates[:, :, 0, :]),
                                 vecs[:, j * DM:(j + 1) * DM].unsqueeze(1).unsqueeze(1).to_broadcast([P, B, GPB, DM]), ALU.mult).then_inc(s_tables, 1)
            v_.tensor_copy(gate_b[:], per_group(gates[:, :, 1, :])).then_inc(s_tables, 1)
            with dve.Fori(0, GROUPS - 1) as g:
                dve_body(g, True)
            dve_body(GROUPS - 1, False)

            def last_slots():
                v_.memset(lastT[:, NE:NE + 1], 0.0).then_inc(s_lastT_sb, 1)
                dve.wait_ge(s_lastT, 1)
                v_.tensor_copy(lastT[:, 0:NE], T4[:, 0:NE]).then_inc(s_lastT_sb, 1)
                dve.wait_ge(s_lastT_sb, 2)

            def slots_T(u, i, e):
                dve.wait_ge(bT_ps[u].sem, bT_ps[u].now(i))
                dve.wait_ge(up_ps[u].sem, up_ps[u].before(i))
                v_.tensor_copy(bT[:, u, 0:512], ps[:, 0, :]).then_inc(bT_done[u].sem, 1)
                v_.tensor_copy(bT[:, u, 512:CM], ps[:, 1, 0:P]).then_inc(bT_done[u].sem, 1)
                if isinstance(e, int):
                    last_slots()
                v_.tensor_copy(bT[:, u, CM:CAP], lastT[:, bass.ds(e, 1)] if not isinstance(e, int) else lastT[:, e:e + 1]).then_inc(bT_done[u].sem, 1)

            def slot_meta(u, i):
                dve.wait_ge(xb_in[u].sem, xb_in[u].now(i))
                dve.wait_ge(outs_left[u].sem, outs_left[u].before(i))
                v_.tensor_copy(meta[:, u], xb[:, u, :, DM:RW]).then_inc(meta_done[u].sem, 1)

            def rows(u, i, lo, hi):
                if lo == 0:
                    dve.wait_ge(meta_done[u].sem, meta_done[u].now(i))
                    dve.wait_ge(outs_left[u].sem, outs_left[u].before(i))
                for a in range(lo, hi):
                    dve.wait_ge(r_ps[u].sem, r_ps[u].now(i, a + 1))
                    v_.tensor_scalar(orow[:, u, a, :], row_bank(u, a)[:, 0:P], meta[:, u, a, 1:2], None, ALU.mult).then_inc(r_done[u].sem, 1)

            def last_products(u, i):
                dve.wait_ge(w2_in[u].sem, w2_in[u].now(i))
                dve.wait_ge(hid_done[u].sem, hid_done[u].now(i))
                v_.tensor_scalar(last_p[:, u], w2t[:, u, 0, :], hid[:, u, 0, CM:CAP], None, ALU.mult).then_inc(last_done[u].sem, 1)
                for f in range(1, FT):
                    dve.wait_ge(last_done[u].sem, last_done[u].now(i, f))
                    v_.scalar_tensor_tensor(last_p[:, u], w2t[:, u, f, :], hid[:, u, f, CM:CAP], last_p[:, u], ALU.mult, ALU.add).then_inc(last_done[u].sem, 1)

            def last_out(u, i):
                v_.tensor_copy(lastO[:, bass.ds(i * 2 + u, 1)], row_bank(u, CT - 1)[:, P:P + 1]).then_inc(r_done[u].sem, 1)

            slots_T(0, 0, 0)
            slot_meta(0, 0)
            with dve.Fori(0, NE // 2) as i:
                slots_T(1, i, i * 2 + 1)
                rows(0, i, 0, 2)
                slot_meta(1, i)
                last_products(0, i)
                rows(0, i, 2, CT)
                last_out(0, i)
                slots_T(0, i + 1, i * 2 + 2)
                rows(1, i, 0, 2)
                last_products(1, i)
                rows(1, i, 2, CT)
                last_out(1, i)
                slot_meta(0, i + 1)
            dve.wait_ge(s_lastO, 1)
            v_.tensor_scalar(lastR[:], T4[0:NE, 0:P], lastx[:, DM + 1:RW], None, ALU.mult).then_inc(s_lastR, 2)
            for n, g in enumerate(VECTOR_OUT):
                dve.wait_ge(s_yb[g], 16)
                v_.tensor_tensor(ys[:, g], yb[:, g, :, 0, :], yb[:, g, :, 1, :], ALU.add).then_inc(s_ys, 1)
                dve.wait_ge(s_ys, n + 1)
                v_.tensor_tensor(ys[:, g], ys[:, g], output_gate(g), ALU.mult).then_inc(s_yg, 1)
                dve.wait_ge(s_yg, n + 1)
                v_.tensor_tensor(yo[:, g].rearrange("p t c -> p (t c)"), ys[:, g].rearrange("p t c -> p (t c)"), X[:, g], ALU.add).then_inc(s_yo, 1)

        @block.tensor
        def _(pe):
            mm = nc.tensor.matmul
            start_ahead(pe, "pe")
            pe.wait_ge(s_vec, 16)
            pe.wait_ge(s_ms, 4)
            mm(ps[:, 1, 0:ROWV], ones_row[:], vec_row[:], start=True, stop=True).then_inc(s_vecp, 1)
            pe.wait_ge(s_wmod, 16)
            pe.wait_ge(s_csilu, 1)
            for n, j in enumerate((0, 1, 3, 4)):
                f = mm(ps[:, 0, n * B:(n + 1) * B], wmod[:, j * DM:(j + 1) * DM], c_silu[:], start=True, stop=True)
            f.then_inc(s_modc, 1)
            pe.wait_ge(s_const, 16)
            pe.wait_ge(s_wall, 16)

            def tr(out, in_, **kw):
                return nc.tensor.transpose(out, in_, ident[0:in_.shape[0], 0:in_.shape[0]])

            def norm_T(g):
                for t in range(TG):
                    pe.wait_ge(n1_done.sem, n1_done.now(g, t + 1))
                    f = tr(T4[:, t * P:(t + 1) * P], n1[:, t, :])
                f.then_inc(n1T.sem, 1)

            def project(g):
                pe.wait_ge(hT_done.sem, hT_done.now(g))
                for t in range(TG):
                    if t >= 2:
                        pe.wait_ge(raw_done.sem, raw_done.now(g, t - 1))
                    mm(ps[:, 5 - t % 2, 0:WALL], hT[:, t * P:(t + 1) * P], wall[:], start=True, stop=True).then_inc(proj.sem, 1)

            def exponents(g):
                pe.wait_ge(raw_done.sem, raw_done.now(g))
                pe.wait_ge(rate_done.sem, rate_done.now(g))
                rv = rate[:].rearrange("p t h -> p (t h)")
                mm(T4[:, 448:448 + BPT], rv, K["blk"], start=True, stop=True).then_inc(sum_ps.sem, 1)
                for i in range(NSUB):
                    f = mm(T5[:, i * TG * HC:(i + 1) * TG * HC], K["gk"][:, i * P:(i + 1) * P], rv, start=True, stop=True)
                f.then_inc(expo_ps.sem, 1)
                pe.wait_ge(sums_done.sem, sums_done.now(g))
                for i, n in enumerate(("own", "cq", "ck")):
                    mm(T4[:, i * TG * HC:(i + 1) * TG * HC], K[n], rv, start=True, stop=True)
                mm(T4[:, 3 * TG * HC:3 * TG * HC + TG * 2 * BPT], K["spread"], sums[:].rearrange("p a b -> p (a b)"),
                   start=True, stop=True).then_inc(expo_ps.sem, 1)

            def query_T(g):
                pe.wait_ge(phi_done.sem, phi_done.now(g))
                pe.wait_ge(ex_done.sem, ex_done.now(g))
                for t in range(TG):
                    f = tr(T4[:, t * P:(t + 1) * P], phi[:, t, 0:H, :].rearrange("p h d -> p (h d)"))
                f.then_inc(tq.sem, 1)
                pe.wait_ge(fq_done.sem, fq_done.now(g))
                fqv = fq[:].rearrange("p (t h) i -> p t (h i)", t=TG)
                for t in range(TG):
                    f = tr(T5[:, t * P:(t + 1) * P], fqv[:, t, :])
                f.then_inc(tfq.sem, 1)

            def key_T(g):
                pe.wait_ge(qx_done.sem, qx_done.now(g))
                for t in range(TG):
                    f = tr(T4[:, t * P:(t + 1) * P], phi[:, t, H:2 * H, :].rearrange("p h d -> p (h d)"))
                f.then_inc(tk.sem, 1)
                pe.wait_ge(fqx_done.sem, fqx_done.now(g))
                for t in range(TG):
                    f = tr(T5[:, t * P:(t + 1) * P], fk[:, t].rearrange("p h i -> p (h i)"))
                f.then_inc(tfk.sem, 1)

            def decayed_query_T(g):
                pe.wait_ge(qi_done.sem, qi_done.now(g))
                pe.wait_ge(kT_done.sem, kT_done.now(g))
                pe.wait_ge(fkT_done.sem, fkT_done.now(g))
                for a in range(2):
                    for t in range(TG):
                        f = tr(ps[:, 4 + a, t * P:(t + 1) * P], qi[:, t, a * HALF:(a + 1) * HALF].rearrange("p h c d -> p (h c d)"))
                    f.then_inc(tqi.sem, 1)

            def attention(g, t):
                if t == 0:
                    pe.wait_ge(qiT_done.sem, qiT_done.now(g))
                pe.wait_ge(sbd_done.sem, sbd_done.now(g, t + 1))
                pe.wait_ge(y_done.sem, y_done.now(g, t) if t else y_done.before(g))
                for j in range(BPT):
                    for a in range(2):
                        mm(O_ps[j * BLK:(j + 1) * BLK, a * SW:(a + 1) * SW], qiT[:, a, t * P + j * BLK:t * P + (j + 1) * BLK],
                           sbd[:, t % 2, j, a, :], start=(a == 0), stop=False, skip_group_check=True, tile_position=(0, j * BLK))
                pe.wait_ge(w_done.sem, w_done.now(g, t + 1))
                apart(pe)
                for n in range(H):
                    h = ((n % 8) // HG * 2 + n // 8) * HG + n % HG
                    for j in range(BPT):
                        r = slice(j * BLK, (j + 1) * BLK)
                        f = mm(O_ps[r, h * E1:(h + 1) * E1], wts[r, t % 2, n, :], v1[r, t, h, :], start=False, stop=True,
                               skip_group_check=True, tile_position=(j * BLK, j * BLK))
                f.then_inc(att_ps.sem, 1)

            def adds(g, t, first=False):
                if t:
                    pe.wait_ge(st_done.sem, st_done.now(g, 2 * t * BPT))
                else:
                    if not first:
                        pe.wait_ge(z3_done.sem, z3_done.now(g - 1))
                    pe.wait_ge(vx_done.sem, vx_done.now(g))
                    pe.wait_ge(ks_done.sem, ks_done.now(g))
                for a in range(2):
                    for c in range(HALF // HP):
                        h = a * HALF + c * HP
                        f = mm(U_ps[c * 32:(c + 1) * 32, a, :, :], ks[:, t, h:h + HP].rearrange("p h c d -> p (h c d)"),
                               vx[:, t, :, h * E1:h * E1 + PW], start=True, stop=True, tile_position=(0, c * 32))
                f.then_inc(u_ps.sem, 1)

            def scores(g, t):
                pe.wait_ge(s_copied.sem, s_copied.now(g, t) if t else s_copied.before(g))
                pe.wait_ge(w_done.sem, w_done.now(g, t) if t else w_done.before(g))
                apart(pe)
                for hg in range(NHG):
                    if hg >= 2:
                        pe.wait_ge(sd_group.sem, sd_group.now(g, NHG * t + hg - 1))
                        apart(pe)
                    r = slice(hg * 32, hg * 32 + 32)
                    for w, (st, mv_) in enumerate(((kT, qx), (fkT, fqx))):
                        for j in range(BPT):
                            f = mm(ps[j * BLK:(j + 1) * BLK, 2 * (hg % 2) + w, hg // 2 * P:(hg // 2 + 1) * P],
                                   st[r, t * P + j * BLK:t * P + (j + 1) * BLK], mv_[r, t, j].rearrange("p h s -> p (h s)"),
                                   start=True, stop=True, tile_position=(hg * 32, j * BLK))
                    f.then_inc(sd_group.sem, 1)

            def tile_ahead(g, t):
                adds(g, t)
                scores(g, t)

            def output_T(p):
                pe.wait_ge(y_done.sem, y_done.now(p.g, p.hi))
                for t in p.tiles:
                    f = tr(p.T_y[:, t * P:(t + 1) * P], y[:, t].rearrange("p h d -> p (h d)"))
                f.then_inc(yT_ps.sem, 1)

            def input_back(p):
                if p.T_o is T7:
                    pe.wait_ge(st_done.sem, st_done.now(p.g))
                pe.wait_ge(keep_done.sem, keep_done.now(p.g))
                for t in p.tiles:
                    mm(p.T_o[:, t * P:(t + 1) * P], h_keep[:, t * P:(t + 1) * P], ident, start=(t == p.lo), stop=False,
                       skip_group_check=True)

            def out_project(p):
                pe.wait_ge(yT_done.sem, yT_done.now(p.step))
                for t in p.tiles:
                    f = mm(p.T_o[:, t * P:(t + 1) * P], yT[:, t * P:(t + 1) * P], wo[:], start=False, stop=True,
                           skip_group_check=True)
                f.then_inc(o_ps.sem, 1)

            def second_T(p):
                for t in p.tiles:
                    pe.wait_ge(n2_done.sem, n2_done.now(p.g, t + 1))
                    f = tr(p.T_n[:, t * P:(t + 1) * P], n2[:, t, :])
                f.then_inc(n2T.sem, 1)

            def route(p):
                pe.wait_ge(h2T_done.sem, h2T_done.now(p.step))
                for t in p.tiles:
                    f = mm(p.T_l[:, t * NE:(t + 1) * NE], h2T[:, t * P:(t + 1) * P], rwt[:], start=True, stop=True)
                f.then_inc(lg_ps.sem, 1)
                for t in p.tiles:
                    f = tr(p.T_h[:, t * P:(t + 1) * P], h2T[:, t * P:(t + 1) * P])
                f.then_inc(h2_ps.sem, 1)

            def ranks(p):
                pe.wait_ge(lg_done.sem, lg_done.now(p.step))
                pe.wait_ge(pre_done.sem, pre_done.now(p.g, p.hi + 1))
                rk_o = p.T_l[:, 64 + p.lo * NE:64 + p.hi * NE]
                mm(rk_o, tri_b[:], msk[:, p.lo:p.hi].rearrange("p t e -> p (t e)"), start=True, stop=False)
                mm(rk_o, ones_b[:], pre[:, p.lo:p.hi, :].rearrange("p t e -> p (t e)"), start=False, stop=True).then_inc(rk_ps.sem, 1)

            def pe_body(g, more):
                n = g + 1
                tile_ahead(g, 2)
                if more:
                    pe.wait_ge(slot_steps.sem, slot_steps.before(g))
                    pe.wait_ge(row_done.sem, row_done.before(g))
                    norm_T(n)
                    project(n)
                attention(g, 1)
                tile_ahead(g, 3)
                if more:
                    exponents(n)
                if more:
                    attention(g, 2)
                    query_T(n)
                    attention(g, 3)
                    key_T(n)
                    input_back(whole(g))
                    output_T(whole(g))
                    out_project(whole(g))
                    decayed_query_T(n)
                    scores(n, 0)
                    adds(n, 0)
                    pe.wait_ge(qiT_done.sem, qiT_done.now(n))
                    scores(n, 1)
                    second_T(whole(g))
                    adds(n, 1)
                    route(whole(g))
                    attention(n, 0)
                    ranks(whole(g))
                else:
                    pe.wait_ge(slot_steps.sem, slot_steps.before(g))
                    pe.wait_ge(row_done.sem, row_done.before(g))
                    input_back(half_a)
                    output_T(half_a)
                    out_project(half_a)
                    attention(g, 2)
                    attention(g, 3)
                    second_T(half_a)
                    input_back(half_b)
                    output_T(half_b)
                    route(half_a)
                    out_project(half_b)
                    ranks(half_a)
                    second_T(half_b)
                    route(half_b)
                    ranks(half_b)

            norm_T(0)
            project(0)
            pe.wait_ge(s_crep, 1)
            for b in range(B):
                mm(ps[:, 2 + 4 * b, :], c_rep[:, b, :], wmod[:, 0:512], start=True, stop=True)
                f = mm(ps[:, 3 + 4 * b, 0:256], c_rep[:, b, :], wmod[:, 512:768], start=True, stop=True)
            f.then_inc(s_modb, 1)
            pe.wait_ge(s_small, 32)
            pe.wait_ge(s_trib, 2)
            exponents(0)
            query_T(0)
            key_T(0)
            decayed_query_T(0)
            pe.wait_ge(s_gate, 2)
            adds(0, 0, first=True)
            scores(0, 0)
            tile_ahead(0, 1)
            attention(0, 0)
            with pe.Fori(0, GROUPS - 1) as g:
                pe_body(g, True)
            pe_body(GROUPS - 1, False)

            def slots_T(u, i):
                pe.wait_ge(xb_in[u].sem, xb_in[u].now(i))
                if u == 0:
                    pe.wait_ge(bT_done[1].sem, bT_done[1].before(i))
                    pe.wait_ge(hid_done[1].sem, hid_done[1].before(i, 2 * FT - 2))
                else:
                    pe.wait_ge(bT_done[0].sem, bT_done[0].now(i))
                    pe.wait_ge(hid_done[0].sem, hid_done[0].now(i, 2 * FT - 2))
                for a in range(CT):
                    f = tr(ps[:, a // 4, (a % 4) * P:(a % 4 + 1) * P], xb[:, u, a, 0:DM])
                f.then_inc(bT_ps[u].sem, 1)

            def up(u, i):
                pe.wait_ge(w1_in[u].sem, w1_in[u].now(i))
                pe.wait_ge(bT_done[u].sem, bT_done[u].now(i))
                for f in range(FT):
                    for n, (c0, cn) in enumerate(NHALF):
                        k = 2 * f + n
                        if k >= 4:
                            pe.wait_ge(hid_done[u].sem, hid_done[u].now(i, k - 3))
                        elif k >= 2 and u:
                            pe.wait_ge(hid_done[0].sem, hid_done[0].now(i, 2 * FT - 3 + k))
                        elif k >= 2:
                            pe.wait_ge(hid_done[1].sem, hid_done[1].before(i, 2 * FT - 3 + k))
                        mm(ps[:, k % 4, 0:cn], w1t[:, u, f * P:(f + 1) * P], bT[:, u, c0:c0 + cn], start=True, stop=True).then_inc(up_ps[u].sem, 1)

            def down(u, i):
                pe.wait_ge(w2_in[u].sem, w2_in[u].now(i))
                if u:
                    pe.wait_ge(r_done[0].sem, r_done[0].now(i))
                else:
                    pe.wait_ge(r_done[1].sem, r_done[1].before(i))
                for a in range(CT):
                    if a >= 4:
                        pe.wait_ge(r_done[u].sem, r_done[u].now(i, a - 3))
                    for f in range(FT):
                        pe.wait_ge(hid_done[u].sem, hid_done[u].now(i, 2 * f + 1 + (a * P >= CH)))
                        m = mm(row_bank(u, a)[:, 0:P], hid[:, u, f, a * P:(a + 1) * P], w2t[:, u, f, :], start=(f == 0), stop=(f == FT - 1))
                    if a == CT - 1:
                        pe.wait_ge(last_done[u].sem, last_done[u].now(i))
                        m = mm(row_bank(u, a)[:, P:P + 1], last_p[:, u], ones_col[:], start=True, stop=True)
                    m.then_inc(r_ps[u].sem, 1)

            slots_T(0, 0)
            pe.wait_ge(s_lastx, 16)
            tr(T4[:, 0:NE], lastx[:, 0:DM]).then_inc(s_lastT, 1)
            with pe.Fori(0, NE // 2) as i:
                up(0, i)
                slots_T(1, i)
                down(0, i)
                up(1, i)
                slots_T(0, i + 1)
                down(1, i)
            for u in range(2):
                pe.wait_ge(r_done[u].sem, r_done[u].now(NE // 2 - 1))
            tr(T4[0:NE, 0:P], lastO[:]).then_inc(s_lastO, 1)


_OUT = ((B, S, DM), "float32")


def kernel(**inputs):
    import concourse.bacc as _bacc
    from concourse.bass_utils import run_bass_kernel_spmd as _run

    a = {k: np.asarray(v) for k, v in inputs.items()}
    arrays = {
        "x": a["L0_attn_x"],
        "wall": np.concatenate([a["L0_attn_Wq"], a["L0_attn_Wk"], a["L0_attn_Wv"], a["L0_attn_Wbeta"]], axis=1),
        "wo": a["L0_attn_Wo"],
        "rows": np.concatenate([a["L0_attn_bo"], a["L0_attn_ln_gamma"], a["L0_attn_ln_beta"], a["L0_attn_bbeta"]])[None, :],
        "rwt": a["L0_ffn_router_w"].T,
        "w1": a["L0_ffn_w1"],
        "w2": a["L0_ffn_w2"],
        "ct": a["L0_c"].T,
        "wmod": a["L0_wmod"],
        "constants": constants(),
        "bo": a["L0_attn_bo"][:, None],
    }
    arrays = {f"in_{k}": np.ascontiguousarray(v) for k, v in arrays.items()}
    nc = _bacc.Bacc("TRN2", target_bir_lowering=False, num_devices=1)
    args = [nc.dram_tensor(n, v.shape, mybir.dt.from_np(v.dtype), kind="ExternalInput").ap() for n, v in arrays.items()]
    out = nc.dram_tensor("out", _OUT[0], F32, kind="ExternalOutput").ap()
    program(nc, *args, out)
    r = _run(nc, [arrays], core_ids=[0])
    return r.results[0]["out"]
```
